# Optimizing a Trainium2 kernel written in Bass

```python
import numpy as np
import jax
import jax.numpy as jnp

def _softmax(x, axis=-1):
    return jax.nn.softmax(x, axis=axis)
def _gelu(x):
    return jax.nn.gelu(x, approximate=True)
def _silu(x):
    return jax.nn.silu(x)
def _sigmoid(x):
    return jax.nn.sigmoid(x)
def _layernorm(x, axis=-1, eps=1e-5):
    m = jnp.mean(x, axis=axis, keepdims=True)
    v = jnp.var(x, axis=axis, keepdims=True)
    return (x - m) / jnp.sqrt(v + eps)
def _scatter_add(tgt, idx, src, axis=0):
    return tgt.at[idx].add(src)
def _segment_sum(src, seg, n):
    return jax.ops.segment_sum(src, seg, n)

kernel_name = 'mk_conv_attn_hybrid_d2_conv_nchw256_ee825f'

def setup_inputs(seed: int = 0):
    np.random.seed(seed)
    _w = jnp.asarray
    def _rec_inputs():
        import jax
        import jax.numpy as jnp
        _gk = jax.random.key(seed)
        x = -0.0002928 + 1 * jax.random.normal(jax.random.fold_in(_gk, 1), (16, 256, 32, 32), jnp.float32)
        return x
    x = _rec_inputs()
    def _L0_conv_setup():
        import jax, jax.numpy as jnp
        import numpy as np
        B, C, H, W = (16, 256, 32, 32)
        AD, SC, R = (16, 32, 4)

        def _conv1x1(x, w, b):
            return jnp.einsum('oc,bchw->bohw', w, x) + b[None, :, None, None]
        key = jax.random.key(seed)
        ks = jax.random.split(key, 12)
        p = lambda k, shape: jax.random.normal(k, shape, dtype=jnp.float32) * 0.02
        return {'x': jax.random.normal(ks[0], (B, C, H, W), dtype=jnp.float32), 'fc1_w': p(ks[1], (C // R, C)), 'fc1_b': jnp.zeros((C // R,), jnp.float32), 'fc2_w': p(ks[2], (C, C // R)), 'fc2_b': jnp.zeros((C,), jnp.float32), 'qkv_w': p(ks[3], (AD * 2 + SC, SC)), 'qkv_b': jnp.zeros((AD * 2 + SC,), jnp.float32), 'proj_w': p(ks[4], (SC, SC)), 'proj_b': jnp.zeros((SC,), jnp.float32), 'ffn1_w': p(ks[5], (4 * C, C)), 'ffn1_b': jnp.zeros((4 * C,), jnp.float32), 'ffn2_w': p(ks[6], (C, 4 * C)), 'ffn2_b': jnp.zeros((C,), jnp.float32)}
    _L0_conv_all = _L0_conv_setup()
    _L0_conv_in = {k: v for k, v in _L0_conv_all.items() if k in ('fc1_w', 'fc1_b', 'fc2_w', 'fc2_b', 'qkv_w', 'qkv_b', 'proj_w', 'proj_b', 'ffn1_w', 'ffn1_b', 'ffn2_w', 'ffn2_b', )}
    del _L0_conv_all

    def _L1_attn_setup():
        import jax, jax.numpy as jnp
        import numpy as np
        D_MODEL = 256
        D_STATE = 64
        D_CONV = 4
        EXPAND = 2
        HEADDIM = 64
        D_INNER = EXPAND * D_MODEL
        NHEADS = D_INNER // HEADDIM
        CONV_DIM = D_INNER + 2 * D_STATE
        BATCH = 8
        SEQ = 4096

        def _rmsnorm(x, w, eps):
            return x * jax.lax.rsqrt(jnp.mean(x * x, axis=-1, keepdims=True) + eps) * w
        key = jax.random.key(seed)
        ks = jax.random.split(key, 6)
        x = jax.random.normal(ks[0], (BATCH, SEQ, D_MODEL), jnp.float32)
        d_in_proj = 2 * D_INNER + 2 * D_STATE + NHEADS
        W_in = jax.random.normal(ks[1], (d_in_proj, D_MODEL), jnp.float32) / np.sqrt(D_MODEL)
        conv_w = jax.random.normal(ks[2], (CONV_DIM, D_CONV), jnp.float32) / np.sqrt(D_CONV)
        conv_b = jnp.zeros((CONV_DIM,), jnp.float32)
        dt = jnp.exp(jax.random.uniform(ks[3], (NHEADS,), jnp.float32, np.log(0.001), np.log(0.1)))
        dt_bias = dt + jnp.log(-jnp.expm1(-dt))
        A_log = jnp.log(jax.random.uniform(ks[4], (NHEADS,), jnp.float32, 1.0, 16.0))
        Dp = jnp.ones((NHEADS,), jnp.float32)
        gnorm_w = jnp.ones((D_INNER,), jnp.float32)
        norm_w = jnp.ones((D_MODEL,), jnp.float32)
        W_out = jax.random.normal(ks[5], (D_MODEL, D_INNER), jnp.float32) / np.sqrt(D_INNER)
        return {'x': x, 'W_in': W_in, 'conv_w': conv_w, 'conv_b': conv_b, 'dt_bias': dt_bias, 'A_log': A_log, 'Dp': Dp, 'gnorm_w': gnorm_w, 'norm_w': norm_w, 'W_out': W_out}
    _L1_attn_all = _L1_attn_setup()
    _L1_attn_in = {k: v for k, v in _L1_attn_all.items() if k in ('W_in', 'conv_w', 'conv_b', 'dt_bias', 'A_log', 'Dp', 'gnorm_w', 'norm_w', 'W_out', )}
    del _L1_attn_all

    def _L1_ffn_setup():
        import jax, jax.numpy as jnp
        import numpy as np
        B, N, D = (16, 4096, 256)
        NUM_EXPERTS, TOP_K, HEADS = (4, 2, 4)
        N_EDGES = 1048576
        LN_EPS = 1e-05

        def _layernorm(x, g, b):
            mu = x.mean(-1, keepdims=True)
            var = ((x - mu) ** 2).mean(-1, keepdims=True)
            return (x - mu) * jax.lax.rsqrt(var + LN_EPS) * g + b

        def _forward(x, edge_index, W_gat, att_src, att_dst, b_gat, ln_gamma, ln_beta, W1, b1, W2, b2):
            Bc, Nc, Dc = x.shape
            M = Bc * Nc
            x_flat = x.reshape(M, Dc)
            h = (x_flat @ W_gat).reshape(M, HEADS, NUM_EXPERTS)
            loops = jnp.arange(M, dtype=edge_index.dtype)
            src = jnp.concatenate([edge_index[0], loops])
            dst = jnp.concatenate([edge_index[1], loops])
            a_src = (h * att_src).sum(-1)
            a_dst = (h * att_dst).sum(-1)
            e = jax.nn.leaky_relu(a_src[src] + a_dst[dst], negative_slope=0.2)
            e_max = jax.ops.segment_max(e, dst, num_segments=M)
            ee = jnp.exp(e - e_max[dst])
            denom = jax.ops.segment_sum(ee, dst, num_segments=M)
            alpha = ee / (denom[dst] + 1e-16)
            msg = h[src] * alpha[:, :, None]
            agg = jax.ops.segment_sum(msg, dst, num_segments=M).reshape(M, HEADS * NUM_EXPERTS) + b_gat
            scores = _layernorm(agg, ln_gamma, ln_beta).reshape(M, HEADS, NUM_EXPERTS).mean(1)
            scores = scores.reshape(Bc, Nc, NUM_EXPERTS)
            topk_s, topk_i = jax.lax.top_k(scores, TOP_K)
            w = jax.nn.softmax(topk_s, axis=-1)
            out = jnp.zeros_like(x)
            for ei in range(NUM_EXPERTS):
                g = jnp.where(topk_i == ei, w, 0.0).sum(-1)
                hh = jax.nn.gelu(x @ W1[ei] + b1[ei], approximate=False)
                out = out + g[..., None] * (hh @ W2[ei] + b2[ei])
            return out
        key = jax.random.key(seed)
        ks = jax.random.split(key, 8)
        s = 0.05
        return {'x': jax.random.normal(ks[0], (B, N, D), jnp.float32), 'W_gat': jax.random.normal(ks[1], (D, HEADS * NUM_EXPERTS), jnp.float32) * s, 'att_src': jax.random.normal(ks[2], (HEADS, NUM_EXPERTS), jnp.float32) * s, 'att_dst': jax.random.normal(ks[3], (HEADS, NUM_EXPERTS), jnp.float32) * s, 'b_gat': jnp.zeros((HEADS * NUM_EXPERTS,), jnp.float32), 'ln_gamma': jnp.ones((HEADS * NUM_EXPERTS,), jnp.float32), 'ln_beta': jnp.zeros((HEADS * NUM_EXPERTS,), jnp.float32), 'W1': jax.random.normal(ks[4], (NUM_EXPERTS, D, 2 * D), jnp.float32) * s, 'b1': jnp.zeros((NUM_EXPERTS, 2 * D), jnp.float32), 'W2': jax.random.normal(ks[5], (NUM_EXPERTS, 2 * D, D), jnp.float32) * s, 'b2': jnp.zeros((NUM_EXPERTS, D), jnp.float32), 'edge_index': jax.random.randint(ks[6], (2, N_EDGES), 0, B * N, jnp.int32)}
    _L1_ffn_all = _L1_ffn_setup()
    _L1_ffn_in = {k: v for k, v in _L1_ffn_all.items() if k in ('W_gat', 'att_src', 'att_dst', 'b_gat', 'ln_gamma', 'ln_beta', 'W1', 'b1', 'W2', 'b2', 'edge_index', )}
    del _L1_ffn_all

    return {
        "x": x,
        "L0_conv_fc1_w": _L0_conv_in["fc1_w"],
        "L0_conv_fc1_b": _L0_conv_in["fc1_b"],
        "L0_conv_fc2_w": _L0_conv_in["fc2_w"],
        "L0_conv_fc2_b": _L0_conv_in["fc2_b"],
        "L0_conv_qkv_w": _L0_conv_in["qkv_w"],
        "L0_conv_qkv_b": _L0_conv_in["qkv_b"],
        "L0_conv_proj_w": _L0_conv_in["proj_w"],
        "L0_conv_proj_b": _L0_conv_in["proj_b"],
        "L0_conv_ffn1_w": _L0_conv_in["ffn1_w"],
        "L0_conv_ffn1_b": _L0_conv_in["ffn1_b"],
        "L0_conv_ffn2_w": _L0_conv_in["ffn2_w"],
        "L0_conv_ffn2_b": _L0_conv_in["ffn2_b"],
        "L1_attn_W_in": _L1_attn_in["W_in"],
        "L1_attn_conv_w": _L1_attn_in["conv_w"],
        "L1_attn_conv_b": _L1_attn_in["conv_b"],
        "L1_attn_dt_bias": _L1_attn_in["dt_bias"],
        "L1_attn_A_log": _L1_attn_in["A_log"],
        "L1_attn_Dp": _L1_attn_in["Dp"],
        "L1_attn_gnorm_w": _L1_attn_in["gnorm_w"],
        "L1_attn_norm_w": _L1_attn_in["norm_w"],
        "L1_attn_W_out": _L1_attn_in["W_out"],
        "L1_ffn_W_gat": _L1_ffn_in["W_gat"],
        "L1_ffn_att_src": _L1_ffn_in["att_src"],
        "L1_ffn_att_dst": _L1_ffn_in["att_dst"],
        "L1_ffn_b_gat": _L1_ffn_in["b_gat"],
        "L1_ffn_ln_gamma": _L1_ffn_in["ln_gamma"],
        "L1_ffn_ln_beta": _L1_ffn_in["ln_beta"],
        "L1_ffn_W1": _L1_ffn_in["W1"],
        "L1_ffn_b1": _L1_ffn_in["b1"],
        "L1_ffn_W2": _L1_ffn_in["W2"],
        "L1_ffn_b2": _L1_ffn_in["b2"],
        "L1_ffn_edge_index": _L1_ffn_in["edge_index"],
    }

def reference(x, L0_conv_fc1_w, L0_conv_fc1_b, L0_conv_fc2_w, L0_conv_fc2_b, L0_conv_qkv_w, L0_conv_qkv_b, L0_conv_proj_w, L0_conv_proj_b, L0_conv_ffn1_w, L0_conv_ffn1_b, L0_conv_ffn2_w, L0_conv_ffn2_b, L1_attn_W_in, L1_attn_conv_w, L1_attn_conv_b, L1_attn_dt_bias, L1_attn_A_log, L1_attn_Dp, L1_attn_gnorm_w, L1_attn_norm_w, L1_attn_W_out, L1_ffn_W_gat, L1_ffn_att_src, L1_ffn_att_dst, L1_ffn_b_gat, L1_ffn_ln_gamma, L1_ffn_ln_beta, L1_ffn_W1, L1_ffn_b1, L1_ffn_W2, L1_ffn_b2, L1_ffn_edge_index):
    import jax
    import jax.numpy as jnp
    def _L0_conv_ref(x, fc1_w, fc1_b, fc2_w, fc2_b, qkv_w, qkv_b, proj_w, proj_b, ffn1_w, ffn1_b, ffn2_w, ffn2_b):
        import jax, jax.numpy as jnp
        import numpy as np
        B, C, H, W = (16, 256, 32, 32)
        AD, SC, R = (16, 32, 4)

        def _conv1x1(x, w, b):
            return jnp.einsum('oc,bchw->bohw', w, x) + b[None, :, None, None]
        s = x.mean(axis=(2, 3), keepdims=True)
        s = jax.nn.relu(_conv1x1(s, fc1_w, fc1_b))
        s = jax.nn.sigmoid(_conv1x1(s, fc2_w, fc2_b))
        xg = x * s
        attn_part, non_attn_part = (xg[:, :SC], xg[:, SC:])
        qkv = _conv1x1(attn_part, qkv_w, qkv_b)
        q = qkv[:, :AD].reshape(B, AD, H * W)
        k = qkv[:, AD:2 * AD].reshape(B, AD, H * W)
        v = qkv[:, 2 * AD:].reshape(B, SC, H * W)
        scale = AD ** (-0.5)
        attn = jax.nn.softmax(jnp.einsum('bcn,bcm->bnm', q, k) * scale, axis=-1)
        out = jnp.einsum('bcm,bnm->bcn', v, attn).reshape(B, SC, H, W)
        attn_out = _conv1x1(out, proj_w, proj_b)
        y = jnp.concatenate([attn_out, non_attn_part], axis=1)
        h = jax.nn.relu(_conv1x1(y, ffn1_w, ffn1_b))
        return _conv1x1(h, ffn2_w, ffn2_b)

    def _L1_attn_ref(x, W_in, conv_w, conv_b, dt_bias, A_log, Dp, gnorm_w, norm_w, W_out):
        import jax, jax.numpy as jnp
        import numpy as np
        D_MODEL = 256
        D_STATE = 64
        D_CONV = 4
        EXPAND = 2
        HEADDIM = 64
        D_INNER = EXPAND * D_MODEL
        NHEADS = D_INNER // HEADDIM
        CONV_DIM = D_INNER + 2 * D_STATE
        BATCH = 8
        SEQ = 4096

        def _rmsnorm(x, w, eps):
            return x * jax.lax.rsqrt(jnp.mean(x * x, axis=-1, keepdims=True) + eps) * w
        Bsz, L, _ = x.shape
        xn = _rmsnorm(x, norm_w, jnp.finfo(x.dtype).eps)
        zxbcdt = jnp.einsum('bld,ed->ble', xn, W_in)
        z = zxbcdt[..., :D_INNER]
        xBC = zxbcdt[..., D_INNER:D_INNER + CONV_DIM]
        dt = zxbcdt[..., -NHEADS:]
        xpad = jnp.pad(xBC, ((0, 0), (D_CONV - 1, 0), (0, 0)))
        conv = sum((xpad[:, k:k + L, :] * conv_w[:, k] for k in range(D_CONV))) + conv_b
        xBC = jax.nn.silu(conv)
        xs = xBC[..., :D_INNER].reshape(Bsz, L, NHEADS, HEADDIM)
        Bm = xBC[..., D_INNER:D_INNER + D_STATE]
        Cm = xBC[..., D_INNER + D_STATE:]
        dt = jax.nn.softplus(dt + dt_bias)
        dA = jnp.exp(dt * -jnp.exp(A_log))

        def step(state, inp):
            dA_t, dt_t, B_t, C_t, x_t = inp
            state = state * dA_t[:, :, None, None] + (dt_t[:, :, None] * x_t)[..., None] * B_t[:, None, None, :]
            y = jnp.einsum('bhpn,bn->bhp', state, C_t)
            return (state, y)
        init = jnp.zeros((Bsz, NHEADS, HEADDIM, D_STATE), x.dtype)
        tm = lambda a: jnp.moveaxis(a, 1, 0)
        _, ys = jax.lax.scan(step, init, (tm(dA), tm(dt), tm(Bm), tm(Cm), tm(xs)))
        y = jnp.moveaxis(ys, 0, 1) + Dp[None, None, :, None] * xs
        y = y.reshape(Bsz, L, D_INNER)
        y = _rmsnorm(y * jax.nn.silu(z), gnorm_w, 1e-05)
        return x + jnp.einsum('ble,de->bld', y, W_out)

    def _L1_ffn_ref(x, W_gat, att_src, att_dst, b_gat, ln_gamma, ln_beta, W1, b1, W2, b2, edge_index):
        import jax, jax.numpy as jnp
        import numpy as np
        B, N, D = (16, 4096, 256)
        NUM_EXPERTS, TOP_K, HEADS = (4, 2, 4)
        N_EDGES = 1048576
        LN_EPS = 1e-05

        def _layernorm(x, g, b):
            mu = x.mean(-1, keepdims=True)
            var = ((x - mu) ** 2).mean(-1, keepdims=True)
            return (x - mu) * jax.lax.rsqrt(var + LN_EPS) * g + b

        def _forward(x, edge_index, W_gat, att_src, att_dst, b_gat, ln_gamma, ln_beta, W1, b1, W2, b2):
            Bc, Nc, Dc = x.shape
            M = Bc * Nc
            x_flat = x.reshape(M, Dc)
            h = (x_flat @ W_gat).reshape(M, HEADS, NUM_EXPERTS)
            loops = jnp.arange(M, dtype=edge_index.dtype)
            src = jnp.concatenate([edge_index[0], loops])
            dst = jnp.concatenate([edge_index[1], loops])
            a_src = (h * att_src).sum(-1)
            a_dst = (h * att_dst).sum(-1)
            e = jax.nn.leaky_relu(a_src[src] + a_dst[dst], negative_slope=0.2)
            e_max = jax.ops.segment_max(e, dst, num_segments=M)
            ee = jnp.exp(e - e_max[dst])
            denom = jax.ops.segment_sum(ee, dst, num_segments=M)
            alpha = ee / (denom[dst] + 1e-16)
            msg = h[src] * alpha[:, :, None]
            agg = jax.ops.segment_sum(msg, dst, num_segments=M).reshape(M, HEADS * NUM_EXPERTS) + b_gat
            scores = _layernorm(agg, ln_gamma, ln_beta).reshape(M, HEADS, NUM_EXPERTS).mean(1)
            scores = scores.reshape(Bc, Nc, NUM_EXPERTS)
            topk_s, topk_i = jax.lax.top_k(scores, TOP_K)
            w = jax.nn.softmax(topk_s, axis=-1)
            out = jnp.zeros_like(x)
            for ei in range(NUM_EXPERTS):
                g = jnp.where(topk_i == ei, w, 0.0).sum(-1)
                hh = jax.nn.gelu(x @ W1[ei] + b1[ei], approximate=False)
                out = out + g[..., None] * (hh @ W2[ei] + b2[ei])
            return out
        return _forward(x, edge_index, W_gat, att_src, att_dst, b_gat, ln_gamma, ln_beta, W1, b1, W2, b2)

    def _gn(v, G=32, eps=1e-5):
        B_, C_, H_, W_ = v.shape
        g = v.reshape(B_, G, C_ // G, H_, W_)
        m = jnp.mean(g, axis=(2, 3, 4), keepdims=True)
        s = jnp.var(g, axis=(2, 3, 4), keepdims=True)
        return ((g - m) / jnp.sqrt(s + eps)).reshape(v.shape)

    def _ln_c(v, eps=1e-6):
        m = jnp.mean(v, axis=1, keepdims=True)
        s = jnp.var(v, axis=1, keepdims=True)
        return (v - m) / jnp.sqrt(s + eps)

    def _ln_t(v, eps=1e-5):
        m = jnp.mean(v, axis=-1, keepdims=True)
        s = jnp.var(v, axis=-1, keepdims=True)
        return (v - m) / jnp.sqrt(s + eps)

    def _to_tokens(v):
        B_, C_, H_, W_ = v.shape
        return v.reshape(B_, C_, H_ * W_).transpose(0, 2, 1)
    def _from_tokens(t, like):
        B_, C_, H_, W_ = like.shape
        return t.transpose(0, 2, 1).reshape(B_, C_, H_, W_)

    x = x + _L0_conv_ref(_gn(x), L0_conv_fc1_w, L0_conv_fc1_b, L0_conv_fc2_w, L0_conv_fc2_b, L0_conv_qkv_w, L0_conv_qkv_b, L0_conv_proj_w, L0_conv_proj_b, L0_conv_ffn1_w, L0_conv_ffn1_b, L0_conv_ffn2_w, L0_conv_ffn2_b)
    t = _to_tokens(x)
    t = t + _L1_attn_ref(_ln_t(t), L1_attn_W_in, L1_attn_conv_w, L1_attn_conv_b, L1_attn_dt_bias, L1_attn_A_log, L1_attn_Dp, L1_attn_gnorm_w, L1_attn_norm_w, L1_attn_W_out)
    t = t + _L1_ffn_ref(_ln_t(t), L1_ffn_W_gat, L1_ffn_att_src, L1_ffn_att_dst, L1_ffn_b_gat, L1_ffn_ln_gamma, L1_ffn_ln_beta, L1_ffn_W1, L1_ffn_b1, L1_ffn_W2, L1_ffn_b2, L1_ffn_edge_index)
    x = _from_tokens(t, x)
    return x


_drawn_inputs = setup_inputs


def setup_inputs(seed=0):
    import zlib

    import numpy as np

    out = dict(_drawn_inputs(seed))
    spreads = {'L0_conv_fc1_b': (0.0, 0.8),
     'L0_conv_fc2_b': (0.0, 0.677),
     'L0_conv_qkv_b': (0.0, 0.8),
     'L0_conv_proj_b': (0.0, 0.357),
     'L0_conv_ffn1_b': (0.0, 0.1),
     'L0_conv_ffn2_b': (0.0, 0.1),
     'L1_attn_conv_b': (0.0, 0.1),
     'L1_attn_Dp': (1.0, 0.2),
     'L1_attn_gnorm_w': (1.0, 0.2),
     'L1_attn_norm_w': (1.0, 0.2),
     'L1_ffn_b_gat': (0.0, 0.1),
     'L1_ffn_ln_gamma': (1.0, 0.2),
     'L1_ffn_ln_beta': (0.0, 0.1),
     'L1_ffn_b1': (0.0, 0.339),
     'L1_ffn_b2': (0.0, 0.1)}
    factors = {'L0_conv_fc1_w': 27.012,
     'L0_conv_fc2_w': 8.0,
     'L0_conv_qkv_w': 28.556,
     'L0_conv_proj_w': 8.0,
     'L1_ffn_att_dst': 2.719}
    for name, (base, spread) in spreads.items():
        noise = np.random.default_rng([zlib.crc32(name.encode()), seed]).standard_normal(out[name].shape)
        drawn = base * np.exp(spread * noise) if base else spread * noise
        out[name] = jnp.asarray(drawn.astype(out[name].dtype))
    for name, factor in factors.items():
        out[name] = (out[name] * factor).astype(out[name].dtype)
    return out
```

```python
from contextlib import ExitStack

import numpy as np
import concourse.bass as bass
from concourse import mybir

ALU = mybir.AluOpType
ACT = mybir.ActivationFunctionType
AXX = mybir.AxisListType.X
F32 = mybir.dt.float32
I32 = mybir.dt.int32
U32 = mybir.dt.uint32

P = 128
B, C, HW = 16, 256, 1024
M = B * HW
CH = C // P
HALF = 512


class Steps:

    def __init__(self, eng, sem):
        self.eng, self.sem, self.base, self.k = eng, sem, 0, 0

    def turn(self, base):
        self.base, self.k = base, 0

    def did(self, instruction):
        instruction.then_inc(self.sem, 1)
        self.k += 1

    def wait(self):
        self.eng.wait_ge(self.sem, self.base + self.k)


class Space:

    def __init__(self, nc, ctx, phase):
        self.nc, self.ctx, self.phase, self.signals = nc, ctx, phase, []
        ctx.callback(self.clear_signals)

    def sb(self, name, shape, dt=F32):
        return self.ctx.enter_context(self.nc.sbuf_tensor(f"{self.phase}_{name}", shape, dt))

    def ps(self, name, cols, dt=F32):
        return self.ctx.enter_context(self.nc.psum_tensor(f"{self.phase}_{name}", [P, cols], dt))

    def sem(self, name):
        self.signals.append(self.nc.alloc_semaphore(name=f"{self.phase}_{name}"))
        return self.signals[-1]

    def clear_signals(self):
        self.nc.clear_and_free_semaphores(self.signals)
        self.nc.all_engine_barrier()

    def sems(self, name, n):
        return [self.sem(f"{name}{j}") for j in range(n)]


AD, SC = 16, 32
HID = 4 * C
HID_T = HID // P
NT = HW // P
GN_EPS = 1e-5
VEC_HEAD = 15


def phase_conv(nc, D):
    with ExitStack() as ctx:
        s = Space(nc, ctx, "conv")
        sb, ps, sem, sems = s.sb, s.ps, s.sem, s.sems
        group = sb("group", [P, P])
        fc1 = sb("fc1", [P, CH, 64])
        fc2 = sb("fc2", [64, C])
        wq, wk = sb("wq", [SC, 4 * AD]), sb("wk", [SC, 4 * AD])
        wv = sb("wv", [SC, SC])
        proj = sb("proj", [SC, 2 * SC])
        ffn1 = sb("ffn1", [P, CH, HID])
        ffn2 = sb("ffn2", [P, HID_T, C])
        fc1_b, fc2_b = sb("fc1_b", [64, 1]), sb("fc2_b", [P, CH])
        bq, bk, bv = sb("bq", [AD, 1]), sb("bk", [AD, 1]), sb("bv", [SC, 1])
        proj_b = sb("proj_b", [SC, 1])
        ffn1_b, ffn2_b = sb("ffn1_b", [P, HID_T]), sb("ffn2_b", [P, CH])
        ident = sb("ident", [P, P])
        loads = [(group, "c_group"), (fc1, "fc1"), (fc2, "fc2"), (wq, "wq"), (wk, "wk"), (wv, "wv"),
                 (proj, "proj"), (ffn1, "ffn1"), (ffn2, "ffn2"), (fc1_b, "fc1_b"), (fc2_b, "fc2_b"),
                 (bq, "bq"), (bk, "bk"), (bv, "bv"), (proj_b, "proj_b"), (ffn1_b, "ffn1_b"),
                 (ffn2_b, "ffn2_b"), (ident, "c_ident")]
        nfc2_b, fence = sb("nfc2_b", [P, CH]), sb("fence", [P, 1])
        ones = sb("ones", [33, 2 * SC])
        X = [sb(f"X{u}", [P, CH, HW]) for u in range(2)]
        Y = [sb(f"Y{u}", [P, CH, HW]) for u in range(2)]
        T = [sb(f"T{u}", [P, CH, HW]) for u in range(2)]
        stats, mv = sb("stats", [P, CH, 2, 6]), sb("mv", [P, CH, 2])
        sq, st2 = sb("sq", [P, CH]), sb("st2", [P, 4])
        gs, var, sd, rs = sb("gs", [P, 4]), sb("var", [P, CH]), sb("sd", [P, CH]), sb("rs", [P, CH])
        nmr, sein = sb("nmr", [P, CH]), sb("sein", [P, CH])
        f1, ex, gate = sb("f1", [64, 1]), sb("ex", [P, CH]), sb("gate", [P, CH])
        scale, shift = sb("scale", [P, CH]), sb("shift", [P, CH])
        qq, kk = sb("qq", [AD + 1, HW]), sb("kk", [AD + 1, HW])
        vT = sb("vT", [P, NT, SC + 1])
        nmax, nmaxT = sb("nmax", [P, NT]), sb("nmaxT", [NT, P])
        PR = sb("PR", [P, NT, HW])
        rrow, osb, att = sb("rrow", [33, HW]), sb("osb", [SC, HW]), sb("att", [SC, HW])
        H = sb("H", [P, HID_T, HALF])
        pA, pB, pO = ps("pA", HW), ps("pB", HW), ps("pO", HW)
        pM, pF = ps("pM", HALF), ps("pF", HALF)
        pAB = [pA, pB]
        banks = [pA[:, 0:HALF], pA[:, HALF:HW], pB[:, 0:HALF], pB[:, HALF:HW]]

        weights_in, consts = sem("weights_in"), sem("consts")
        x_in, x_free = sems("x_in", 2), sems("x_free", 2)
        vec, gs_done, var_done, sd_done = sem("vec"), sem("gs_done"), sem("var_done"), sem("sd_done")
        st2_done, sein_done = sem("st2_done"), sem("sein_done")
        fc1_done, f1_done, fc2_done, ex_done = sem("fc1_done"), sem("f1_done"), sem("fc2_done"), sem("ex_done")
        y_done, qk_done, q_in, v_done, vT_in = sem("y_done"), sem("qk_done"), sem("q_in"), sem("v_done"), sem("vT_in")
        s_done, max_done = sem("s_done"), sem("max_done")
        maxT_done, maxT_in, nmax_in = sem("maxT_done"), sem("maxT_in"), sem("nmax_in")
        st_done, exp_done, pv_done = sem("st_done"), sem("exp_done"), sem("pv_done")
        rrow_done, bc_done, att_done, proj_done, y0_done = sem("rrow_done"), sem("bc_done"), sem("att_done"), sem("proj_done"), sem("y0_done")
        h_done, relu_done, o_done, t_done = sem("h_done"), sem("relu_done"), sem("o_done"), sem("t_done")
        t_out = sems("t_out", 2)
        block = ctx.enter_context(nc.Block())
        tv = D["t1"]

        @block.gpsimd
        def _(pool):
            pool.memset(ones[:, :], 1.0).then_inc(consts, 1)
            pool.memset(vT[:, :, SC:SC + 1], 1.0).then_inc(consts, 1)
            pool.memset(kk[:, :], 1.0).then_inc(consts, 1)
            with pool.Fori(0, B // 2) as i:
                n16 = pool.snap(i * 16 + 16)
                for u in range(2):
                    pool.wait_ge(x_free[u], n16)
                    pool.dma_start(X[u][:, :, :], D["x"][i * 2 + u].rearrange("(h p) n -> p h n", p=P)).then_inc(x_in[u], 16)

        @block.sync
        def _(sync):
            for dst, name in loads:
                sync.dma_start(dst[tuple(slice(None) for _ in dst.shape)], D[name]).then_inc(weights_in, 16)
            with sync.Fori(0, B // 2) as i:
                b0 = sync.snap(i * 2)
                for u in range(2):
                    sync.wait_ge(maxT_in, b0 + (u + 1))
                    sync.dma_start(qq[AD:AD + 1, :].rearrange("a (t p) -> a t p", p=P), nmaxT[:, :]).then_inc(nmax_in, 16)
                    sync.wait_ge(t_done, b0 * 4 + 4 * (u + 1))
                    sync.dma_start(tv[i * 2 + u].rearrange("(h p) n -> p h n", p=P), T[u][:, :, :]).then_inc(t_out[u], 16)
            for u in range(2):
                sync.wait_ge(t_out[u], 16 * (B // 2 + 1))

        @block.vector
        def _(v):
            own = Steps(v, vec)
            v.wait_ge(weights_in, 16 * len(loads))
            v.tensor_scalar(nfc2_b[:, :], fc2_b[:, :], -1.0, None, ALU.mult).then_inc(consts, 1)
            for u in range(2):
                v.sem_inc(x_free[u], 16)
                v.sem_inc(t_out[u], 16)
            with v.Fori(0, B // 2) as i:
                b0 = v.snap(i * 2)
                for u in range(2):
                    own.turn(i * (2 * VEC_HEAD) + u * VEC_HEAD)
                    b1 = v.snap(b0 + (u + 1))
                    v.wait_ge(x_in[u], i * 16 + 16)
                    for h in range(CH):
                        for c in range(2):
                            ins = v.bn_stats(stats[:, h, c, :], X[u][:, h, c * HALF:(c + 1) * HALF])
                    own.did(ins)
                    own.wait()
                    v.memset(fence[:, :], 0.0)
                    for h in range(CH):
                        ins = v.bn_aggr(mv[:, h, :], stats[:, h, :, :])
                    own.did(ins)
                    own.wait()
                    v.tensor_copy(st2[:, 0:2], mv[:, :, 0])
                    own.did(v.tensor_tensor(sq[:, :], mv[:, :, 0], mv[:, :, 0], ALU.mult))
                    own.wait()
                    v.tensor_tensor(st2[:, 2:4], sq[:, :], mv[:, :, 1], ALU.add).then_inc(st2_done, 1)
                    v.wait_ge(gs_done, b1)
                    own.did(v.tensor_copy(gs[:, :], pM[:, 0:4]))
                    own.wait()
                    own.did(v.tensor_tensor(sq[:, :], gs[:, 0:2], gs[:, 0:2], ALU.mult))
                    own.wait()
                    own.did(v.tensor_tensor(var[:, :], gs[:, 2:4], sq[:, :], ALU.subtract))
                    own.wait()
                    v.tensor_scalar(var[:, :], var[:, :], 0.0, GN_EPS, ALU.max, ALU.add).then_inc(var_done, 1)
                    v.wait_ge(sd_done, b1)
                    own.did(v.reciprocal(rs[:, :], sd[:, :]))
                    own.wait()
                    own.did(v.scalar_tensor_tensor(nmr[:, :], gs[:, 0:2], -1.0, rs[:, :], ALU.mult, ALU.mult))
                    own.did(v.tensor_tensor(sein[:, :], st2[:, 0:2], rs[:, :], ALU.mult))
                    own.wait()
                    v.tensor_tensor(sein[:, :], sein[:, :], nmr[:, :], ALU.add).then_inc(sein_done, 1)
                    v.wait_ge(ex_done, b1)
                    own.did(v.tensor_scalar(gate[:, :], ex[:, :], 1.0, None, ALU.add))
                    own.wait()
                    own.did(v.reciprocal(gate[:, :], gate[:, :]))
                    own.wait()
                    own.did(v.tensor_tensor(scale[:, :], rs[:, :], gate[:, :], ALU.mult))
                    own.did(v.tensor_tensor(shift[:, :], nmr[:, :], gate[:, :], ALU.mult))
                    own.wait()
                    for h in range(CH):
                        ins = v.tensor_scalar(Y[u][:, h, :], X[u][:, h, :], scale[:, h:h + 1], shift[:, h:h + 1], ALU.mult, ALU.add)
                    ins.then_inc(y_done, 1)
                    v.wait_ge(v_done, b1)
                    v.tensor_copy(vT[:, :, 0:SC], pF[:, 0:NT * SC].rearrange("p (t c) -> p t c", c=SC)).then_inc(vT_in, 1)
                    for t in range(NT):
                        v.wait_ge(s_done, b0 * NT + (u * NT + t + 1))
                        v.tensor_reduce(nmax[:, t:t + 1], pAB[t % 2][:, :], AXX, ALU.max, negate=True).then_inc(max_done, 1)
                    v.wait_ge(maxT_done, b1)
                    v.tensor_copy(nmaxT[:, :], pM[0:NT, 0:P]).then_inc(maxT_in, 1)
                    v.wait_ge(pv_done, b1)
                    v.reciprocal(rrow[SC:SC + 1, :], pO[SC:SC + 1, :]).then_inc(rrow_done, 1)
                    own.did(v.tensor_copy(osb[:, :], pO[0:SC, :]))
                    v.wait_ge(bc_done, b1)
                    own.wait()
                    own.did(v.tensor_tensor(att[:, :], osb[:, :], pA[0:SC, :], ALU.mult))
                    own.wait()
                    v.tensor_scalar(att[:, :], att[:, :], bv[:, 0:1], None, ALU.add).then_inc(att_done, 1)
                    v.wait_ge(proj_done, b1)
                    v.tensor_scalar(Y[u][0:SC, 0, :], pB[0:SC, :], proj_b[:, 0:1], None, ALU.add).then_inc(y0_done, 1)
                    v.wait_ge(t_out[u], i * 16 + 16)
                    for th in range(2):
                        for o in range(CH):
                            k = th * CH + o
                            v.wait_ge(o_done, b0 * 4 + (u * 4 + k + 1))
                            cols = slice(th * HALF, (th + 1) * HALF)
                            ins = v.scalar_tensor_tensor(T[u][:, o, cols], pO[:, o * HALF:(o + 1) * HALF], ffn2_b[:, o:o + 1],
                                                         X[u][:, o, cols], ALU.add, ALU.add)
                            ins.then_inc(t_done, 1)
                    v.wait_ge(t_done, b0 * 4 + 4 * (u + 1))
                    v.sem_inc(x_free[u], 16)
            assert own.k == VEC_HEAD

        @block.tensor
        def _(pe):
            pe.wait_ge(weights_in, 16 * len(loads))
            pe.wait_ge(consts, 4)
            with pe.Fori(0, B // 2) as i:
                b0 = pe.snap(i * 2)
                for u in range(2):
                    b1 = pe.snap(b0 + (u + 1))
                    pe.wait_ge(st2_done, b1)
                    pe.matmul(pM[:, 0:4], group[:, :], st2[:, :], start=True, stop=True).then_inc(gs_done, 1)
                    pe.wait_ge(sein_done, b1)
                    for h in range(CH):
                        mm = pe.matmul(pM[0:64, 4:5], fc1[:, h, :], sein[:, h:h + 1], start=(h == 0), stop=(h == CH - 1))
                    mm.then_inc(fc1_done, 1)
                    pe.wait_ge(f1_done, b1)
                    for h in range(CH):
                        mm = pe.matmul(pM[:, 5 + h:6 + h], fc2[:, h * P:(h + 1) * P], f1[:, :], start=True, stop=True)
                    mm.then_inc(fc2_done, 1)
                    pe.wait_ge(y_done, b1)
                    for j in range(2):
                        cols = slice(j * HALF, (j + 1) * HALF)
                        pe.matmul(pA[0:4 * AD, cols], wq[:, :], Y[u][0:SC, 0, cols], start=True, stop=True)
                        mm = pe.matmul(pB[0:4 * AD, cols], wk[:, :], Y[u][0:SC, 0, cols], start=True, stop=True)
                    mm.then_inc(qk_done, 1)
                    for t in range(NT):
                        mm = pe.matmul(pF[:, t * SC:(t + 1) * SC], Y[u][0:SC, 0, t * P:(t + 1) * P], wv[:, :], start=True, stop=True)
                    mm.then_inc(v_done, 1)
                    pe.wait_ge(q_in, b1)
                    for t in range(NT):
                        if t >= 2:
                            pe.wait_ge(max_done, b0 * NT + (u * NT + t - 1))
                        for j in range(2):
                            mm = pe.matmul(pAB[t % 2][:, j * HALF:(j + 1) * HALF], qq[0:AD, t * P:(t + 1) * P],
                                           kk[0:AD, j * HALF:(j + 1) * HALF], start=True, stop=True)
                        mm.then_inc(s_done, 1)
                    pe.wait_ge(max_done, b0 * NT + (u + 1) * NT)
                    pe.transpose(pM[0:NT, 0:P], nmax[:, :], ident[:, :]).then_inc(maxT_done, 1)
                    pe.wait_ge(nmax_in, b1 * 16)
                    pe.wait_ge(vT_in, b1)

                    def weighted(t):
                        pe.wait_ge(exp_done, b0 * NT + (u * NT + t + 1))
                        for j in range(2):
                            mm = pe.matmul(pO[0:SC + 1, j * HALF:(j + 1) * HALF], vT[:, t, :], PR[:, t, j * HALF:(j + 1) * HALF],
                                           start=(t == 0), stop=(t == NT - 1))
                        return mm

                    for t in range(NT):
                        if t >= 2:
                            pe.wait_ge(exp_done, b0 * NT + (u * NT + t - 1))
                        for j in range(2):
                            mm = pe.matmul(pAB[t % 2][:, j * HALF:(j + 1) * HALF], kk[0:AD + 1, t * P:(t + 1) * P],
                                           qq[0:AD + 1, j * HALF:(j + 1) * HALF], start=True, stop=True)
                        mm.then_inc(st_done, 1)
                        if t >= 1:
                            weighted(t - 1)
                    weighted(NT - 1).then_inc(pv_done, 1)
                    pe.wait_ge(rrow_done, b1)
                    for j in range(2):
                        mm = pe.matmul(pA[0:2 * SC, j * HALF:(j + 1) * HALF], ones[SC:SC + 1, :], rrow[SC:SC + 1, j * HALF:(j + 1) * HALF],
                                       start=True, stop=True)
                    mm.then_inc(bc_done, 1)
                    pe.wait_ge(att_done, b1)
                    for j in range(2):
                        mm = pe.matmul(pB[0:2 * SC, j * HALF:(j + 1) * HALF], proj[:, :], att[:, j * HALF:(j + 1) * HALF], start=True, stop=True)
                    mm.then_inc(proj_done, 1)
                    pe.wait_ge(y0_done, b1)
                    for th in range(2):
                        cols = slice(th * HALF, (th + 1) * HALF)
                        for f in range(HID_T):
                            g = th * HID_T + f
                            if g >= 4:
                                pe.wait_ge(relu_done, b0 * 2 * HID_T + (u * 2 * HID_T + g - 3))
                            for h in range(CH):
                                mm = pe.matmul(banks[g % 4], ffn1[:, h, f * P:(f + 1) * P], Y[u][:, h, cols], start=(h == 0), stop=(h == CH - 1))
                            mm.then_inc(h_done, 1)
                        pe.wait_ge(relu_done, b0 * 2 * HID_T + (u * 2 + th + 1) * HID_T)
                        for o in range(CH):
                            if th:
                                pe.wait_ge(t_done, b0 * 4 + (u * 4 + o + 1))
                            for f in range(HID_T):
                                mm = pe.matmul(pO[:, o * HALF:(o + 1) * HALF], ffn2[:, f, o * P:(o + 1) * P], H[:, f, :],
                                               start=(f == 0), stop=(f == HID_T - 1))
                            mm.then_inc(o_done, 1)

        @block.scalar
        def _(act):
            act.wait_ge(weights_in, 16 * len(loads))
            act.wait_ge(consts, 4)
            with act.Fori(0, B // 2) as i:
                b0 = act.snap(i * 2)
                for u in range(2):
                    b1 = act.snap(b0 + (u + 1))
                    act.wait_ge(var_done, b1)
                    act.activation(sd[:, :], var[:, :], ACT.Sqrt).then_inc(sd_done, 1)
                    act.wait_ge(fc1_done, b1)
                    act.activation(f1[:, :], pM[0:64, 4:5], ACT.Relu, bias=fc1_b[:, 0:1]).then_inc(f1_done, 1)
                    act.wait_ge(fc2_done, b1)
                    for h in range(CH):
                        ins = act.activation(ex[:, h:h + 1], pM[:, 5 + h:6 + h], ACT.Exp, bias=nfc2_b[:, h:h + 1], scale=-1.0)
                    ins.then_inc(ex_done, 1)
                    act.wait_ge(qk_done, b1)
                    act.activation(qq[0:AD, :], pA[0:AD, :], ACT.Identity, bias=bq[:, 0:1])
                    act.activation(kk[0:AD, :], pB[0:AD, :], ACT.Identity, bias=bk[:, 0:1]).then_inc(q_in, 1)
                    for t in range(NT):
                        act.wait_ge(st_done, b0 * NT + (u * NT + t + 1))
                        act.activation(PR[:, t, :], pAB[t % 2][:, :], ACT.Exp, scale=float(AD) ** -0.5).then_inc(exp_done, 1)
                    for th in range(2):
                        if th:
                            act.wait_ge(o_done, b0 * 4 + (u * 4 + CH))
                        for f in range(HID_T):
                            g = th * HID_T + f
                            act.wait_ge(h_done, b0 * 2 * HID_T + (u * 2 * HID_T + g + 1))
                            act.activation(H[:, f, :], banks[g % 4], ACT.Relu, bias=ffn1_b[:, f:f + 1]).then_inc(relu_done, 1)


DI = 512
NH, HD, DS = 8, 64, 64
KC = 4
NX = DI // P
ST = 512
NSUP = HW // ST
NC_ = ST // P
NG = NSUP * NC_
LN_EPS = 1e-5
RMS_EPS = float(np.finfo(np.float32).eps)
CREDIT = 2
SSM_STEPS = 122


def phase_ssm(nc, D):
    with ExitStack() as ctx:
        s_ = Space(nc, ctx, "ssm")
        sb, ps, sem, sems = s_.sb, s_.ps, s_.sem, s_.sems
        w_x = sb("w_x", [P, CH, DI + 2 * DS])
        w_z = sb("w_z", [P, CH, DI])
        w_dt = sb("w_dt", [P, CH, NH])
        w_out = sb("w_out", [P, NX, C])
        norm_w, gnorm_w = sb("norm_w", [P, CH]), sb("gnorm_w", [P, NX])
        conv_w, conv_b = sb("conv_w", [P, NX + 2, KC]), sb("conv_b", [P, NX + 2])
        dt_b, a_log, dp = sb("dt_b", [P, NH]), sb("a_log", [P, NH]), sb("dp", [P, NH])
        ident, upper, ones = sb("ident", [P, P]), sb("upper", [P, P]), sb("ones", [P, P])
        loads = [(w_x, "w_x"), (w_z, "w_z"), (w_dt, "w_dt"), (w_out, "w_out"), (norm_w, "norm_w"), (gnorm_w, "gnorm_w"),
                 (conv_w, "conv_w"), (conv_b, "conv_b"), (dt_b, "dt_b"), (a_log, "a_log"), (dp, "dp"),
                 (ident, "c_ident"), (upper, "c_upper")]
        neg_a, fence = sb("neg_a", [P, NH]), sb("fence", [P, 1])
        X = [sb(f"X{s}", [P, CH, ST]) for s in range(NSUP)]
        tT = sb("tT", [P, NC_, C])
        stats, mv = sb("stats", [P, NC_, 6]), sb("mv", [P, NC_, 2])
        ve, rstd, ve2, r2, xr = (sb(n, [P, NC_]) for n in ("ve", "rstd", "ve2", "r2", "xr"))
        xnT = [sb(f"xnT{j}", [P, C]) for j in range(NC_)]
        xnF = sb("xnF", [P, CH, ST])
        XC = [sb(f"XC{s}", [P, NX + 2, KC - 1 + ST]) for s in range(NSUP)]
        CV = sb("CV", [P, NX + 2, ST])
        XS = sb("XS", [P, NX + 2, ST])
        zs = sb("zs", [P, NC_, DI])
        dv, de, du, dd, dt4, dtA = (sb(n, [P, NC_, NH]) for n in ("dv", "de", "du", "dd", "dt4", "dtA"))
        cumS = [sb(f"cumS{j}", [P, 2 * NH]) for j in range(2)]
        sm = [sb(f"sm{j}", [P, 3, NH]) for j in range(2)]
        se = [sb(f"se{j}", [P, 3, NH]) for j in range(2)]
        dec = [sb(f"dec{j}", [P, NH, P]) for j in range(2)]
        Mm = [sb(f"Mm{j}", [P, P]) for j in range(2)]
        BT = [sb(f"BT{j}", [P, DS]) for j in range(2)]
        xdt = [sb(f"xdt{j}", [P, DI]) for j in range(2)]
        xw = [sb(f"xw{j}", [P, DI]) for j in range(2)]
        xd = [sb(f"xd{j}", [P, DI]) for j in range(2)]
        ya = [sb(f"ya{j}", [P, DI]) for j in range(2)]
        state, state_dec = sb("state", [DS, DI]), sb("state_dec", [DS, DI])
        squares = sb("squares", [P, DI])
        ss = sb("ss", [P, NC_])
        vr, rr = sb("vr", [P, NC_]), sb("rr", [P, NC_])
        gF = sb("gF", [P, NX, P])
        oT = sb("oT", [P, NC_, C])
        OUT = [sb(f"OUT{s}", [P, NC_, C]) for s in range(NSUP)]
        k_t, k_p0, k_p1, k_s = ps("k_t", 512), ps("k_p0", 512), ps("k_p1", 512), ps("k_s", 512)
        k_decay, k_y, k_off = ps("k_decay", 1024), ps("k_y", 512), ps("k_off", 512)
        kp = [k_p0, k_p1]
        k_turn = [k_t, k_y]
        DTP, CUM, TOT, MT, BTP = (k_s[:, a:a + n] for a, n in ((0, 32), (32, NH), (32 + NH, NH), (128, P), (256, DS)))

        weights_in, consts, own_s = sem("weights_in"), sem("consts"), sem("vec")
        names = ("t_turned sq1_in sq1 sq2_in sq2 xn_in xn_turned xnF_in xc_done xc_in cv_in silu_in z_done z_in dt_done "
                 "dabs_in dexp_in du_in dln_in dt_in cum_done xs_turned t_in dec_in exp_in sm_in se_in bt_in xdt_in xw_in w_in px_read "
                 "y_done off_done snew_done h_in g_in g_turned gf_in o_done o_in ss_in rr_in rrs t2_in").split()
        S = {n: sem(n) for n in names}
        x_in, out_out = sems("x_in", NSUP), sems("out_out", NSUP)
        block = ctx.enter_context(nc.Block())

        def need(eng, name, value):
            eng.wait_ge(S[name], value + CREDIT)

        by_engine = {"act": "sq1 sq2 xnF_in xc_in silu_in z_in dexp_in dln_in exp_in se_in gf_in o_in ss_in rrs",
                     "pe": "t_turned xn_turned xc_done z_done dt_done cum_done xs_turned y_done off_done snew_done g_turned o_done"}

        def credit(eng, which):
            mine = by_engine[which].split() if which in by_engine else [n for n in names if n not in " ".join(by_engine.values()).split()]
            for n in mine:
                eng.sem_inc(S[n], CREDIT)

        @block.gpsimd
        def _(pool):
            pool.memset(ones[:, :], 1.0).then_inc(consts, 1)
            pool.memset(XC[0][:, :, 0:KC - 1], 0.0).then_inc(consts, 1)
            pool.memset(XC[1][:, NX:NX + 2, :], 0.0).then_inc(consts, 1)
            pool.memset(XC[0][:, NX:NX + 2, KC - 1:], 0.0).then_inc(consts, 1)
            with pool.Fori(0, B) as i:
                for s in range(NSUP):
                    need(pool, "sq1_in", i * NSUP + (s + 1 - NSUP))
                    pool.dma_start(X[s][:, :, :], D["t1"][i].rearrange("(h p) n -> p h n", p=P)[:, :, s * ST:(s + 1) * ST]).then_inc(x_in[s], 16)

        @block.sync
        def _(sync):
            for dst, name in loads:
                sync.dma_start(dst[tuple(slice(None) for _ in dst.shape)], D[name]).then_inc(weights_in, 16)
            with sync.Fori(0, B) as i:
                for s in range(NSUP):
                    need(sync, "t2_in", i * NG + (s + 1) * NC_)
                    sync.dma_start(D["t2"][i].rearrange("(s c p) f -> s p c f", p=P, c=NC_)[s], OUT[s][:, :, :]).then_inc(out_out[s], 16)
            for s in range(NSUP):
                sync.wait_ge(out_out[s], 16 * (B + 1))

        @block.vector
        def _(v):
            own = Steps(v, own_s)
            v.wait_ge(weights_in, 16 * len(loads))
            for s in range(NSUP):
                v.sem_inc(out_out[s], 16)
            for k in range(CH):
                for w in (w_x, w_z, w_dt):
                    v.tensor_scalar(w[:, k, :], w[:, k, :], norm_w[:, k:k + 1], None, ALU.mult)
            for k in range(NX):
                ins = v.tensor_scalar(w_out[:, k, :], w_out[:, k, :], gnorm_w[:, k:k + 1], None, ALU.mult)
            ins.then_inc(consts, 1)
            v.wait_ge(consts, 6)
            v.tensor_scalar(neg_a[:, :], neg_a[:, :], -1.0, None, ALU.mult).then_inc(consts, 1)
            v.wait_ge(consts, 7)
            credit(v, "v")
            with v.Fori(0, B) as i:
                own.turn(i * SSM_STEPS)
                g0, s0 = v.snap(i * NG), v.snap(i * NSUP)
                for s in range(NSUP):
                    s1 = v.snap(s0 + (s + 1))
                    for q in range(2):
                        need(v, "t_turned", i * 2 * NSUP + (s * 2 + q + 1))
                        v.tensor_copy(tT[:, 2 * q:2 * q + 2, :], k_turn[q][:, :].rearrange("p (c f) -> p c f", c=2)).then_inc(S["t_in"], 1)
                    need(v, "t_in", i * 2 * NSUP + (s + 1) * 2)
                    for c in range(NC_):
                        ins = v.bn_stats(stats[:, c, :], tT[:, c, :])
                    own.did(ins)
                    own.wait()
                    v.memset(fence[:, :], 0.0)
                    for c in range(NC_):
                        ins = v.bn_aggr(mv[:, c, :], stats[:, c, :])
                    own.did(ins)
                    own.wait()
                    v.tensor_scalar(ve[:, :], mv[:, :, 1], LN_EPS, None, ALU.add).then_inc(S["sq1_in"], 1)
                    need(v, "sq1", s1)
                    own.did(v.reciprocal(rstd[:, :], rstd[:, :]))
                    own.wait()
                    own.did(v.tensor_tensor(ve2[:, :], mv[:, :, 1], rstd[:, :], ALU.mult))
                    own.wait()
                    own.did(v.tensor_tensor(ve2[:, :], ve2[:, :], rstd[:, :], ALU.mult))
                    own.wait()
                    v.tensor_scalar(ve2[:, :], ve2[:, :], RMS_EPS, None, ALU.add).then_inc(S["sq2_in"], 1)
                    need(v, "sq2", s1)
                    own.did(v.reciprocal(r2[:, :], r2[:, :]))
                    own.wait()
                    own.did(v.tensor_tensor(xr[:, :], r2[:, :], rstd[:, :], ALU.mult))
                    own.wait()
                    for c in range(NC_):
                        v.tensor_scalar(xnT[c][:, :], tT[:, c, :], mv[:, c, 0:1], xr[:, c:c + 1], ALU.subtract, ALU.mult).then_inc(S["xn_in"], 1)
                    if s:
                        own.did(v.tensor_copy(XC[s][:, :, 0:KC - 1], XC[0][:, :, ST:ST + KC - 1]))
                    for m in range(NX + 2):
                        need(v, "xc_in", s0 * (NX + 2) + (s * (NX + 2) + m + 1))
                        rows = P if m < NX else DS
                        own.wait()
                        own.did(v.tensor_scalar(CV[0:rows, m, :], XC[s][0:rows, m, 0:ST], conv_w[0:rows, m, 0:1], None, ALU.mult))
                        for k in range(1, KC):
                            own.wait()
                            ins = v.scalar_tensor_tensor(CV[0:rows, m, :], XC[s][0:rows, m, k:k + ST], conv_w[0:rows, m, k:k + 1], CV[0:rows, m, :], ALU.mult, ALU.add)
                            if k < KC - 1:
                                own.did(ins)
                        ins.then_inc(S["cv_in"], 1)
                    need(v, "dt_done", s1)
                    own.did(v.tensor_tensor(dv[:, :, :], DTP.rearrange("p (c h) -> p c h", h=NH), dt_b[:, :].unsqueeze(1).to_broadcast([P, NC_, NH]), ALU.add))
                    own.wait()
                    v.scalar_tensor_tensor(de[:, :, :], dv[:, :, :], -1.0, dv[:, :, :], ALU.mult, ALU.max).then_inc(S["dabs_in"], 1)
                    need(v, "dexp_in", s1)
                    v.tensor_scalar(du[:, :, :], de[:, :, :], 1.0, None, ALU.add).then_inc(S["du_in"], 1)
                    need(v, "du_in", s1)
                    own.did(v.tensor_scalar(dd[:, :, :], du[:, :, :], 1.0, None, ALU.subtract))
                    own.wait()
                    own.did(v.tensor_scalar(dtA[:, :, :], dd[:, :, :], 0.0, None, ALU.is_equal))
                    own.did(v.tensor_scalar(dd[:, :, :], dd[:, :, :], 1e-30, None, ALU.max))
                    own.wait()
                    own.did(v.reciprocal(dd[:, :, :], dd[:, :, :]))
                    own.wait()
                    need(v, "dln_in", s1)
                    own.did(v.tensor_tensor(dd[:, :, :], dt4[:, :, :], dd[:, :, :], ALU.mult))
                    own.wait()
                    own.did(v.tensor_tensor(dd[:, :, :], dtA[:, :, :], dd[:, :, :], ALU.add))
                    own.wait()
                    own.did(v.tensor_tensor(dd[:, :, :], de[:, :, :], dd[:, :, :], ALU.mult))
                    own.wait()
                    own.did(v.scalar_tensor_tensor(dt4[:, :, :], dv[:, :, :], 0.0, dd[:, :, :], ALU.max, ALU.add))
                    own.wait()
                    v.tensor_tensor(dtA[:, :, :], dt4[:, :, :], neg_a[:, :].unsqueeze(1).to_broadcast([P, NC_, NH]), ALU.mult).then_inc(S["dt_in"], 1)
                    for c in range(NC_):
                        g, j = s * NC_ + c, c % 2
                        g1 = v.snap(g0 + (g + 1))
                        if g == 0:
                            v.memset(state[:, :], 0.0).then_inc(S["h_in"], 1)
                        need(v, "cum_done", g1)
                        own.did(v.tensor_copy(cumS[j][:, :], k_s[:, 32:32 + 2 * NH]))
                        own.wait()
                        v.tensor_tensor(sm[j][:, 0, :], cumS[j][:, NH:2 * NH], cumS[j][:, 0:NH], ALU.subtract)
                        v.tensor_copy(sm[j][:, 1:3, :], cumS[j][:, :].rearrange("p (a h) -> p a h", h=NH)).then_inc(S["sm_in"], 1)
                        for h in range(NH):
                            ins = v.tensor_scalar(dec[j][:, h, :], k_decay[:, h * P:(h + 1) * P], cumS[j][:, h:h + 1], 0.0, ALU.subtract, ALU.min)
                        ins.then_inc(S["dec_in"], 1)
                        own.did(v.tensor_tensor(Mm[j][:, :], MT, upper[:, :], ALU.mult))
                        v.tensor_copy(BT[j][:, :], BTP).then_inc(S["bt_in"], 1)
                        need(v, "xs_turned", g1)
                        heads = k_p0[:, :].rearrange("p (h d) -> p h d", h=NH)
                        v.tensor_tensor(xdt[j][:, :].rearrange("p (h d) -> p h d", h=NH), heads, dt4[:, c, :].unsqueeze(2).to_broadcast([P, NH, HD]), ALU.mult).then_inc(S["xdt_in"], 1)
                        v.tensor_tensor(xd[j][:, :].rearrange("p (h d) -> p h d", h=NH), heads, dp[:, :].unsqueeze(2).to_broadcast([P, NH, HD]), ALU.mult).then_inc(S["px_read"], 1)
                        need(v, "se_in", g1)
                        need(v, "xdt_in", g1)
                        v.tensor_tensor(xw[j][:, :].rearrange("p (h d) -> p h d", h=NH), xdt[j][:, :].rearrange("p (h d) -> p h d", h=NH),
                                        se[j][:, 0, :].unsqueeze(2).to_broadcast([P, NH, HD]), ALU.mult).then_inc(S["xw_in"], 1)
                        need(v, "exp_in", g1)
                        own.wait()
                        v.tensor_tensor(dec[j][:, :, :], dec[j][:, :, :], Mm[j][:, :].unsqueeze(1).to_broadcast([P, NH, P]), ALU.mult).then_inc(S["w_in"], 1)
                        need(v, "off_done", g1)
                        own.did(v.tensor_tensor(ya[j][:, :].rearrange("p (h d) -> p h d", h=NH), k_off[:, :].rearrange("p (h d) -> p h d", h=NH),
                                                se[j][:, 1, :].unsqueeze(2).to_broadcast([P, NH, HD]), ALU.mult))
                        if g < NG - 1:
                            own.did(v.tensor_tensor(state_dec[:, :].rearrange("p (h d) -> p h d", h=NH), state[:, :].rearrange("p (h d) -> p h d", h=NH),
                                                    se[j][0:DS, 2, :].unsqueeze(2).to_broadcast([DS, NH, HD]), ALU.mult))
                            need(v, "snew_done", i * (NG - 1) + (g + 1))
                            own.wait()
                            v.tensor_tensor(state[:, :], state_dec[:, :], k_p1[0:DS, :], ALU.add).then_inc(S["h_in"], 1)
                        need(v, "y_done", g1)
                        own.wait()
                        own.did(v.tensor_tensor(ya[j][:, :], ya[j][:, :], k_y[:, :], ALU.add))
                        need(v, "px_read", g1)
                        own.wait()
                        own.did(v.tensor_tensor(ya[j][:, :], ya[j][:, :], xd[j][:, :], ALU.add))
                        need(v, "z_in", g1)
                        own.wait()
                        v.tensor_tensor(ya[j][:, :], ya[j][:, :], zs[:, c, :], ALU.mult).then_inc(S["g_in"], 1)
                    need(v, "ss_in", g0 + (s + 1) * NC_)
                    v.tensor_scalar(vr[:, :], ss[:, :], 1.0 / DI, LN_EPS, ALU.mult, ALU.add).then_inc(S["rr_in"], 1)
                    need(v, "rrs", s1)
                    own.did(v.reciprocal(rr[:, :], rr[:, :]))
                    own.wait()
                    v.wait_ge(out_out[s], i * 16 + 16)
                    for c in range(NC_):
                        need(v, "o_in", g0 + (s * NC_ + c + 1))
                        ins = v.scalar_tensor_tensor(oT[:, c, :], oT[:, c, :], rr[:, c:c + 1], tT[:, c, :], ALU.mult, ALU.add)
                        v.tensor_scalar(OUT[s][:, c, :], tT[:, c, :], mv[:, c, 0:1], rstd[:, c:c + 1], ALU.subtract, ALU.mult)
                    own.did(ins)
                    own.did(v.tensor_scalar(vr[:, :], vr[:, :], 1.0, None, ALU.mult))
                    own.wait()
                    for c in range(NC_):
                        v.tensor_tensor(OUT[s][:, c, :], OUT[s][:, c, :], oT[:, c, :], ALU.add).then_inc(S["t2_in"], 1)
            assert own.k == SSM_STEPS

        @block.tensor
        def _(pe):
            pe.wait_ge(weights_in, 16 * len(loads))
            pe.wait_ge(consts, 7)
            credit(pe, "pe")
            with pe.Fori(0, B) as i:
                g0, s0 = pe.snap(i * NG), pe.snap(i * NSUP)
                for s in range(NSUP):
                    s1 = pe.snap(s0 + (s + 1))
                    pe.wait_ge(x_in[s], i * 16 + 16)
                    need(pe, "o_in", g0 + s * NC_)
                    for c in range(NC_):
                        for k in range(CH):
                            mm = pe.transpose(k_turn[c // 2][:, (c % 2) * C + k * P:(c % 2) * C + (k + 1) * P], X[s][:, k, c * P:(c + 1) * P], ident[:, :])
                        if c % 2:
                            mm.then_inc(S["t_turned"], 1)
                    for c in range(NC_):
                        need(pe, "xn_in", g0 + (s * NC_ + c + 1))
                        for k in range(CH):
                            mm = pe.transpose(k_turn[c // 2][:, (c % 2) * C + k * P:(c % 2) * C + (k + 1) * P], xnT[c][:, k * P:(k + 1) * P], ident[:, :])
                        if c % 2:
                            mm.then_inc(S["xn_turned"], 1)
                    need(pe, "xnF_in", i * 2 * NSUP + (s + 1) * 2)
                    need(pe, "px_read", g0 + s * NC_)
                    need(pe, "h_in", g0 + s * NC_) if s else None
                    n = 0
                    for m in range(NX + 2):
                        rows = P if m < NX else DS
                        at = m * P if m < NX else DI + (m - NX) * DS
                        if m >= 2:
                            need(pe, "xc_in", s0 * (NX + 2) + (s * (NX + 2) + m - 1))
                        for k in range(CH):
                            mm = pe.matmul(kp[m % 2][0:rows, :], w_x[:, k, at:at + rows], xnF[:, k, :], start=(k == 0), stop=(k == CH - 1))
                        mm.then_inc(S["xc_done"], 1)
                    for c in range(NC_):
                        need(pe, "xc_in", s0 * (NX + 2) + (s + 1) * (NX + 2)) if c == 0 else None
                        if c >= 2:
                            need(pe, "z_in", g0 + (s * NC_ + c - 1))
                        for k in range(CH):
                            mm = pe.matmul(kp[c % 2][:, :], xnF[:, k, c * P:(c + 1) * P], w_z[:, k, :], start=(k == 0), stop=(k == CH - 1))
                        mm.then_inc(S["z_done"], 1)
                    for c in range(NC_):
                        for k in range(CH):
                            mm = pe.matmul(DTP[:, c * NH:(c + 1) * NH], xnF[:, k, c * P:(c + 1) * P], w_dt[:, k, :], start=(k == 0), stop=(k == CH - 1))
                    mm.then_inc(S["dt_done"], 1)
                    need(pe, "z_in", g0 + (s + 1) * NC_)
                    need(pe, "silu_in", s0 * (NX + 2) + (s + 1) * (NX + 2))
                    need(pe, "dt_in", s1)
                    for c in range(NC_):
                        g, j = s * NC_ + c, c % 2
                        g1 = pe.snap(g0 + (g + 1))
                        cols = slice(c * P, (c + 1) * P)
                        need(pe, "bt_in", g0 + g)
                        pe.matmul(CUM, upper[:, :], dtA[:, c, :], start=True, stop=True)
                        pe.matmul(TOT, ones[:, :], dtA[:, c, :], start=True, stop=True)
                        for h in range(NH):
                            pe.matmul(k_decay[:, h * P:(h + 1) * P], dtA[:, c, h:h + 1].to_broadcast([P, P]), upper[:, :], start=True, stop=True)
                        pe.transpose(BTP, XS[0:DS, NX, cols], ident[0:DS, 0:DS])
                        pe.matmul(MT, XS[0:DS, NX, cols], XS[0:DS, NX + 1, cols], start=True, stop=True).then_inc(S["cum_done"], 1)
                        need(pe, "px_read", g0 + g)
                        for m in range(NX):
                            mm = pe.transpose(k_p0[:, m * P:(m + 1) * P], XS[:, m, cols], ident[:, :])
                        mm.then_inc(S["xs_turned"], 1)
                        need(pe, "h_in", g1)
                        need(pe, "g_in", g0 + g)
                        pe.matmul(k_off[:, :], XS[0:DS, NX + 1, cols], state[:, :], start=True, stop=True).then_inc(S["off_done"], 1)
                        if g < NG - 1:
                            need(pe, "xw_in", g1)
                            need(pe, "bt_in", g1)
                            pe.matmul(k_p1[0:DS, :], BT[j][:, :], xw[j][:, :], start=True, stop=True).then_inc(S["snew_done"], 1)
                        need(pe, "w_in", g1)
                        need(pe, "gf_in", g0 + g)
                        for h in range(NH):
                            mm = pe.matmul(k_y[:, h * HD:(h + 1) * HD], dec[j][:, h, :], xdt[j][:, h * HD:(h + 1) * HD], start=True, stop=True)
                        mm.then_inc(S["y_done"], 1)
                        need(pe, "g_in", g1)
                        for m in range(NX):
                            mm = pe.transpose(k_y[:, m * P:(m + 1) * P], ya[j][:, m * P:(m + 1) * P], ident[:, :])
                        mm.then_inc(S["g_turned"], 1)
                        need(pe, "gf_in", g1)
                        need(pe, "o_in", g0 + g)
                        for m in range(NX):
                            mm = pe.matmul(k_t[:, 0:C], gF[:, m, :], w_out[:, m, :], start=(m == 0), stop=(m == NX - 1))
                        mm.then_inc(S["o_done"], 1)

        @block.scalar
        def _(act):
            act.wait_ge(weights_in, 16 * len(loads))
            act.activation(neg_a[:, :], a_log[:, :], ACT.Exp).then_inc(consts, 1)
            act.wait_ge(consts, 7)
            credit(act, "act")
            with act.Fori(0, B) as i:
                g0, s0 = act.snap(i * NG), act.snap(i * NSUP)
                for s in range(NSUP):
                    s1 = act.snap(s0 + (s + 1))
                    need(act, "sq1_in", s1)
                    act.activation(rstd[:, :], ve[:, :], ACT.Sqrt).then_inc(S["sq1"], 1)
                    need(act, "sq2_in", s1)
                    act.activation(r2[:, :], ve2[:, :], ACT.Sqrt).then_inc(S["sq2"], 1)
                    for q in range(2):
                        need(act, "xn_turned", i * 2 * NSUP + (s * 2 + q + 1))
                        for k in range(CH):
                            ins = act.activation(xnF[:, k, 2 * q * P:2 * (q + 1) * P].rearrange("p (c t) -> p c t", c=2),
                                                 k_turn[q][:, :].rearrange("p (c k t) -> p c k t", c=2, k=CH)[:, :, k, :], ACT.Copy)
                        ins.then_inc(S["xnF_in"], 1)
                    for m in range(NX + 2):
                        rows = P if m < NX else DS
                        need(act, "xc_done", s0 * (NX + 2) + (s * (NX + 2) + m + 1))
                        act.activation(XC[s][0:rows, m, KC - 1:], kp[m % 2][0:rows, :], ACT.Copy).then_inc(S["xc_in"], 1)
                    for c in range(NC_):
                        need(act, "z_done", g0 + (s * NC_ + c + 1))
                        act.activation(zs[:, c, :], kp[c % 2][:, :], ACT.Silu).then_inc(S["z_in"], 1)
                    for m in range(NX + 2):
                        rows = P if m < NX else DS
                        need(act, "cv_in", s0 * (NX + 2) + (s * (NX + 2) + m + 1))
                        act.activation(XS[0:rows, m, :], CV[0:rows, m, :], ACT.Silu, bias=conv_b[0:rows, m:m + 1]).then_inc(S["silu_in"], 1)
                    need(act, "dabs_in", s1)
                    act.activation(de[:, :, :], de[:, :, :], ACT.Exp, scale=-1.0).then_inc(S["dexp_in"], 1)
                    need(act, "du_in", s1)
                    act.activation(dt4[:, :, :], du[:, :, :], ACT.Ln).then_inc(S["dln_in"], 1)
                    for c in range(NC_):
                        g, j = s * NC_ + c, c % 2
                        g1 = act.snap(g0 + (g + 1))
                        need(act, "sm_in", g1)
                        act.activation(se[j][:, :, :], sm[j][:, :, :], ACT.Exp).then_inc(S["se_in"], 1)
                        need(act, "dec_in", g1)
                        act.activation(dec[j][:, :, :], dec[j][:, :, :], ACT.Exp).then_inc(S["exp_in"], 1)
                        need(act, "g_in", g1)
                        act.activation(squares[:, :], ya[j][:, :], ACT.Square, accum_out=ss[:, c:c + 1]).then_inc(S["ss_in"], 1)
                        need(act, "g_turned", g1)
                        act.activation(gF[:, :, :], k_y[:, :].rearrange("p (m t) -> p m t", m=NX), ACT.Copy).then_inc(S["gf_in"], 1)
                        need(act, "o_done", g1)
                        act.activation(oT[:, c, :], k_t[:, 0:C], ACT.Copy).then_inc(S["o_in"], 1)
                    need(act, "rr_in", s1)
                    act.activation(rr[:, :], vr[:, :], ACT.Sqrt).then_inc(S["rrs"], 1)
EDGES = 1048576
COLS = EDGES // P
ROW_BITS, P_BITS = COLS.bit_length() - 1, 7
NODE_BITS = M.bit_length() - 1
KEY_BASE = 0x20000000
KEY_DROPPED = 2.0 ** -31
TB = 4


def phase_sort(nc, D):
    with ExitStack() as ctx:
        s_ = Space(nc, ctx, "sort")
        sb, ps, sem = s_.sb, s_.ps, s_.sem
        keys = [sb("keys0", [P, COLS]), sb("keys1", [P, COLS])]
        signs = sb("signs", [P, P_BITS])
        ident, ones = sb("ident", [P, P]), sb("ones", [P, P])
        count, total, edge_of = sb("count", [P, 1]), sb("total", [P, 1], I32), sb("edge_of", [1, 2])
        banks = [ps(f"bank{k}", 512) for k in range(4)]
        edges_in, consts_in, stored = sem("edges_in"), sem("consts_in"), sem("stored")
        ordered, turned, read, counted, ends_in = sem("ordered"), sem("turned"), sem("read"), sem("counted"), sem("ends_in")
        block = ctx.enter_context(nc.Block())
        NB = COLS // (TB * P)
        turns = 2 * P_BITS

        final = {}

        @block.vector
        def _(v):
            n = 0
            cur = 0

            def did(ins):
                nonlocal n
                ins.then_inc(ordered, 1)
                n += 1

            def exchange(lo_out, hi_out, lo, hi, lo_rev, hi_rev):
                v.wait_ge(ordered, n)
                v.tensor_tensor(lo_out, lo, hi_rev, ALU.min)
                did(v.tensor_tensor(hi_out, hi, lo_rev, ALU.max))

            def in_rows(size, mirrored):
                nonlocal cur
                a = keys[cur][:, :].rearrange("p (n b) -> p n b", b=size)
                o = keys[1 - cur][:, :].rearrange("p (n b) -> p n b", b=size)
                h = size // 2
                lo, hi = a[:, :, 0:h], a[:, :, h:size]
                exchange(o[:, :, 0:h], o[:, :, h:size], lo, hi, lo[:, :, ::-1] if mirrored else lo, hi[:, :, ::-1] if mirrored else hi)
                cur = 1 - cur

            def flip(r):
                v.wait_ge(ordered, n)
                did(v.tensor_scalar(keys[cur][:, :], keys[cur][:, :], signs[:, r:r + 1], None, ALU.mult))

            def take_turned(t, scale):
                nonlocal cur
                for b in range(NB):
                    v.wait_ge(turned, t * NB + b + 1)
                    cols = slice(b * TB * P, (b + 1) * TB * P)
                    if scale is None:
                        ins = v.tensor_copy(keys[1 - cur][:, cols], banks[b % 4][:, :])
                    else:
                        ins = v.tensor_scalar(keys[1 - cur][:, cols], banks[b % 4][:, :], signs[:, scale:scale + 1], None, ALU.mult)
                    ins.then_inc(read, 1)
                v.wait_ge(read, (t + 1) * NB)
                cur = 1 - cur

            ready = []
            v.memset(edge_of[:, :], 1.0).then_inc(ends_in, 1)
            v.memset(ones[:, :], 1.0).then_inc(counted, 1)
            v.wait_ge(edges_in, 32)
            v.wait_ge(consts_in, 32)
            dst, src = keys[0][:, :].bitcast(I32), keys[1][:, :].bitcast(I32)
            v.tensor_scalar(dst, dst, float(M), None, ALU.min)
            did(v.tensor_scalar(src, src, float(M - 1), None, ALU.min))
            v.wait_ge(ordered, n)
            did(v.tensor_scalar(dst, dst, NODE_BITS, KEY_BASE, ALU.logical_shift_left, ALU.bitwise_or))
            v.wait_ge(ordered, n)
            did(v.tensor_tensor(dst, dst, src, ALU.bitwise_or))
            flip(0)
            for k in range(1, ROW_BITS + 1):
                in_rows(1 << k, True)
                for j in range(k - 1, 0, -1):
                    in_rows(1 << j, False)
            flip(0)
            t = 0
            for r in range(P_BITS):
                ready.append((n, cur))
                take_turned(t, None)
                t += 1
                for q in range(r, -1, -1):
                    dirs = 2 if r < P_BITS - 1 else 1
                    w = 1 << q
                    shape = dict(d=dirs, s=1 << (r - q), e=2, w=w)
                    a = keys[cur][:, :].rearrange("p (n d s e w) -> p n d s e w", **shape)
                    o = keys[1 - cur][:, :].rearrange("p (n d s e w) -> p n d s e w", **shape)
                    v.wait_ge(ordered, n)
                    for d in range(dirs):
                        lo, hi = a[:, :, d, :, 0, :], a[:, :, d, :, 1, :]
                        v.tensor_tensor(o[:, :, d, :, 0, :], lo, hi, ALU.max if d else ALU.min)
                        ins = v.tensor_tensor(o[:, :, d, :, 1, :], lo, hi, ALU.min if d else ALU.max)
                    did(ins)
                    cur = 1 - cur
                ready.append((n, cur))
                take_turned(t, r + 1 if r < P_BITS - 1 else None)
                t += 1
                for j in range(ROW_BITS, 0, -1):
                    in_rows(1 << j, False)
                if r < P_BITS - 1:
                    flip(r + 1)
            v.wait_ge(ordered, n)
            v.tensor_scalar(keys[1 - cur][:, :], keys[cur][:, :], KEY_DROPPED, None, ALU.is_lt, ALU.add, accum_out=count[:, :]).then_inc(ends_in, 1)
            v.wait_ge(turned, turns * NB + 1)
            v.tensor_copy(total[:, :], banks[0][:, 0:1]).then_inc(counted, 1)
            final.update(at=cur, ready=ready)

        @block.tensor
        def _(pe):
            pe.wait_ge(consts_in, 32)
            for t, (n, cur) in enumerate(final["ready"]):
                pe.wait_ge(ordered, n)
                for b in range(NB):
                    k = t * NB + b
                    if k >= 4:
                        pe.wait_ge(read, k - 3)
                    for x in range(TB):
                        at = (b * TB + x) * P
                        mm = pe.transpose(banks[b % 4][:, x * P:(x + 1) * P], keys[cur][:, at:at + P], ident[:, :])
                    mm.then_inc(turned, 1)
            pe.wait_ge(counted, 1)
            pe.wait_ge(ends_in, 2)
            pe.matmul(banks[0][:, 0:1], ones[:, :], count[:, :], start=True, stop=True).then_inc(turned, 1)

        @block.sync
        def _(sync):
            sync.dma_start(signs[:, :], D["c_signs"]).then_inc(consts_in, 16)
            sync.dma_start(ident[:, :], D["c_ident"]).then_inc(consts_in, 16)
            sync.dma_start(keys[0][:, :].bitcast(I32), D["edges"][1].rearrange("(p c) -> p c", p=P)).then_inc(edges_in, 16)
            sync.dma_start(keys[1][:, :].bitcast(I32), D["edges"][0].rearrange("(p c) -> p c", p=P)).then_inc(edges_in, 16)
            sync.wait_ge(ends_in, 1)
            sync.dma_start(D["keys"][0:1].rearrange("(a n) -> a n", a=1), edge_of[:, 0:1]).then_inc(stored, 16)
            sync.dma_start(D["keys"][EDGES + 1:EDGES + 2].rearrange("(a n) -> a n", a=1), edge_of[:, 1:2]).then_inc(stored, 16)
            sync.wait_ge(counted, 2)
            sync.dma_start(D["keys"][1:EDGES + 1].rearrange("(p c) -> p c", p=P), keys[final["at"]][:, :]).then_inc(stored, 16)
            sync.dma_start(D["n_edges"], total[0:1, :]).then_inc(stored, 16)
            sync.wait_ge(stored, 64)
NE, GH = 4, 4
GF = GH * NE
NJ = M // ST


def phase_nodes(nc, D):
    with ExitStack() as ctx:
        s_ = Space(nc, ctx, "nodes")
        sb, ps, sem, sems = s_.sb, s_.ps, s_.sem, s_.sems
        ident, w_gat = sb("ident", [P, P]), sb("w_gat", [P, CH, GF])
        att = sb("att", [P, 2, GF])
        T = [sb(f"T{u}", [P, NC_, C]) for u in range(2)]
        N = sb("N", [P, NC_, C])
        stats, mv = sb("stats", [P, NC_, 6]), sb("mv", [P, NC_, 2])
        fence = sb("fence", [P, 1])
        ve, rstd = sb("ve", [P, NC_]), sb("rstd", [P, NC_])
        XF = [sb(f"XF{u}", [P, CH, ST]) for u in range(2)]
        TF = [sb(f"TF{u}", [P, CH, ST]) for u in range(2)]
        TAB = [sb(f"TAB{u}", [P, NC_, GF + GH]) for u in range(2)]
        VT = [sb(f"VT{u}", [P, NC_, GH]) for u in range(2)]
        hs = sb("hs", [P, NC_, GF])
        prod = sb("prod", [P, 2, NC_, GF])
        kx, kt, kh = [ps(f"kx{k}", 512) for k in range(CH)], [ps(f"kt{k}", 512) for k in range(CH)], ps("kh", 512)
        consts_in, own_s = sem("consts_in"), sem("vec")
        t_in, stored = sems("t_in", 2), sems("stored", 2)
        S = {n: sem(n) for n in "ve_in sd_in n_in x_turned t_turned xf_in tf_in h_done v_in".split()}
        STEPS = 5
        block = ctx.enter_context(nc.Block())
        rows = D["t2"].rearrange("b n f -> (b n) f").rearrange("(j c p) f -> j p c f", p=P, c=NC_)

        @block.gpsimd
        def _(pool):
            with pool.Fori(0, NJ // 2) as i:
                for u in range(2):
                    pool.wait_ge(S["n_in"], i * 2 + (u + 1))
                    pool.wait_ge(S["t_turned"], i * 2 + (u + 1))
                    pool.dma_start(T[u][:, :, :], rows[i * 2 + u]).then_inc(t_in[u], 16)

        @block.sync
        def _(sync):
            sync.dma_start(ident[:, :], D["c_ident"]).then_inc(consts_in, 16)
            sync.dma_start(w_gat[:, :, :], D["w_gat"]).then_inc(consts_in, 16)
            sync.dma_start(att[:, :, :], D["att"]).then_inc(consts_in, 16)
            for u in range(2):
                sync.sem_inc(stored[u], 64)
            tabv = D["table"].rearrange("(j c p) f -> j p c f", p=P, c=NC_)
            vv = D["vtable"].rearrange("(j c p) f -> j p c f", p=P, c=NC_)
            with sync.Fori(0, NJ // 2) as i:
                for u in range(2):
                    sync.wait_ge(S["xf_in"], i * 2 + (u + 2))
                    sync.dma_start(D["x3F"][i * 2 + u].rearrange("(k p) n -> p k n", p=P), XF[u][:, :, :]).then_inc(stored[u], 16)
                    sync.wait_ge(S["tf_in"], i * 2 + (u + 2))
                    sync.dma_start(D["t2F"][i * 2 + u].rearrange("(k p) n -> p k n", p=P), TF[u][:, :, :]).then_inc(stored[u], 16)
                    sync.wait_ge(S["v_in"], i * 2 + (u + 2))
                    sync.dma_start(tabv[i * 2 + u], TAB[u][:, :, :]).then_inc(stored[u], 16)
                    sync.dma_start(vv[i * 2 + u], VT[u][:, :, :]).then_inc(stored[u], 16)
            for u in range(2):
                sync.wait_ge(stored[u], 64 * (NJ // 2 + 1))

        @block.vector
        def _(v):
            own = Steps(v, own_s)
            v.wait_ge(consts_in, 48)
            v.sem_inc(S["n_in"], 2)
            with v.Fori(0, NJ // 2) as i:
                for u in range(2):
                    own.turn(i * (2 * STEPS) + u * STEPS)
                    j1 = v.snap(i * 2 + (u + 1))
                    v.wait_ge(t_in[u], i * 16 + 16)
                    for c in range(NC_):
                        ins = v.bn_stats(stats[:, c, :], T[u][:, c, :])
                    own.did(ins)
                    own.wait()
                    v.memset(fence[:, :], 0.0)
                    for c in range(NC_):
                        ins = v.bn_aggr(mv[:, c, :], stats[:, c, :])
                    own.did(ins)
                    own.wait()
                    v.tensor_scalar(ve[:, :], mv[:, :, 1], LN_EPS, None, ALU.add).then_inc(S["ve_in"], 1)
                    v.wait_ge(S["sd_in"], j1)
                    own.did(v.reciprocal(rstd[:, :], rstd[:, :]))
                    own.wait()
                    for c in range(NC_):
                        ins = v.tensor_scalar(N[:, c, :], T[u][:, c, :], mv[:, c, 0:1], rstd[:, c:c + 1], ALU.subtract, ALU.mult)
                    ins.then_inc(S["n_in"], 1)
                    v.wait_ge(S["h_done"], j1)
                    v.wait_ge(stored[u], i * 64 + 64)
                    own.did(v.tensor_copy(hs[:, :, :], kh[:, 0:NC_ * GF].rearrange("p (c f) -> p c f", f=GF)))
                    own.wait()
                    v.tensor_copy(TAB[u][:, :, 0:GF], hs[:, :, :])
                    for a in range(2):
                        ins = v.tensor_tensor(prod[:, a, :, :], hs[:, :, :], att[:, a, :].unsqueeze(1).to_broadcast([P, NC_, GF]), ALU.mult)
                    own.did(ins)
                    own.wait()
                    v.tensor_reduce(TAB[u][:, :, GF:GF + GH], prod[:, 0, :, :].rearrange("p c (h e) -> p c h e", e=NE), AXX, ALU.add)
                    v.tensor_reduce(VT[u][:, :, :], prod[:, 1, :, :].rearrange("p c (h e) -> p c h e", e=NE), AXX, ALU.add).then_inc(S["v_in"], 1)
            assert own.k == STEPS, own.k

        @block.tensor
        def _(pe):
            pe.wait_ge(consts_in, 48)
            pe.sem_inc(S["x_turned"], 1)
            pe.sem_inc(S["t_turned"], 2)
            with pe.Fori(0, NJ // 2) as i:
                for u in range(2):
                    j0 = pe.snap(i * 2 + u + 1)
                    pe.wait_ge(t_in[u], i * 16 + 16)
                    pe.wait_ge(S["tf_in"], j0)
                    for k in range(CH):
                        for c in range(NC_):
                            mm = pe.transpose(kt[k][:, c * P:(c + 1) * P], T[u][:, c, k * P:(k + 1) * P], ident[:, :])
                    mm.then_inc(S["t_turned"], 1)
                    pe.wait_ge(S["n_in"], j0 + 2)
                    pe.wait_ge(S["xf_in"], j0)
                    for k in range(CH):
                        for c in range(NC_):
                            mm = pe.transpose(kx[k][:, c * P:(c + 1) * P], N[:, c, k * P:(k + 1) * P], ident[:, :])
                    mm.then_inc(S["x_turned"], 1)
                    pe.wait_ge(S["xf_in"], j0 + 1)
                    pe.wait_ge(S["v_in"], j0)
                    for c in range(NC_):
                        for k in range(CH):
                            mm = pe.matmul(kh[:, c * GF:(c + 1) * GF], XF[u][:, k, c * P:(c + 1) * P], w_gat[:, k, :], start=(k == 0), stop=(k == CH - 1))
                    mm.then_inc(S["h_done"], 1)

        @block.scalar
        def _(act):
            act.wait_ge(consts_in, 48)
            for n in ("xf_in", "tf_in", "v_in"):
                act.sem_inc(S[n], 1)
            with act.Fori(0, NJ // 2) as i:
                for u in range(2):
                    j1 = act.snap(i * 2 + (u + 1))
                    act.wait_ge(S["ve_in"], j1)
                    act.activation(rstd[:, :], ve[:, :], ACT.Sqrt).then_inc(S["sd_in"], 1)
                    act.wait_ge(stored[u], i * 64 + 64)
                    act.wait_ge(S["t_turned"], j1 + 2)
                    for k in range(CH):
                        ins = act.activation(TF[u][:, k, :], kt[k][:, :], ACT.Copy)
                    ins.then_inc(S["tf_in"], 1)
                    act.wait_ge(S["x_turned"], j1 + 1)
                    for k in range(CH):
                        ins = act.activation(XF[u][:, k, :], kx[k][:, :], ACT.Copy)
                    ins.then_inc(S["xf_in"], 1)
CW = 64
CS = P * CW
NCHUNK = EDGES // CS
HE = NE + 1
SUMS = GH * HE
RES = GH + SUMS
FAR = 1.0e30
EDGE_STEPS = 24


def phase_edges(nc, D):
    with ExitStack() as ctx:
        s_ = Space(nc, ctx, "edges")
        sb, ps, sem, sems = s_.sb, s_.ps, s_.sem, s_.sems
        ident = sb("ident", [P, P])
        n_edges = sb("n_edges", [1, 1], I32)
        K = [[sb(f"K{u}_{w}", [P, CW], U32) for w in range(3)] for u in range(2)]
        dst = [sb(f"dst{w}", [P, CW], U32) for w in range(3)]
        src_i = [sb(f"src_i{u}", [P, CW], U32) for u in range(2)]
        dst_i = [sb(f"dst_i{u}", [P, CW], U32) for u in range(2)]
        end_i = [sb(f"end_i{u}", [P, CW], U32) for u in range(2)]
        cont, pen, whole, more = sb("cont", [P, CW]), sb("pen", [P, CW]), sb("whole", [P, 1]), sb("more", [P, CW])
        G = [sb(f"G{u}", [P, CW, GF + GH]) for u in range(2)]
        V = [sb(f"V{u}", [P, CW, GH]) for u in range(2)]
        R = [sb(f"R{u}", [P, CW + 1, RES]) for u in range(2)]
        z, e = sb("z", [P, GH, CW]), sb("e", [P, GH, CW])
        ab = sb("ab", [P, 2, GH, CW])
        W = sb("W", [P, GH, HE, CW])
        rows = sb("rows", [P, 4, SUMS])
        RT = sb("RT", [SUMS, 4, P])
        cpen = sb("cpen", [SUMS, 2, P])
        EM, ES = sb("EM", [SUMS, P + 1]), sb("ES", [SUMS, P + 1])
        cab, cW = sb("cab", [SUMS, 2, P]), sb("cW", [SUMS, P])
        start = sb("start", [SUMS, 2, P])
        empty = sb("empty", [P, P, RES])
        k_rows, k_start = ps("k_rows", 512), ps("k_start", 512)
        consts, own_s = sem("consts"), sem("vec")
        k_in, gathered, scattered = sems("k_in", 2), sems("gathered", 2), sems("scattered", 2)
        S = {n: sem(n) for n in "idx_in g_read ab1 ab1e rows_in rows_turned cab_in cabe start_in start_turned ab2 ab2e r_in landed went".split()}
        block = ctx.enter_context(nc.Block())
        keys = D["keys"].bitcast(U32)

        def chunks(eng, body):
            eng.wait_ge(consts, 32)
            n = eng.value_load(n_edges[0:1, 0:1], min_val=0, max_val=EDGES)
            with eng.Fori(0, NCHUNK // 2) as i:
                for u in range(2):
                    with eng.If(i * (2 * CS) + u * CS < n):
                        body(i, u)

        @block.sync
        def _(sync):
            sync.dma_start(ident[:, :], D["c_ident"]).then_inc(consts, 16)
            sync.dma_start(n_edges[:, :], D["n_edges"]).then_inc(consts, 16)

            def body(i, u):
                at = [sync.snap(i * (2 * CS) + (u * CS + w)) for w in range(3)]
                sync.wait_ge(S["idx_in"], i * 2 + (u + 1))
                sync.sem_inc(S["went"], 1)
                for w in range(3):
                    sync.dma_start(K[u][w][:, :], keys[bass.ds(at[w], CS)].rearrange("(p c) -> p c", p=P)).then_inc(k_in[u], 16)
            chunks(sync, body)

        @block.gpsimd
        def _(pool):
            pool.memset(empty[:, :, :], 0.0).then_inc(S["r_in"], 1)
            pool.wait_ge(S["r_in"], 1)
            pool.memset(empty[:, :, 0:GH], -FAR).then_inc(S["r_in"], 1)
            pool.wait_ge(S["r_in"], 2)
            pool.dma_start(D["result"].rearrange("(p q) f -> p q f", p=P), empty[:, :, :]).then_inc(scattered[0], 16)
            pool.wait_ge(scattered[0], 16)
            pool.sem_inc(S["landed"], 2)

            def body(i, u):
                pool.wait_ge(S["idx_in"], i * 2 + (u + 3))
                pool.wait_ge(S["g_read"], i * 2 + (u + 1))
                pool.sem_inc(S["went"], 1)
                for c in range(CW):
                    pool.indirect_dma_start(G[u][:, c, :], None, D["table"], bass.IndirectOffsetOnAxis(ap=src_i[u][:, c:c + 1], axis=0),
                                            bounds_check=M - 1, oob_is_err=False).then_inc(gathered[u], 16)
                    pool.indirect_dma_start(V[u][:, c, :], None, D["vtable"], bass.IndirectOffsetOnAxis(ap=dst_i[u][:, c:c + 1], axis=0),
                                            bounds_check=M - 1, oob_is_err=False).then_inc(gathered[u], 16)
                pool.wait_ge(S["r_in"], i * 2 + (u + 3))
                pool.sem_inc(S["went"], 1)
                for c in range(CW):
                    pool.indirect_dma_start(D["result"], bass.IndirectOffsetOnAxis(ap=end_i[u][:, c:c + 1], axis=0), R[u][:, c + 1, :], None,
                                            bounds_check=M - 1, oob_is_err=False).then_inc(scattered[u], 16)
                pool.wait_ge(scattered[u], i * (16 * CW) + (16 * CW + (16 if u == 0 else 0)))
                pool.sem_inc(S["landed"], 1)
            chunks(pool, body)

        @block.vector
        def _(v):
            own = Steps(v, own_s)
            v.sem_inc(S["idx_in"], 2)
            v.sem_inc(S["g_read"], 2)
            v.memset(EM[:, P:P + 1], -FAR)
            own.did(v.memset(ES[:, P:P + 1], 0.0))

            def body(i, u):
                own.turn(i * (2 * EDGE_STEPS) + (u * EDGE_STEPS + 1))
                n1 = v.snap(i * 2 + (u + 1))
                v.wait_ge(k_in[u], i * 48 + 48)
                v.wait_ge(S["landed"], n1)
                for w in range(3):
                    v.tensor_scalar(dst[w][:, :], K[u][w][:, :], NODE_BITS, 2 * M - 1, ALU.logical_shift_right, ALU.bitwise_and)
                own.did(v.tensor_scalar(src_i[u][:, :], K[u][1][:, :], M - 1, None, ALU.bitwise_and))
                own.wait()
                v.tensor_scalar(dst_i[u][:, :], dst[1][:, :], float(M - 1), None, ALU.min)
                v.tensor_tensor(cont[:, :], dst[0][:, :], dst[1][:, :], ALU.is_equal)
                own.did(v.tensor_tensor(more[:, :], dst[2][:, :], dst[1][:, :], ALU.is_equal))
                own.wait()
                own.did(v.tensor_scalar(pen[:, :], cont[:, :], 1.0, FAR, ALU.subtract, ALU.mult))
                v.scalar_tensor_tensor(end_i[u][:, :], more[:, :], float(2 * M), dst[1][:, :], ALU.mult, ALU.add).then_inc(S["idx_in"], 1)
                v.wait_ge(gathered[u], i * (32 * CW) + 32 * CW)
                own.did(v.tensor_tensor(z[:, :, :], G[u][:, :, GF:GF + GH].rearrange("p c h -> p h c"), V[u][:, :, :].rearrange("p c h -> p h c"), ALU.add))
                own.wait()
                own.did(v.scalar_tensor_tensor(e[:, :, :], z[:, :, :], 0.2, z[:, :, :], ALU.mult, ALU.max))
                r = R[u]
                maxima = r[:, :, 0:GH].rearrange("p c h -> p h c")

                def scans(first, name):
                    own.wait()
                    for h in range(GH):
                        ins = v.tensor_tensor_scan(r[:, 1:, h], pen[:, :], e[:, h, :], r[:, 0, h:h + 1], ALU.add, ALU.max)
                    own.did(ins)
                    own.wait()
                    own.did(v.tensor_tensor(z[:, :, :], maxima[:, :, 0:CW], pen[:, :].unsqueeze(1).to_broadcast([P, GH, CW]), ALU.add))
                    own.wait()
                    v.tensor_tensor(ab[:, 0, :, :], z[:, :, :], maxima[:, :, 1:], ALU.subtract)
                    v.tensor_tensor(ab[:, 1, :, :], e[:, :, :], maxima[:, :, 1:], ALU.subtract).then_inc(S[name], 1)
                    v.wait_ge(S[name + "e"], n1)
                    for h in range(GH):
                        v.tensor_copy(W[:, h, 0, :], ab[:, 1, h, :])
                        ins = v.tensor_tensor(W[:, h, 1:, :], G[u][:, :, h * NE:(h + 1) * NE].rearrange("p c k -> p k c"),
                                              ab[:, 1, h, :].unsqueeze(1).to_broadcast([P, NE, CW]), ALU.mult)
                    own.did(ins)
                    own.wait()
                    for h in range(GH):
                        for k in range(HE):
                            f = GH + h * HE + k
                            ins = v.tensor_tensor_scan(r[:, 1:, f], ab[:, 0, h, :], W[:, h, k, :], r[:, 0, f:f + 1], ALU.mult, ALU.add)
                    return ins

                v.memset(r[:, 0, 0:GH], -FAR)
                own.did(v.memset(r[:, 0, GH:], 0.0))
                own.did(scans(True, "ab1"))
                own.wait()
                v.tensor_copy(rows[:, 0, :].rearrange("p (h k) -> p h k", k=HE), r[:, CW, 0:GH].unsqueeze(2).to_broadcast([P, GH, HE]))
                v.tensor_copy(rows[:, 1, :], r[:, CW, GH:])
                v.tensor_copy(rows[:, 3, :], cont[:, 0:1].to_broadcast([P, SUMS]))
                own.did(v.tensor_tensor(whole[:, :], dst[1][:, 0:1], dst[1][:, CW - 1:CW], ALU.is_equal))
                own.wait()
                v.tensor_tensor(rows[:, 2, :], rows[:, 3, :], whole[:, :].to_broadcast([P, SUMS]), ALU.mult).then_inc(S["rows_in"], 1)
                v.tensor_copy(EM[:, 0:1], EM[:, P:P + 1])
                own.did(v.tensor_copy(ES[:, 0:1], ES[:, P:P + 1]))
                v.wait_ge(S["rows_turned"], n1)
                own.did(v.tensor_copy(RT[:, :, :], k_rows[0:SUMS, :].rearrange("p (a b) -> p a b", a=4)))
                own.wait()
                own.did(v.tensor_scalar(cpen[:, :, :], RT[:, 2:4, :], 1.0, FAR, ALU.subtract, ALU.mult))
                own.wait()
                own.did(v.tensor_tensor_scan(EM[:, 1:], cpen[:, 0, :], RT[:, 0, :], EM[:, 0:1], ALU.add, ALU.max))
                own.wait()
                own.did(v.tensor_tensor(cab[:, 0, :], EM[:, 0:P], cpen[:, 0, :], ALU.add))
                own.wait()
                own.did(v.tensor_tensor(cab[:, 0, :], cab[:, 0, :], EM[:, 1:], ALU.subtract))
                v.tensor_tensor(cab[:, 1, :], RT[:, 0, :], EM[:, 1:], ALU.subtract).then_inc(S["cab_in"], 1)
                own.did(v.tensor_tensor(start[:, 0, :], EM[:, 0:P], cpen[:, 1, :], ALU.add))
                v.wait_ge(S["cabe"], n1)
                own.did(v.tensor_tensor(cW[:, :], RT[:, 1, :], cab[:, 1, :], ALU.mult))
                own.wait()
                own.did(v.tensor_tensor_scan(ES[:, 1:], cab[:, 0, :], cW[:, :], ES[:, 0:1], ALU.mult, ALU.add))
                own.wait()
                v.tensor_tensor(start[:, 1, :], ES[:, 0:P], RT[:, 3, :], ALU.mult).then_inc(S["start_in"], 1)
                v.wait_ge(S["start_turned"], n1)
                v.tensor_copy(r[:, 0, 0:GH], k_start[:, 0:SUMS].rearrange("p (h k) -> p h k", k=HE)[:, :, 0])
                own.did(v.tensor_copy(r[:, 0, GH:], k_start[:, 32:32 + SUMS]))
                scans(False, "ab2").then_inc(S["r_in"], 1)
                v.wait_ge(S["r_in"], n1 + 2)
                v.memset(z[:, 0, 0:1], 0.0).then_inc(S["g_read"], 1)
            v.wait_ge(own_s, 1)
            chunks(v, body)
            assert own.k == EDGE_STEPS

        @block.tensor
        def _(pe):
            def body(i, u):
                n1 = pe.snap(i * 2 + (u + 1))
                pe.wait_ge(S["rows_in"], n1)
                for a in range(4):
                    mm = pe.transpose(k_rows[0:SUMS, a * P:(a + 1) * P], rows[:, a, :], ident[:, :])
                mm.then_inc(S["rows_turned"], 1)
                pe.wait_ge(S["start_in"], n1)
                pe.matmul(k_start[:, 511:512], ident[:, :], ident[:, 0:1], start=True, stop=True)
                for a in range(2):
                    mm = pe.transpose(k_start[:, a * 32:a * 32 + SUMS], start[:, a, :], ident[0:SUMS, 0:SUMS])
                mm.then_inc(S["start_turned"], 1)
            chunks(pe, body)

        @block.scalar
        def _(act):
            def body(i, u):
                n1 = act.snap(i * 2 + (u + 1))
                act.wait_ge(S["ab1"], n1)
                act.activation(ab[:, :, :, :], ab[:, :, :, :], ACT.Exp).then_inc(S["ab1e"], 1)
                act.wait_ge(S["cab_in"], n1)
                act.activation(cab[:, :, :], cab[:, :, :], ACT.Exp).then_inc(S["cabe"], 1)
                act.wait_ge(S["ab2"], n1)
                act.activation(ab[:, :, :, :], ab[:, :, :, :], ACT.Exp).then_inc(S["ab2e"], 1)
            chunks(act, body)
NQ = M // P


def phase_gates(nc, D):
    with ExitStack() as ctx:
        s_ = Space(nc, ctx, "gates")
        sb, sem = s_.sb, s_.sem
        R, T, V = sb("R", [P, NQ, RES]), sb("T", [P, NQ, GF + GH]), sb("V", [P, NQ, GH])
        b_gat, ln_g, ln_b = sb("b_gat", [P, GF]), sb("ln_g", [P, GF]), sb("ln_b", [P, GF])
        z, es = sb("z", [P, NQ, GH]), sb("es", [P, NQ, GH])
        w2 = sb("w2", [P, 2, NQ, GH])
        den, num, tmp = sb("den", [P, NQ, GH]), sb("num", [P, NQ, GF]), sb("tmp", [P, NQ, GF])
        mean, var = sb("mean", [P, NQ]), sb("var", [P, NQ])
        score, rank, cmp = sb("score", [P, NE, NQ]), sb("rank", [P, NE, NQ]), sb("cmp", [P, NQ])
        top, gate, total = sb("top", [P, NQ]), sb("gate", [P, NE, NQ]), sb("total", [P, NQ])
        ins_in, out_in = sem("ins_in"), sem("out_in")
        step, exp1_in, exp1, var_in, sd_in, exp2_in, exp2, gates_in = (sem(n) for n in "step exp1_in exp1 var_in sd_in exp2_in exp2 gates_in".split())
        block = ctx.enter_context(nc.Block())

        @block.sync
        def _(sync):
            sync.dma_start(R[:, :, :], D["result"].rearrange("(p q) f -> p q f", p=P)).then_inc(ins_in, 16)
            sync.dma_start(T[:, :, :], D["table"].rearrange("(p q) f -> p q f", p=P)).then_inc(ins_in, 16)
            sync.dma_start(V[:, :, :], D["vtable"].rearrange("(p q) f -> p q f", p=P)).then_inc(ins_in, 16)
            for dst, name in ((b_gat, "b_gat"), (ln_g, "ln_g"), (ln_b, "ln_b")):
                sync.dma_start(dst[:, :], D[name]).then_inc(ins_in, 16)
            sync.wait_ge(gates_in, 1)
            sync.dma_start(D["gates"].rearrange("e (p q) -> p e q", p=P), gate[:, :, :]).then_inc(out_in, 16)
            sync.wait_ge(out_in, 16)

        @block.vector
        def _(v):
            own = Steps(v, step)

            def do(ins):
                own.did(ins)
                own.wait()

            def wide(x, k=GF):
                return x.unsqueeze(2).to_broadcast([P, NQ, k])

            def per_feature(x):
                return x.unsqueeze(1).to_broadcast([P, NQ, GF])

            v.wait_ge(ins_in, 96)
            do(v.tensor_tensor(z[:, :, :], T[:, :, GF:], V[:, :, :], ALU.add))
            do(v.scalar_tensor_tensor(es[:, :, :], z[:, :, :], 0.2, z[:, :, :], ALU.mult, ALU.max))
            do(v.tensor_tensor(z[:, :, :], es[:, :, :], R[:, :, 0:GH], ALU.max))
            do(v.tensor_tensor(w2[:, 0, :, :], R[:, :, 0:GH], z[:, :, :], ALU.subtract))
            v.tensor_tensor(w2[:, 1, :, :], es[:, :, :], z[:, :, :], ALU.subtract).then_inc(exp1_in, 1)
            v.wait_ge(exp1, 1)
            sums = R[:, :, GH:].rearrange("p q (h k) -> p q h k", k=HE)
            do(v.tensor_tensor(den[:, :, :], sums[:, :, :, 0], w2[:, 0, :, :], ALU.mult))
            do(v.tensor_tensor(den[:, :, :], den[:, :, :], w2[:, 1, :, :], ALU.add))
            do(v.tensor_scalar(den[:, :, :], den[:, :, :], 1e-16, None, ALU.add))
            do(v.reciprocal(den[:, :, :], den[:, :, :]))
            for h in range(GH):
                f = slice(h * NE, (h + 1) * NE)
                v.tensor_tensor(num[:, :, f], sums[:, :, h, 1:], wide(w2[:, 0, :, h], NE), ALU.mult)
                ins = v.tensor_tensor(tmp[:, :, f], T[:, :, f], wide(w2[:, 1, :, h], NE), ALU.mult)
            do(ins)
            do(v.tensor_tensor(num[:, :, :], num[:, :, :], tmp[:, :, :], ALU.add))
            for h in range(GH):
                f = slice(h * NE, (h + 1) * NE)
                ins = v.tensor_tensor(num[:, :, f], num[:, :, f], wide(den[:, :, h], NE), ALU.mult)
            do(ins)
            do(v.tensor_tensor(num[:, :, :], num[:, :, :], per_feature(b_gat[:, :]), ALU.add))
            do(v.tensor_reduce(mean[:, :], num[:, :, :], AXX, ALU.add))
            do(v.tensor_scalar(mean[:, :], mean[:, :], 1.0 / GF, None, ALU.mult))
            do(v.tensor_tensor(num[:, :, :], num[:, :, :], wide(mean[:, :]), ALU.subtract))
            do(v.tensor_tensor(tmp[:, :, :], num[:, :, :], num[:, :, :], ALU.mult))
            do(v.tensor_reduce(var[:, :], tmp[:, :, :], AXX, ALU.add))
            v.tensor_scalar(var[:, :], var[:, :], 1.0 / GF, LN_EPS, ALU.mult, ALU.add).then_inc(var_in, 1)
            v.wait_ge(sd_in, 1)
            do(v.reciprocal(var[:, :], var[:, :]))
            do(v.tensor_tensor(num[:, :, :], num[:, :, :], wide(var[:, :]), ALU.mult))
            do(v.tensor_tensor(num[:, :, :], num[:, :, :], per_feature(ln_g[:, :]), ALU.mult))
            do(v.tensor_tensor(num[:, :, :], num[:, :, :], per_feature(ln_b[:, :]), ALU.add))
            for k in range(NE):
                ins = v.tensor_reduce(score[:, k, :], num[:, :, k::NE], AXX, ALU.add)
            do(ins)
            do(v.tensor_scalar(score[:, :, :], score[:, :, :], 1.0 / GH, None, ALU.mult))
            v.memset(rank[:, :, :], 0.0)
            do(v.tensor_tensor(top[:, :], score[:, 0, :], score[:, 1, :], ALU.max))
            for k in range(2, NE):
                do(v.tensor_tensor(top[:, :], top[:, :], score[:, k, :], ALU.max))
            for k in range(NE):
                for j in range(NE):
                    if j != k:
                        do(v.tensor_tensor(cmp[:, :], score[:, j, :], score[:, k, :], ALU.is_ge if j < k else ALU.is_gt))
                        do(v.tensor_tensor(rank[:, k, :], rank[:, k, :], cmp[:, :], ALU.add))
            do(v.tensor_scalar(rank[:, :, :], rank[:, :, :], 2.0, None, ALU.is_lt))
            v.tensor_tensor(gate[:, :, :], score[:, :, :], top[:, :].unsqueeze(1).to_broadcast([P, NE, NQ]), ALU.subtract).then_inc(exp2_in, 1)
            v.wait_ge(exp2, 1)
            do(v.tensor_tensor(gate[:, :, :], gate[:, :, :], rank[:, :, :], ALU.mult))
            do(v.tensor_reduce(total[:, :], gate[:, :, :].rearrange("p e q -> p q e"), AXX, ALU.add))
            do(v.reciprocal(total[:, :], total[:, :]))
            v.tensor_tensor(gate[:, :, :], gate[:, :, :], total[:, :].unsqueeze(1).to_broadcast([P, NE, NQ]), ALU.mult).then_inc(gates_in, 1)

        @block.scalar
        def _(act):
            act.wait_ge(exp1_in, 1)
            act.activation(w2[:, :, :, :], w2[:, :, :, :], ACT.Exp).then_inc(exp1, 1)
            act.wait_ge(var_in, 1)
            act.activation(var[:, :], var[:, :], ACT.Sqrt).then_inc(sd_in, 1)
            act.wait_ge(exp2_in, 1)
            act.activation(gate[:, :, :], gate[:, :, :], ACT.Exp).then_inc(exp2, 1)


HF = 2 * C
FT = HF // P


def phase_experts(nc, D):
    with ExitStack() as ctx:
        s_ = Space(nc, ctx, "moe")
        sb, ps, sem, sems = s_.sb, s_.ps, s_.sem, s_.sems
        w1, b1 = sb("w1", [P, NE, CH, HF]), sb("b1", [P, NE, FT])
        w2, b2 = sb("w2", [P, NE, FT, C]), sb("b2", [NE, C])
        pick = sb("pick", [NE, NE, P])
        loads = [(w1, "moe1"), (b1, "moe1_b"), (w2, "moe2"), (b2, "moe2_b"), (pick, "c_pick")]
        X = [sb(f"X{u}", [P, CH, ST]) for u in range(2)]
        T = [sb(f"T{u}", [P, CH, ST]) for u in range(2)]
        g = [sb(f"g{u}", [NE, ST]) for u in range(2)]
        gb = [sb(f"gb{u}", [P, ST]) for u in range(2)]
        H = [sb(f"H{u}", [P, FT, ST]) for u in range(2)]
        O = [sb(f"O{u}", [P, CH, ST]) for u in range(2)]
        k_h = [ps(f"k_h{k}", 512) for k in range(4)]
        k_g = [ps(f"k_g{k}", 512) for k in range(2)]
        k_o = [ps(f"k_o{k}", 512) for k in range(CH)]
        weights_in = sem("weights_in")
        x_in, stored = sems("x_in", 2), sems("stored", 2)
        S = {n: sem(n) for n in "gb_done gb_in h_done gelu_in hg_in o_done o_in".split()}
        per = dict(gb_done=NE, gb_in=NE, h_done=NE * FT, gelu_in=NE * FT, hg_in=NE * FT, o_done=CH, o_in=CH)
        block = ctx.enter_context(nc.Block())

        def start(eng, names):
            for n in names.split():
                eng.sem_inc(S[n], 2 * per[n])

        @block.gpsimd
        def _(pool):
            with pool.Fori(0, NJ // 2) as i:
                for u in range(2):
                    pool.wait_ge(S["o_in"], (i * 2 + (u + 1)) * CH)
                    pool.dma_start(X[u][:, :, :], D["x3F"][i * 2 + u].rearrange("(k p) n -> p k n", p=P)).then_inc(x_in[u], 16)
                    pool.dma_start(T[u][:, :, :], D["t2F"][i * 2 + u].rearrange("(k p) n -> p k n", p=P)).then_inc(x_in[u], 16)
                    pool.dma_start(g[u][:, :], D["gates"].rearrange("e (j n) -> j e n", n=ST)[i * 2 + u]).then_inc(x_in[u], 16)

        @block.sync
        def _(sync):
            for dst, name in loads:
                sync.dma_start(dst[tuple(slice(None) for _ in dst.shape)], D[name]).then_inc(weights_in, 16)
            for u in range(2):
                sync.sem_inc(stored[u], 16)
            with sync.Fori(0, NJ // 2) as i:
                for u in range(2):
                    sync.wait_ge(S["o_in"], (i * 2 + (u + 3)) * CH)
                    sync.dma_start(D["out"][i].rearrange("(k p) n -> p k n", p=P)[:, :, u * ST:(u + 1) * ST], O[u][:, :, :]).then_inc(stored[u], 16)
            for u in range(2):
                sync.wait_ge(stored[u], 16 * (NJ // 2 + 1))

        @block.tensor
        def _(pe):
            pe.wait_ge(weights_in, 16 * len(loads))
            start(pe, "gb_done h_done o_done")
            with pe.Fori(0, NJ // 2) as i:
                for u in range(2):
                    j = pe.snap(i * 2 + (u + 2))
                    jg, jh, jo = pe.snap(j * NE), pe.snap(j * NE * FT), pe.snap(j * CH)
                    pe.wait_ge(x_in[u], i * 48 + 48)

                    def second(e):
                        for f in range(FT):
                            pe.wait_ge(S["hg_in"], jh + (e * FT + f + 1))
                            if e == 0 and f == 0:
                                pe.wait_ge(S["o_in"], jo)
                            for o in range(CH):
                                mm = pe.matmul(k_o[o][:, :], w2[:, e, f, o * P:(o + 1) * P], H[e % 2][:, f, :], start=(e == 0 and f == 0), stop=False)
                        return mm

                    for e in range(NE):
                        pe.wait_ge(S["gb_in"], jg + (e - 1))
                        pe.matmul(k_g[e % 2][:, :], pick[:, e, :], g[u][:, :], start=True, stop=True).then_inc(S["gb_done"], 1)
                        for f in range(FT):
                            n = e * FT + f
                            pe.wait_ge(S["gelu_in"], jh + (n - 3))
                            for k in range(CH):
                                mm = pe.matmul(k_h[n % 4][:, :], w1[:, e, k, f * P:(f + 1) * P], X[u][:, k, :], start=(k == 0), stop=(k == CH - 1))
                            mm.then_inc(S["h_done"], 1)
                        if e:
                            second(e - 1)
                    second(NE - 1)
                    for o in range(CH):
                        pe.matmul(k_o[o][:, :], b2[:, o * P:(o + 1) * P], g[u][:, :], start=False, stop=True).then_inc(S["o_done"], 1)

        @block.scalar
        def _(act):
            act.wait_ge(weights_in, 16 * len(loads))
            start(act, "gelu_in")
            with act.Fori(0, NJ // 2) as i:
                for u in range(2):
                    j = act.snap(i * 2 + (u + 2))
                    jh, jo = act.snap(j * NE * FT), act.snap(j * CH)
                    for e in range(NE):
                        for f in range(FT):
                            n = e * FT + f
                            act.wait_ge(S["h_done"], jh + (n + 1))
                            act.activation(H[e % 2][:, f, :], k_h[n % 4][:, :], ACT.Gelu, bias=b1[:, e, f:f + 1]).then_inc(S["gelu_in"], 1)

        @block.vector
        def _(v):
            v.wait_ge(weights_in, 16 * len(loads))
            start(v, "gb_in hg_in o_in")
            with v.Fori(0, NJ // 2) as i:
                for u in range(2):
                    j = v.snap(i * 2 + (u + 2))
                    jg, jh, jo = v.snap(j * NE), v.snap(j * NE * FT), v.snap(j * CH)
                    for e in range(NE):
                        v.wait_ge(S["gb_done"], jg + (e + 1))
                        v.tensor_copy(gb[e % 2][:, :], k_g[e % 2][:, :]).then_inc(S["gb_in"], 1)
                        for f in range(FT):
                            n = e * FT + f
                            v.wait_ge(S["gelu_in"], jh + (n + 1))
                            if f == 0:
                                v.wait_ge(S["gb_in"], jg + (e + 1))
                            v.tensor_tensor(H[e % 2][:, f, :], H[e % 2][:, f, :], gb[e % 2][:, :], ALU.mult).then_inc(S["hg_in"], 1)
                    v.wait_ge(stored[u], i * 16 + 16)
                    for o in range(CH):
                        v.wait_ge(S["o_done"], jo + (o + 1))
                        v.tensor_tensor(O[u][:, o, :], k_o[o][:, :], T[u][:, o, :], ALU.add).then_inc(S["o_in"], 1)


def build_program(nc, D):
    for name, shape, dt in (("t1", (B, C, HW), F32), ("t2", (B, HW, C), F32),
                            ("keys", (EDGES + 2,), F32), ("n_edges", (1, 1), I32),
                            ("x3F", (NJ, C, ST), F32), ("t2F", (NJ, C, ST), F32),
                            ("table", (M, GF + GH), F32), ("vtable", (M, GH), F32),
                            ("result", (M, RES), F32), ("gates", (NE, M), F32)):
        D[name] = nc.dram_tensor(name, shape, dt, kind="Internal").ap()
    phase_conv(nc, D)
    phase_ssm(nc, D)
    phase_sort(nc, D)
    phase_nodes(nc, D)
    phase_edges(nc, D)
    phase_gates(nc, D)
    phase_experts(nc, D)


def kernel(x, L0_conv_fc1_w, L0_conv_fc1_b, L0_conv_fc2_w, L0_conv_fc2_b, L0_conv_qkv_w, L0_conv_qkv_b,
           L0_conv_proj_w, L0_conv_proj_b, L0_conv_ffn1_w, L0_conv_ffn1_b, L0_conv_ffn2_w, L0_conv_ffn2_b,
           L1_attn_W_in, L1_attn_conv_w, L1_attn_conv_b, L1_attn_dt_bias, L1_attn_A_log, L1_attn_Dp,
           L1_attn_gnorm_w, L1_attn_norm_w, L1_attn_W_out,
           L1_ffn_W_gat, L1_ffn_att_src, L1_ffn_att_dst, L1_ffn_b_gat, L1_ffn_ln_gamma, L1_ffn_ln_beta,
           L1_ffn_W1, L1_ffn_b1, L1_ffn_W2, L1_ffn_b2, L1_ffn_edge_index):
    import concourse.bacc as _bacc
    from concourse import mybir as _mybir
    from concourse.bass_utils import run_bass_kernel_spmd as _run

    def rows_in_tiles(w):
        w = np.asarray(w)
        return w.reshape(-1, P, w.shape[1]).transpose(1, 0, 2)

    def vector_tiles(v):
        return np.asarray(v).reshape(-1, P).T

    def column(v):
        return np.asarray(v)[:, None]

    def on_all(v):
        v = np.asarray(v)
        return np.broadcast_to(v.reshape(1, -1), (P, v.size))

    def xbc_tiles(w):
        w = np.asarray(w)
        t = np.zeros((NX + 2, P, w.shape[1]), w.dtype)
        t[:NX] = w[:DI].reshape(NX, P, -1)
        t[NX, :DS], t[NX + 1, :DS] = w[DI:DI + DS], w[DI + DS:]
        return t.transpose(1, 0, 2)

    qkv, qkv_b = np.asarray(L0_conv_qkv_w), np.asarray(L0_conv_qkv_b)
    w_in = np.asarray(L1_attn_W_in).T
    att = np.stack([np.asarray(L1_ffn_att_src).reshape(-1), np.asarray(L1_ffn_att_dst).reshape(-1)])
    w1, w2 = np.asarray(L1_ffn_W1), np.asarray(L1_ffn_W2)
    lanes = np.arange(P)
    arrays = dict(
        x=np.asarray(x).reshape(B, C, HW),
        fc1=rows_in_tiles(np.asarray(L0_conv_fc1_w).T), fc1_b=column(L0_conv_fc1_b),
        fc2=np.asarray(L0_conv_fc2_w).T, fc2_b=vector_tiles(L0_conv_fc2_b),
        wq=np.tile(qkv[:AD].T, (1, 4)), wk=np.tile(qkv[AD:2 * AD].T, (1, 4)), wv=qkv[2 * AD:].T,
        bq=column(qkv_b[:AD]), bk=column(qkv_b[AD:2 * AD]), bv=column(qkv_b[2 * AD:]),
        proj=np.tile(np.asarray(L0_conv_proj_w).T, (1, 2)), proj_b=column(L0_conv_proj_b),
        ffn1=rows_in_tiles(np.asarray(L0_conv_ffn1_w).T), ffn1_b=vector_tiles(L0_conv_ffn1_b),
        ffn2=rows_in_tiles(np.asarray(L0_conv_ffn2_w).T), ffn2_b=vector_tiles(L0_conv_ffn2_b),
        w_z=rows_in_tiles(w_in[:, :DI]), w_x=rows_in_tiles(w_in[:, DI:2 * DI + 2 * DS]),
        w_dt=rows_in_tiles(w_in[:, 2 * DI + 2 * DS:]), w_out=rows_in_tiles(np.asarray(L1_attn_W_out).T),
        norm_w=vector_tiles(L1_attn_norm_w), gnorm_w=vector_tiles(L1_attn_gnorm_w),
        conv_w=xbc_tiles(L1_attn_conv_w), conv_b=xbc_tiles(column(L1_attn_conv_b))[:, :, 0],
        dt_b=on_all(L1_attn_dt_bias), a_log=on_all(L1_attn_A_log), dp=on_all(L1_attn_Dp),
        w_gat=rows_in_tiles(L1_ffn_W_gat), att=np.broadcast_to(att, (P, 2, GF)),
        edges=np.asarray(L1_ffn_edge_index),
        b_gat=on_all(L1_ffn_b_gat), ln_g=on_all(L1_ffn_ln_gamma), ln_b=on_all(L1_ffn_ln_beta),
        moe1=w1.reshape(NE, CH, P, HF).transpose(2, 0, 1, 3),
        moe1_b=np.asarray(L1_ffn_b1).reshape(NE, FT, P).transpose(2, 0, 1),
        moe2=w2.reshape(NE, FT, P, C).transpose(2, 0, 1, 3), moe2_b=np.asarray(L1_ffn_b2),
        c_ident=np.eye(P, dtype=np.float32),
        c_group=np.kron(np.eye(16, dtype=np.float32), np.full((8, 8), 1 / 8, np.float32)),
        c_upper=np.triu(np.ones((P, P), np.float32)),
        c_signs=np.stack([1.0 - 2.0 * ((lanes >> k) & 1) for k in range(P_BITS)], 1).astype(np.float32),
        c_pick=np.repeat(np.eye(NE, dtype=np.float32)[:, :, None], P, 2))
    arrays = {name: np.ascontiguousarray(a) for name, a in arrays.items()}

    nc = _bacc.Bacc("TRN2", target_bir_lowering=False, num_devices=1)
    D = {name: nc.dram_tensor(name, a.shape, _mybir.dt.from_np(a.dtype), kind="ExternalInput").ap()
         for name, a in arrays.items()}
    D["out"] = nc.dram_tensor("out", (B, C, HW), _mybir.dt.float32, kind="ExternalOutput").ap()
    build_program(nc, D)
    r = _run(nc, [arrays], core_ids=[0])
    return r.results[0]["out"].reshape(B, C, 32, 32)
```

```python
from contextlib import ExitStack

import numpy as np
import concourse.bass as bass
from concourse import mybir

ALU = mybir.AluOpType
ACT = mybir.ActivationFunctionType
AXX = mybir.AxisListType.X
F32 = mybir.dt.float32
I32 = mybir.dt.int32
U32 = mybir.dt.uint32
BF16 = mybir.dt.bfloat16

P = 128
B, C, HW = 16, 256, 1024
M = B * HW
CH = C // P
HALF = 512


class Steps:

    def __init__(self, eng, sem):
        self.eng, self.sem, self.base, self.k = eng, sem, 0, 0

    def turn(self, base):
        self.base, self.k = base, 0

    def did(self, instruction):
        instruction.then_inc(self.sem, 1)
        self.k += 1

    def wait(self):
        self.eng.wait_ge(self.sem, self.base + self.k)


class Space:

    def __init__(self, nc, ctx, phase):
        self.nc, self.ctx, self.phase, self.signals = nc, ctx, phase, []
        ctx.callback(self.clear_signals)

    def sb(self, name, shape, dt=F32):
        return self.ctx.enter_context(self.nc.sbuf_tensor(f"{self.phase}_{name}", shape, dt))

    def ps(self, name, cols, dt=F32):
        return self.ctx.enter_context(self.nc.psum_tensor(f"{self.phase}_{name}", [P, cols], dt))

    def sem(self, name):
        self.signals.append(self.nc.alloc_semaphore(name=f"{self.phase}_{name}"))
        return self.signals[-1]

    def clear_signals(self):
        self.nc.clear_and_free_semaphores(self.signals)
        self.nc.all_engine_barrier()

    def sems(self, name, n):
        return [self.sem(f"{name}{j}") for j in range(n)]


AD, SC = 16, 32
HID = 4 * C
HID_T = HID // P
NT = HW // P
GN_EPS = 1e-5
VEC_HEAD = 15


def phase_conv(nc, D):
    with ExitStack() as ctx:
        s = Space(nc, ctx, "conv")
        sb, ps, sem, sems = s.sb, s.ps, s.sem, s.sems
        group = sb("group", [P, P])
        fc1 = sb("fc1", [P, CH, 64])
        fc2 = sb("fc2", [64, C])
        wq, wk = sb("wq", [SC, 4 * AD]), sb("wk", [SC, 4 * AD])
        wv = sb("wv", [SC, SC])
        proj = sb("proj", [SC, 2 * SC])
        ffn1 = sb("ffn1", [P, CH, HID])
        ffn2 = sb("ffn2", [P, HID_T, C])
        fc1_b, fc2_b = sb("fc1_b", [64, 1]), sb("fc2_b", [P, CH])
        bq, bk, bv = sb("bq", [AD, 1]), sb("bk", [AD, 1]), sb("bv", [SC, 1])
        proj_b = sb("proj_b", [SC, 1])
        ffn1_b, ffn2_b = sb("ffn1_b", [P, HID_T]), sb("ffn2_b", [P, CH])
        ident = sb("ident", [P, P])
        loads = [(group, "c_group"), (fc1, "fc1"), (fc2, "fc2"), (wq, "wq"), (wk, "wk"), (wv, "wv"),
                 (proj, "proj"), (ffn1, "ffn1"), (ffn2, "ffn2"), (fc1_b, "fc1_b"), (fc2_b, "fc2_b"),
                 (bq, "bq"), (bk, "bk"), (bv, "bv"), (proj_b, "proj_b"), (ffn1_b, "ffn1_b"),
                 (ffn2_b, "ffn2_b"), (ident, "c_ident")]
        nfc2_b, fence = sb("nfc2_b", [P, CH]), sb("fence", [P, 1])
        ones = sb("ones", [33, 2 * SC])
        X = [sb(f"X{u}", [P, CH, HW]) for u in range(2)]
        Y = [sb(f"Y{u}", [P, CH, HW]) for u in range(2)]
        T = [sb(f"T{u}", [P, CH, HW]) for u in range(2)]
        stats, mv = sb("stats", [P, CH, 2, 6]), sb("mv", [P, CH, 2])
        sq, st2 = sb("sq", [P, CH]), sb("st2", [P, 4])
        gs, var, sd, rs = sb("gs", [P, 4]), sb("var", [P, CH]), sb("sd", [P, CH]), sb("rs", [P, CH])
        nmr, sein = sb("nmr", [P, CH]), sb("sein", [P, CH])
        f1, ex, gate = sb("f1", [64, 1]), sb("ex", [P, CH]), sb("gate", [P, CH])
        scale, shift = sb("scale", [P, CH]), sb("shift", [P, CH])
        qq, kk = sb("qq", [AD + 1, HW]), sb("kk", [AD + 1, HW])
        vT = sb("vT", [P, NT, SC + 1])
        nmax, nmaxT = sb("nmax", [P, NT]), sb("nmaxT", [NT, P])
        PR = sb("PR", [P, NT, HW])
        rrow, osb, att = sb("rrow", [33, HW]), sb("osb", [SC, HW]), sb("att", [SC, HW])
        H = sb("H", [P, HID_T, HALF])
        pA, pB, pO = ps("pA", HW), ps("pB", HW), ps("pO", HW)
        pM, pF = ps("pM", HALF), ps("pF", HALF)
        pAB = [pA, pB]
        banks = [pA[:, 0:HALF], pA[:, HALF:HW], pB[:, 0:HALF], pB[:, HALF:HW]]

        weights_in, consts = sem("weights_in"), sem("consts")
        x_in, x_free = sems("x_in", 2), sems("x_free", 2)
        vec, gs_done, var_done, sd_done = sem("vec"), sem("gs_done"), sem("var_done"), sem("sd_done")
        st2_done, sein_done = sem("st2_done"), sem("sein_done")
        fc1_done, f1_done, fc2_done, ex_done = sem("fc1_done"), sem("f1_done"), sem("fc2_done"), sem("ex_done")
        y_done, qk_done, q_in, v_done, vT_in = sem("y_done"), sem("qk_done"), sem("q_in"), sem("v_done"), sem("vT_in")
        s_done, max_done = sem("s_done"), sem("max_done")
        maxT_done, maxT_in, nmax_in = sem("maxT_done"), sem("maxT_in"), sem("nmax_in")
        st_done, exp_done, pv_done = sem("st_done"), sem("exp_done"), sem("pv_done")
        rrow_done, bc_done, att_done, proj_done, y0_done = sem("rrow_done"), sem("bc_done"), sem("att_done"), sem("proj_done"), sem("y0_done")
        h_done, relu_done, o_done, t_done = sem("h_done"), sem("relu_done"), sem("o_done"), sem("t_done")
        t_out = sems("t_out", 2)
        block = ctx.enter_context(nc.Block())
        tv = D["t1"]

        @block.gpsimd
        def _(pool):
            pool.memset(ones[:, :], 1.0).then_inc(consts, 1)
            pool.memset(vT[:, :, SC:SC + 1], 1.0).then_inc(consts, 1)
            pool.memset(kk[:, :], 1.0).then_inc(consts, 1)
            with pool.Fori(0, B // 2) as i:
                n16 = pool.snap(i * 16 + 16)
                for u in range(2):
                    pool.wait_ge(x_free[u], n16)
                    pool.dma_start(X[u][:, :, :], D["x"][i * 2 + u].rearrange("(h p) n -> p h n", p=P)).then_inc(x_in[u], 16)

        @block.sync
        def _(sync):
            for dst, name in loads:
                sync.dma_start(dst[tuple(slice(None) for _ in dst.shape)], D[name]).then_inc(weights_in, 16)
            with sync.Fori(0, B // 2) as i:
                b0 = sync.snap(i * 2)
                for u in range(2):
                    sync.wait_ge(maxT_in, b0 + (u + 1))
                    sync.dma_start(qq[AD:AD + 1, :].rearrange("a (t p) -> a t p", p=P), nmaxT[:, :]).then_inc(nmax_in, 16)
                    sync.wait_ge(t_done, b0 * 4 + 4 * (u + 1))
                    sync.dma_start(tv[i * 2 + u].rearrange("(h p) n -> p h n", p=P), T[u][:, :, :]).then_inc(t_out[u], 16)
            for u in range(2):
                sync.wait_ge(t_out[u], 16 * (B // 2 + 1))

        @block.vector
        def _(v):
            own = Steps(v, vec)
            v.wait_ge(weights_in, 16 * len(loads))
            v.tensor_scalar(nfc2_b[:, :], fc2_b[:, :], -1.0, None, ALU.mult).then_inc(consts, 1)
            for u in range(2):
                v.sem_inc(x_free[u], 16)
                v.sem_inc(t_out[u], 16)
            with v.Fori(0, B // 2) as i:
                b0 = v.snap(i * 2)
                for u in range(2):
                    own.turn(i * (2 * VEC_HEAD) + u * VEC_HEAD)
                    b1 = v.snap(b0 + (u + 1))
                    v.wait_ge(x_in[u], i * 16 + 16)
                    for h in range(CH):
                        for c in range(2):
                            ins = v.bn_stats(stats[:, h, c, :], X[u][:, h, c * HALF:(c + 1) * HALF])
                    own.did(ins)
                    own.wait()
                    v.memset(fence[:, :], 0.0)
                    for h in range(CH):
                        ins = v.bn_aggr(mv[:, h, :], stats[:, h, :, :])
                    own.did(ins)
                    own.wait()
                    v.tensor_copy(st2[:, 0:2], mv[:, :, 0])
                    own.did(v.tensor_tensor(sq[:, :], mv[:, :, 0], mv[:, :, 0], ALU.mult))
                    own.wait()
                    v.tensor_tensor(st2[:, 2:4], sq[:, :], mv[:, :, 1], ALU.add).then_inc(st2_done, 1)
                    v.wait_ge(gs_done, b1)
                    own.did(v.tensor_copy(gs[:, :], pM[:, 0:4]))
                    own.wait()
                    own.did(v.tensor_tensor(sq[:, :], gs[:, 0:2], gs[:, 0:2], ALU.mult))
                    own.wait()
                    own.did(v.tensor_tensor(var[:, :], gs[:, 2:4], sq[:, :], ALU.subtract))
                    own.wait()
                    v.tensor_scalar(var[:, :], var[:, :], 0.0, GN_EPS, ALU.max, ALU.add).then_inc(var_done, 1)
                    v.wait_ge(sd_done, b1)
                    own.did(v.reciprocal(rs[:, :], sd[:, :]))
                    own.wait()
                    own.did(v.scalar_tensor_tensor(nmr[:, :], gs[:, 0:2], -1.0, rs[:, :], ALU.mult, ALU.mult))
                    own.did(v.tensor_tensor(sein[:, :], st2[:, 0:2], rs[:, :], ALU.mult))
                    own.wait()
                    v.tensor_tensor(sein[:, :], sein[:, :], nmr[:, :], ALU.add).then_inc(sein_done, 1)
                    v.wait_ge(ex_done, b1)
                    own.did(v.tensor_scalar(gate[:, :], ex[:, :], 1.0, None, ALU.add))
                    own.wait()
                    own.did(v.reciprocal(gate[:, :], gate[:, :]))
                    own.wait()
                    own.did(v.tensor_tensor(scale[:, :], rs[:, :], gate[:, :], ALU.mult))
                    own.did(v.tensor_tensor(shift[:, :], nmr[:, :], gate[:, :], ALU.mult))
                    own.wait()
                    for h in range(CH):
                        ins = v.tensor_scalar(Y[u][:, h, :], X[u][:, h, :], scale[:, h:h + 1], shift[:, h:h + 1], ALU.mult, ALU.add)
                    ins.then_inc(y_done, 1)
                    v.wait_ge(v_done, b1)
                    v.tensor_copy(vT[:, :, 0:SC], pF[:, 0:NT * SC].rearrange("p (t c) -> p t c", c=SC)).then_inc(vT_in, 1)
                    for t in range(NT):
                        v.wait_ge(s_done, b0 * NT + (u * NT + t + 1))
                        v.tensor_reduce(nmax[:, t:t + 1], pAB[t % 2][:, :], AXX, ALU.max, negate=True).then_inc(max_done, 1)
                    v.wait_ge(maxT_done, b1)
                    v.tensor_copy(nmaxT[:, :], pM[0:NT, 0:P]).then_inc(maxT_in, 1)
                    v.wait_ge(pv_done, b1)
                    v.reciprocal(rrow[SC:SC + 1, :], pO[SC:SC + 1, :]).then_inc(rrow_done, 1)
                    own.did(v.tensor_copy(osb[:, :], pO[0:SC, :]))
                    v.wait_ge(bc_done, b1)
                    own.wait()
                    own.did(v.tensor_tensor(att[:, :], osb[:, :], pA[0:SC, :], ALU.mult))
                    own.wait()
                    v.tensor_scalar(att[:, :], att[:, :], bv[:, 0:1], None, ALU.add).then_inc(att_done, 1)
                    v.wait_ge(proj_done, b1)
                    v.tensor_scalar(Y[u][0:SC, 0, :], pB[0:SC, :], proj_b[:, 0:1], None, ALU.add).then_inc(y0_done, 1)
                    v.wait_ge(t_out[u], i * 16 + 16)
                    for th in range(2):
                        for o in range(CH):
                            k = th * CH + o
                            v.wait_ge(o_done, b0 * 4 + (u * 4 + k + 1))
                            cols = slice(th * HALF, (th + 1) * HALF)
                            ins = v.scalar_tensor_tensor(T[u][:, o, cols], pO[:, o * HALF:(o + 1) * HALF], ffn2_b[:, o:o + 1],
                                                         X[u][:, o, cols], ALU.add, ALU.add)
                            ins.then_inc(t_done, 1)
                    v.wait_ge(t_done, b0 * 4 + 4 * (u + 1))
                    v.sem_inc(x_free[u], 16)
            assert own.k == VEC_HEAD

        @block.tensor
        def _(pe):
            pe.wait_ge(weights_in, 16 * len(loads))
            pe.wait_ge(consts, 4)
            with pe.Fori(0, B // 2) as i:
                b0 = pe.snap(i * 2)
                for u in range(2):
                    b1 = pe.snap(b0 + (u + 1))
                    pe.wait_ge(st2_done, b1)
                    pe.matmul(pM[:, 0:4], group[:, :], st2[:, :], start=True, stop=True).then_inc(gs_done, 1)
                    pe.wait_ge(sein_done, b1)
                    for h in range(CH):
                        mm = pe.matmul(pM[0:64, 4:5], fc1[:, h, :], sein[:, h:h + 1], start=(h == 0), stop=(h == CH - 1))
                    mm.then_inc(fc1_done, 1)
                    pe.wait_ge(f1_done, b1)
                    for h in range(CH):
                        mm = pe.matmul(pM[:, 5 + h:6 + h], fc2[:, h * P:(h + 1) * P], f1[:, :], start=True, stop=True)
                    mm.then_inc(fc2_done, 1)
                    pe.wait_ge(y_done, b1)
                    for j in range(2):
                        cols = slice(j * HALF, (j + 1) * HALF)
                        pe.matmul(pA[0:4 * AD, cols], wq[:, :], Y[u][0:SC, 0, cols], start=True, stop=True)
                        mm = pe.matmul(pB[0:4 * AD, cols], wk[:, :], Y[u][0:SC, 0, cols], start=True, stop=True)
                    mm.then_inc(qk_done, 1)
                    for t in range(NT):
                        mm = pe.matmul(pF[:, t * SC:(t + 1) * SC], Y[u][0:SC, 0, t * P:(t + 1) * P], wv[:, :], start=True, stop=True)
                    mm.then_inc(v_done, 1)
                    pe.wait_ge(q_in, b1)
                    for t in range(NT):
                        if t >= 2:
                            pe.wait_ge(max_done, b0 * NT + (u * NT + t - 1))
                        for j in range(2):
                            mm = pe.matmul(pAB[t % 2][:, j * HALF:(j + 1) * HALF], qq[0:AD, t * P:(t + 1) * P],
                                           kk[0:AD, j * HALF:(j + 1) * HALF], start=True, stop=True)
                        mm.then_inc(s_done, 1)
                    pe.wait_ge(max_done, b0 * NT + (u + 1) * NT)
                    pe.transpose(pM[0:NT, 0:P], nmax[:, :], ident[:, :]).then_inc(maxT_done, 1)
                    pe.wait_ge(nmax_in, b1 * 16)
                    pe.wait_ge(vT_in, b1)

                    def weighted(t):
                        pe.wait_ge(exp_done, b0 * NT + (u * NT + t + 1))
                        for j in range(2):
                            mm = pe.matmul(pO[0:SC + 1, j * HALF:(j + 1) * HALF], vT[:, t, :], PR[:, t, j * HALF:(j + 1) * HALF],
                                           start=(t == 0), stop=(t == NT - 1))
                        return mm

                    for t in range(NT):
                        if t >= 2:
                            pe.wait_ge(exp_done, b0 * NT + (u * NT + t - 1))
                        for j in range(2):
                            mm = pe.matmul(pAB[t % 2][:, j * HALF:(j + 1) * HALF], kk[0:AD + 1, t * P:(t + 1) * P],
                                           qq[0:AD + 1, j * HALF:(j + 1) * HALF], start=True, stop=True)
                        mm.then_inc(st_done, 1)
                        if t >= 1:
                            weighted(t - 1)
                    weighted(NT - 1).then_inc(pv_done, 1)
                    pe.wait_ge(rrow_done, b1)
                    for j in range(2):
                        mm = pe.matmul(pA[0:2 * SC, j * HALF:(j + 1) * HALF], ones[SC:SC + 1, :], rrow[SC:SC + 1, j * HALF:(j + 1) * HALF],
                                       start=True, stop=True)
                    mm.then_inc(bc_done, 1)
                    pe.wait_ge(att_done, b1)
                    for j in range(2):
                        mm = pe.matmul(pB[0:2 * SC, j * HALF:(j + 1) * HALF], proj[:, :], att[:, j * HALF:(j + 1) * HALF], start=True, stop=True)
                    mm.then_inc(proj_done, 1)
                    pe.wait_ge(y0_done, b1)
                    for th in range(2):
                        cols = slice(th * HALF, (th + 1) * HALF)
                        for f in range(HID_T):
                            g = th * HID_T + f
                            if g >= 4:
                                pe.wait_ge(relu_done, b0 * 2 * HID_T + (u * 2 * HID_T + g - 3))
                            for h in range(CH):
                                mm = pe.matmul(banks[g % 4], ffn1[:, h, f * P:(f + 1) * P], Y[u][:, h, cols], start=(h == 0), stop=(h == CH - 1))
                            mm.then_inc(h_done, 1)
                        pe.wait_ge(relu_done, b0 * 2 * HID_T + (u * 2 + th + 1) * HID_T)
                        for o in range(CH):
                            if th:
                                pe.wait_ge(t_done, b0 * 4 + (u * 4 + o + 1))
                            for f in range(HID_T):
                                mm = pe.matmul(pO[:, o * HALF:(o + 1) * HALF], ffn2[:, f, o * P:(o + 1) * P], H[:, f, :],
                                               start=(f == 0), stop=(f == HID_T - 1))
                            mm.then_inc(o_done, 1)

        @block.scalar
        def _(act):
            act.wait_ge(weights_in, 16 * len(loads))
            act.wait_ge(consts, 4)
            with act.Fori(0, B // 2) as i:
                b0 = act.snap(i * 2)
                for u in range(2):
                    b1 = act.snap(b0 + (u + 1))
                    act.wait_ge(var_done, b1)
                    act.activation(sd[:, :], var[:, :], ACT.Sqrt).then_inc(sd_done, 1)
                    act.wait_ge(fc1_done, b1)
                    act.activation(f1[:, :], pM[0:64, 4:5], ACT.Relu, bias=fc1_b[:, 0:1]).then_inc(f1_done, 1)
                    act.wait_ge(fc2_done, b1)
                    for h in range(CH):
                        ins = act.activation(ex[:, h:h + 1], pM[:, 5 + h:6 + h], ACT.Exp, bias=nfc2_b[:, h:h + 1], scale=-1.0)
                    ins.then_inc(ex_done, 1)
                    act.wait_ge(qk_done, b1)
                    act.activation(qq[0:AD, :], pA[0:AD, :], ACT.Identity, bias=bq[:, 0:1])
                    act.activation(kk[0:AD, :], pB[0:AD, :], ACT.Identity, bias=bk[:, 0:1]).then_inc(q_in, 1)
                    for t in range(NT):
                        act.wait_ge(st_done, b0 * NT + (u * NT + t + 1))
                        act.activation(PR[:, t, :], pAB[t % 2][:, :], ACT.Exp, scale=float(AD) ** -0.5).then_inc(exp_done, 1)
                    for th in range(2):
                        if th:
                            act.wait_ge(o_done, b0 * 4 + (u * 4 + CH))
                        for f in range(HID_T):
                            g = th * HID_T + f
                            act.wait_ge(h_done, b0 * 2 * HID_T + (u * 2 * HID_T + g + 1))
                            act.activation(H[:, f, :], banks[g % 4], ACT.Relu, bias=ffn1_b[:, f:f + 1]).then_inc(relu_done, 1)


DI = 512
NH, HD, DS = 8, 64, 64
KC = 4
NX = DI // P
ST = 512
NSUP = HW // ST
NC_ = ST // P
NG = NSUP * NC_
LN_EPS = 1e-5
RMS_EPS = float(np.finfo(np.float32).eps)
CREDIT = 2
SSM_STEPS = 122


def phase_ssm(nc, D):
    with ExitStack() as ctx:
        s_ = Space(nc, ctx, "ssm")
        sb, ps, sem, sems = s_.sb, s_.ps, s_.sem, s_.sems
        w_x = sb("w_x", [P, CH, DI + 2 * DS])
        w_z = sb("w_z", [P, CH, DI])
        w_dt = sb("w_dt", [P, CH, NH])
        w_out = sb("w_out", [P, NX, C])
        norm_w, gnorm_w = sb("norm_w", [P, CH]), sb("gnorm_w", [P, NX])
        conv_w, conv_b = sb("conv_w", [P, NX + 2, KC]), sb("conv_b", [P, NX + 2])
        dt_b, a_log, dp = sb("dt_b", [P, NH]), sb("a_log", [P, NH]), sb("dp", [P, NH])
        ident, upper, ones = sb("ident", [P, P]), sb("upper", [P, P]), sb("ones", [P, P])
        loads = [(w_x, "w_x"), (w_z, "w_z"), (w_dt, "w_dt"), (w_out, "w_out"), (norm_w, "norm_w"), (gnorm_w, "gnorm_w"),
                 (conv_w, "conv_w"), (conv_b, "conv_b"), (dt_b, "dt_b"), (a_log, "a_log"), (dp, "dp"),
                 (ident, "c_ident"), (upper, "c_upper")]
        neg_a, fence = sb("neg_a", [P, NH]), sb("fence", [P, 1])
        X = [sb(f"X{s}", [P, CH, ST]) for s in range(NSUP)]
        tT = sb("tT", [P, NC_, C])
        stats, mv = sb("stats", [P, NC_, 6]), sb("mv", [P, NC_, 2])
        ve, rstd, ve2, r2, xr = (sb(n, [P, NC_]) for n in ("ve", "rstd", "ve2", "r2", "xr"))
        xnT = [sb(f"xnT{j}", [P, C]) for j in range(NC_)]
        xnF = sb("xnF", [P, CH, ST])
        XC = [sb(f"XC{s}", [P, NX + 2, KC - 1 + ST]) for s in range(NSUP)]
        CV = sb("CV", [P, NX + 2, ST])
        XS = sb("XS", [P, NX + 2, ST])
        zs = sb("zs", [P, NC_, DI])
        dv, de, du, dd, dt4, dtA = (sb(n, [P, NC_, NH]) for n in ("dv", "de", "du", "dd", "dt4", "dtA"))
        cumS = [sb(f"cumS{j}", [P, 2 * NH]) for j in range(2)]
        sm = [sb(f"sm{j}", [P, 3, NH]) for j in range(2)]
        se = [sb(f"se{j}", [P, 3, NH]) for j in range(2)]
        dec = [sb(f"dec{j}", [P, NH, P]) for j in range(2)]
        Mm = [sb(f"Mm{j}", [P, P]) for j in range(2)]
        BT = [sb(f"BT{j}", [P, DS]) for j in range(2)]
        xdt = [sb(f"xdt{j}", [P, DI]) for j in range(2)]
        xw = [sb(f"xw{j}", [P, DI]) for j in range(2)]
        xd = [sb(f"xd{j}", [P, DI]) for j in range(2)]
        ya = [sb(f"ya{j}", [P, DI]) for j in range(2)]
        state, state_dec = sb("state", [DS, DI]), sb("state_dec", [DS, DI])
        yo = sb("yo", [P, DI])
        squares = sb("squares", [P, DI])
        ss = sb("ss", [P, NC_])
        vr, rr = sb("vr", [P, NC_]), sb("rr", [P, NC_])
        gF = sb("gF", [P, NX, P])
        oT = sb("oT", [P, NC_, C])
        OUT = [sb(f"OUT{s}", [P, NC_, C]) for s in range(NSUP)]
        k_t, k_p0, k_p1, k_s = ps("k_t", 512), ps("k_p0", 512), ps("k_p1", 512), ps("k_s", 512)
        k_decay, k_y, k_off = ps("k_decay", 1024), ps("k_y", 512), ps("k_off", 512)
        kp = [k_p0, k_p1]
        k_turn = [k_t, k_y]
        DTP, CUM, TOT, MT, BTP = (k_s[:, a:a + n] for a, n in ((0, 32), (32, NH), (32 + NH, NH), (128, P), (256, DS)))

        weights_in, consts, own_s = sem("weights_in"), sem("consts"), sem("vec")
        names = ("t_turned sq1_in sq1 sq2_in sq2 xn_in xn_turned xnF_in xc_done xc_in cv_in silu_in z_done z_in dt_done "
                 "dabs_in dexp_in du_in dln_in dt_in cum_done xs_turned t_in dec_in exp_in sm_in se_in bt_in xdt_in xw_in w_in px_read "
                 "y_done off_done snew_done h_in g_in g_turned gf_in o_done o_in ss_in rr_in rrs t2_in").split()
        S = {n: sem(n) for n in names}
        x_in, out_out = sems("x_in", NSUP), sems("out_out", NSUP)
        block = ctx.enter_context(nc.Block())

        def need(eng, name, value):
            eng.wait_ge(S[name], value + CREDIT)

        by_engine = {"act": "sq1 sq2 xnF_in xc_in silu_in z_in dexp_in dln_in exp_in se_in gf_in o_in ss_in rrs",
                     "pe": "t_turned xn_turned xc_done z_done dt_done cum_done xs_turned y_done off_done snew_done g_turned o_done"}

        def credit(eng, which):
            mine = by_engine[which].split() if which in by_engine else [n for n in names if n not in " ".join(by_engine.values()).split()]
            for n in mine:
                eng.sem_inc(S[n], CREDIT)

        @block.gpsimd
        def _(pool):
            pool.memset(ones[:, :], 1.0).then_inc(consts, 1)
            pool.memset(XC[0][:, :, 0:KC - 1], 0.0).then_inc(consts, 1)
            pool.memset(XC[1][:, NX:NX + 2, :], 0.0).then_inc(consts, 1)
            pool.memset(XC[0][:, NX:NX + 2, KC - 1:], 0.0).then_inc(consts, 1)
            with pool.Fori(0, B) as i:
                for s in range(NSUP):
                    need(pool, "sq1_in", i * NSUP + (s + 1 - NSUP))
                    pool.dma_start(X[s][:, :, :], D["t1"][i].rearrange("(h p) n -> p h n", p=P)[:, :, s * ST:(s + 1) * ST]).then_inc(x_in[s], 16)

        @block.sync
        def _(sync):
            for dst, name in loads:
                sync.dma_start(dst[tuple(slice(None) for _ in dst.shape)], D[name]).then_inc(weights_in, 16)
            with sync.Fori(0, B) as i:
                for s in range(NSUP):
                    need(sync, "t2_in", i * NG + (s + 1) * NC_)
                    sync.dma_start(D["t2"][i].rearrange("(s c p) f -> s p c f", p=P, c=NC_)[s], OUT[s][:, :, :]).then_inc(out_out[s], 16)
            for s in range(NSUP):
                sync.wait_ge(out_out[s], 16 * (B + 1))

        @block.vector
        def _(v):
            own = Steps(v, own_s)
            v.wait_ge(weights_in, 16 * len(loads))
            for s in range(NSUP):
                v.sem_inc(out_out[s], 16)
            for k in range(CH):
                for w in (w_x, w_z, w_dt):
                    v.tensor_scalar(w[:, k, :], w[:, k, :], norm_w[:, k:k + 1], None, ALU.mult)
            for k in range(NX):
                ins = v.tensor_scalar(w_out[:, k, :], w_out[:, k, :], gnorm_w[:, k:k + 1], None, ALU.mult)
            ins.then_inc(consts, 1)
            v.wait_ge(consts, 6)
            v.tensor_scalar(neg_a[:, :], neg_a[:, :], -1.0, None, ALU.mult).then_inc(consts, 1)
            v.wait_ge(consts, 7)
            credit(v, "v")
            with v.Fori(0, B) as i:
                own.turn(i * SSM_STEPS)
                g0, s0 = v.snap(i * NG), v.snap(i * NSUP)
                for s in range(NSUP):
                    s1 = v.snap(s0 + (s + 1))
                    for q in range(2):
                        need(v, "t_turned", i * 2 * NSUP + (s * 2 + q + 1))
                        v.tensor_copy(tT[:, 2 * q:2 * q + 2, :], k_turn[q][:, :].rearrange("p (c f) -> p c f", c=2)).then_inc(S["t_in"], 1)
                    need(v, "t_in", i * 2 * NSUP + (s + 1) * 2)
                    for c in range(NC_):
                        ins = v.bn_stats(stats[:, c, :], tT[:, c, :])
                    own.did(ins)
                    own.wait()
                    v.memset(fence[:, :], 0.0)
                    for c in range(NC_):
                        ins = v.bn_aggr(mv[:, c, :], stats[:, c, :])
                    own.did(ins)
                    own.wait()
                    v.tensor_scalar(ve[:, :], mv[:, :, 1], LN_EPS, None, ALU.add).then_inc(S["sq1_in"], 1)
                    need(v, "sq1", s1)
                    own.did(v.reciprocal(rstd[:, :], rstd[:, :]))
                    own.wait()
                    own.did(v.tensor_tensor(ve2[:, :], mv[:, :, 1], rstd[:, :], ALU.mult))
                    own.wait()
                    own.did(v.tensor_tensor(ve2[:, :], ve2[:, :], rstd[:, :], ALU.mult))
                    own.wait()
                    v.tensor_scalar(ve2[:, :], ve2[:, :], RMS_EPS, None, ALU.add).then_inc(S["sq2_in"], 1)
                    need(v, "sq2", s1)
                    own.did(v.reciprocal(r2[:, :], r2[:, :]))
                    own.wait()
                    own.did(v.tensor_tensor(xr[:, :], r2[:, :], rstd[:, :], ALU.mult))
                    own.wait()
                    for c in range(NC_):
                        v.tensor_scalar(xnT[c][:, :], tT[:, c, :], mv[:, c, 0:1], xr[:, c:c + 1], ALU.subtract, ALU.mult).then_inc(S["xn_in"], 1)
                    if s:
                        own.did(v.tensor_copy(XC[s][:, :, 0:KC - 1], XC[0][:, :, ST:ST + KC - 1]))
                    def conv(m):
                        need(v, "xc_in", s0 * (NX + 2) + (s * (NX + 2) + m + 1))
                        rows = P if m < NX else DS
                        own.wait()
                        own.did(v.tensor_scalar(CV[0:rows, m, :], XC[s][0:rows, m, 0:ST], conv_w[0:rows, m, 0:1], None, ALU.mult))
                        for k in range(1, KC):
                            own.wait()
                            ins = v.scalar_tensor_tensor(CV[0:rows, m, :], XC[s][0:rows, m, k:k + ST], conv_w[0:rows, m, k:k + 1], CV[0:rows, m, :], ALU.mult, ALU.add)
                            if k < KC - 1:
                                own.did(ins)
                        ins.then_inc(S["cv_in"], 1)
                    need(v, "dt_done", s1)
                    own.did(v.tensor_tensor(dv[:, :, :], DTP.rearrange("p (c h) -> p c h", h=NH), dt_b[:, :].unsqueeze(1).to_broadcast([P, NC_, NH]), ALU.add))
                    own.wait()
                    v.scalar_tensor_tensor(de[:, :, :], dv[:, :, :], -1.0, dv[:, :, :], ALU.mult, ALU.max).then_inc(S["dabs_in"], 1)
                    conv(0)
                    need(v, "dexp_in", s1)
                    v.tensor_scalar(du[:, :, :], de[:, :, :], 1.0, None, ALU.add).then_inc(S["du_in"], 1)
                    need(v, "du_in", s1)
                    own.did(v.tensor_scalar(dd[:, :, :], du[:, :, :], 1.0, None, ALU.subtract))
                    own.wait()
                    own.did(v.tensor_scalar(dtA[:, :, :], dd[:, :, :], 0.0, None, ALU.is_equal))
                    own.did(v.tensor_scalar(dd[:, :, :], dd[:, :, :], 1e-30, None, ALU.max))
                    own.wait()
                    own.did(v.reciprocal(dd[:, :, :], dd[:, :, :]))
                    conv(1)
                    need(v, "dln_in", s1)
                    own.wait()
                    own.did(v.tensor_tensor(dd[:, :, :], dt4[:, :, :], dd[:, :, :], ALU.mult))
                    own.wait()
                    own.did(v.tensor_tensor(dd[:, :, :], dtA[:, :, :], dd[:, :, :], ALU.add))
                    own.wait()
                    own.did(v.tensor_tensor(dd[:, :, :], de[:, :, :], dd[:, :, :], ALU.mult))
                    own.wait()
                    own.did(v.scalar_tensor_tensor(dt4[:, :, :], dv[:, :, :], 0.0, dd[:, :, :], ALU.max, ALU.add))
                    own.wait()
                    v.tensor_tensor(dtA[:, :, :], dt4[:, :, :], neg_a[:, :].unsqueeze(1).to_broadcast([P, NC_, NH]), ALU.mult).then_inc(S["dt_in"], 1)
                    for m in range(2, NX + 2):
                        conv(m)
                    def prepare(c):
                        g, j = s * NC_ + c, c % 2
                        g1 = v.snap(g0 + (g + 1))
                        if g == 0:
                            v.memset(state[:, :], 0.0).then_inc(S["h_in"], 1)
                        need(v, "cum_done", g1)
                        own.did(v.tensor_copy(cumS[j][:, :], k_s[:, 32:32 + 2 * NH]))
                        own.wait()
                        v.tensor_tensor(sm[j][:, 0, :], cumS[j][:, NH:2 * NH], cumS[j][:, 0:NH], ALU.subtract)
                        v.tensor_copy(sm[j][:, 1:3, :], cumS[j][:, :].rearrange("p (a h) -> p a h", h=NH)).then_inc(S["sm_in"], 1)
                        for h in range(NH):
                            ins = v.tensor_scalar(dec[j][:, h, :], k_decay[:, h * P:(h + 1) * P], cumS[j][:, h:h + 1], 0.0, ALU.subtract, ALU.min)
                        ins.then_inc(S["dec_in"], 1)
                        own.did(v.tensor_tensor(Mm[j][:, :], MT, upper[:, :], ALU.mult))
                        v.tensor_copy(BT[j][:, :], BTP).then_inc(S["bt_in"], 1)
                        need(v, "xs_turned", g1)
                        heads = k_p0[:, :].rearrange("p (h d) -> p h d", h=NH)
                        v.tensor_tensor(xdt[j][:, :].rearrange("p (h d) -> p h d", h=NH), heads, dt4[:, c, :].unsqueeze(2).to_broadcast([P, NH, HD]), ALU.mult).then_inc(S["xdt_in"], 1)
                        v.tensor_tensor(xd[j][:, :].rearrange("p (h d) -> p h d", h=NH), heads, dp[:, :].unsqueeze(2).to_broadcast([P, NH, HD]), ALU.mult).then_inc(S["px_read"], 1)
                        need(v, "se_in", g1)
                        need(v, "xdt_in", g1)
                        v.tensor_tensor(xw[j][:, :].rearrange("p (h d) -> p h d", h=NH), xdt[j][:, :].rearrange("p (h d) -> p h d", h=NH),
                                        se[j][:, 0, :].unsqueeze(2).to_broadcast([P, NH, HD]), ALU.mult).then_inc(S["xw_in"], 1)
                        need(v, "exp_in", g1)
                        own.wait()
                        v.tensor_tensor(dec[j][:, :, :], dec[j][:, :, :], Mm[j][:, :].unsqueeze(1).to_broadcast([P, NH, P]), ALU.mult).then_inc(S["w_in"], 1)

                    def finish(c):
                        g, j = s * NC_ + c, c % 2
                        g1 = v.snap(g0 + (g + 1))
                        if g < NG - 1:
                            own.wait()
                            own.did(v.tensor_tensor(state_dec[:, :].rearrange("p (h d) -> p h d", h=NH), state[:, :].rearrange("p (h d) -> p h d", h=NH),
                                                    se[j][0:DS, 2, :].unsqueeze(2).to_broadcast([DS, NH, HD]), ALU.mult))
                            need(v, "snew_done", i * (NG - 1) + (g + 1))
                            need(v, "off_done", g1)
                            own.wait()
                            v.tensor_tensor(state[:, :], state_dec[:, :], k_p1[0:DS, :], ALU.add).then_inc(S["h_in"], 1)
                        need(v, "y_done", g1)
                        need(v, "px_read", g1)
                        own.wait()
                        own.did(v.tensor_tensor(ya[j][:, :], xd[j][:, :], k_y[:, :], ALU.add))
                        need(v, "off_done", g1)
                        own.did(v.tensor_tensor(yo[:, :].rearrange("p (h d) -> p h d", h=NH), k_off[:, :].rearrange("p (h d) -> p h d", h=NH),
                                                se[j][:, 1, :].unsqueeze(2).to_broadcast([P, NH, HD]), ALU.mult))
                        own.wait()
                        own.did(v.tensor_tensor(ya[j][:, :], ya[j][:, :], yo[:, :], ALU.add))
                        need(v, "z_in", g1)
                        own.wait()
                        v.tensor_tensor(ya[j][:, :], ya[j][:, :], zs[:, c, :], ALU.mult).then_inc(S["g_in"], 1)

                    prepare(0)
                    for c in range(NC_):
                        if c + 1 < NC_:
                            prepare(c + 1)
                        finish(c)
                    need(v, "ss_in", g0 + (s + 1) * NC_)
                    v.tensor_scalar(vr[:, :], ss[:, :], 1.0 / DI, LN_EPS, ALU.mult, ALU.add).then_inc(S["rr_in"], 1)
                    need(v, "rrs", s1)
                    own.did(v.reciprocal(rr[:, :], rr[:, :]))
                    own.wait()
                    v.wait_ge(out_out[s], i * 16 + 16)
                    for c in range(NC_):
                        need(v, "o_in", g0 + (s * NC_ + c + 1))
                        ins = v.scalar_tensor_tensor(oT[:, c, :], oT[:, c, :], rr[:, c:c + 1], tT[:, c, :], ALU.mult, ALU.add)
                        v.tensor_scalar(OUT[s][:, c, :], tT[:, c, :], mv[:, c, 0:1], rstd[:, c:c + 1], ALU.subtract, ALU.mult)
                    own.did(ins)
                    own.did(v.tensor_scalar(vr[:, :], vr[:, :], 1.0, None, ALU.mult))
                    own.wait()
                    for c in range(NC_):
                        v.tensor_tensor(OUT[s][:, c, :], OUT[s][:, c, :], oT[:, c, :], ALU.add).then_inc(S["t2_in"], 1)
            assert own.k == SSM_STEPS

        @block.tensor
        def _(pe):
            pe.wait_ge(weights_in, 16 * len(loads))
            pe.wait_ge(consts, 7)
            credit(pe, "pe")
            with pe.Fori(0, B) as i:
                g0, s0 = pe.snap(i * NG), pe.snap(i * NSUP)
                for s in range(NSUP):
                    s1 = pe.snap(s0 + (s + 1))
                    pe.wait_ge(x_in[s], i * 16 + 16)
                    need(pe, "o_in", g0 + s * NC_)
                    for c in range(NC_):
                        for k in range(CH):
                            mm = pe.transpose(k_turn[c // 2][:, (c % 2) * C + k * P:(c % 2) * C + (k + 1) * P], X[s][:, k, c * P:(c + 1) * P], ident[:, :])
                        if c % 2:
                            mm.then_inc(S["t_turned"], 1)
                    for c in range(NC_):
                        need(pe, "xn_in", g0 + (s * NC_ + c + 1))
                        for k in range(CH):
                            mm = pe.transpose(k_turn[c // 2][:, (c % 2) * C + k * P:(c % 2) * C + (k + 1) * P], xnT[c][:, k * P:(k + 1) * P], ident[:, :])
                        if c % 2:
                            mm.then_inc(S["xn_turned"], 1)
                    need(pe, "xnF_in", i * 2 * NSUP + (s + 1) * 2)
                    for c in range(NC_):
                        for k in range(CH):
                            mm = pe.matmul(DTP[:, c * NH:(c + 1) * NH], xnF[:, k, c * P:(c + 1) * P], w_dt[:, k, :], start=(k == 0), stop=(k == CH - 1))
                    mm.then_inc(S["dt_done"], 1)
                    need(pe, "px_read", g0 + s * NC_)
                    need(pe, "h_in", g0 + s * NC_) if s else None
                    n = 0
                    for m in range(NX + 2):
                        rows = P if m < NX else DS
                        at = m * P if m < NX else DI + (m - NX) * DS
                        if m >= 2:
                            need(pe, "xc_in", s0 * (NX + 2) + (s * (NX + 2) + m - 1))
                        for k in range(CH):
                            mm = pe.matmul(kp[m % 2][0:rows, :], w_x[:, k, at:at + rows], xnF[:, k, :], start=(k == 0), stop=(k == CH - 1))
                        mm.then_inc(S["xc_done"], 1)
                    for c in range(NC_):
                        need(pe, "xc_in", s0 * (NX + 2) + (s + 1) * (NX + 2)) if c == 0 else None
                        if c >= 2:
                            need(pe, "z_in", g0 + (s * NC_ + c - 1))
                        for k in range(CH):
                            mm = pe.matmul(kp[c % 2][:, :], xnF[:, k, c * P:(c + 1) * P], w_z[:, k, :], start=(k == 0), stop=(k == CH - 1))
                        mm.then_inc(S["z_done"], 1)
                    need(pe, "z_in", g0 + (s + 1) * NC_)
                    need(pe, "silu_in", s0 * (NX + 2) + (s + 1) * (NX + 2))
                    need(pe, "dt_in", s1)

                    def prepare(c):
                        g, j = s * NC_ + c, c % 2
                        g1 = pe.snap(g0 + (g + 1))
                        cols = slice(c * P, (c + 1) * P)
                        need(pe, "bt_in", g0 + g)
                        pe.matmul(CUM, upper[:, :], dtA[:, c, :], start=True, stop=True)
                        pe.matmul(TOT, ones[:, :], dtA[:, c, :], start=True, stop=True)
                        for h in range(NH):
                            pe.matmul(k_decay[:, h * P:(h + 1) * P], dtA[:, c, h:h + 1].to_broadcast([P, P]), upper[:, :], start=True, stop=True)
                        pe.transpose(BTP, XS[0:DS, NX, cols], ident[0:DS, 0:DS])
                        pe.matmul(MT, XS[0:DS, NX, cols], XS[0:DS, NX + 1, cols], start=True, stop=True).then_inc(S["cum_done"], 1)
                        need(pe, "px_read", g0 + g)
                        for m in range(NX):
                            mm = pe.transpose(k_p0[:, m * P:(m + 1) * P], XS[:, m, cols], ident[:, :])
                        mm.then_inc(S["xs_turned"], 1)

                    def finish(c):
                        g, j = s * NC_ + c, c % 2
                        g1 = pe.snap(g0 + (g + 1))
                        cols = slice(c * P, (c + 1) * P)
                        need(pe, "w_in", g1)
                        need(pe, "g_in", g0 + g)
                        for h in range(NH):
                            mm = pe.matmul(k_y[:, h * HD:(h + 1) * HD], dec[j][:, h, :], xdt[j][:, h * HD:(h + 1) * HD], start=True, stop=True)
                        mm.then_inc(S["y_done"], 1)
                        need(pe, "h_in", g1)
                        if g < NG - 1:
                            need(pe, "xw_in", g1)
                            need(pe, "bt_in", g1)
                            pe.matmul(k_p1[0:DS, :], BT[j][:, :], xw[j][:, :], start=True, stop=True).then_inc(S["snew_done"], 1)
                        if c:
                            output(c - 1)
                        need(pe, "gf_in", g0 + g)
                        pe.matmul(k_off[:, :], XS[0:DS, NX + 1, cols], state[:, :], start=True, stop=True).then_inc(S["off_done"], 1)

                    def turn(c):
                        g, j = s * NC_ + c, c % 2
                        need(pe, "g_in", g0 + (g + 1))
                        for m in range(NX):
                            mm = pe.transpose(k_off[:, m * P:(m + 1) * P], ya[j][:, m * P:(m + 1) * P], ident[:, :])
                        mm.then_inc(S["g_turned"], 1)

                    def output(c):
                        g1 = pe.snap(g0 + (s * NC_ + c + 1))
                        need(pe, "gf_in", g1)
                        need(pe, "o_in", g1 - 1)
                        for m in range(NX):
                            mm = pe.matmul(k_t[:, 0:C], gF[:, m, :], w_out[:, m, :], start=(m == 0), stop=(m == NX - 1))
                        mm.then_inc(S["o_done"], 1)

                    prepare(0)
                    for c in range(NC_):
                        if c + 1 < NC_:
                            prepare(c + 1)
                        if c:
                            turn(c - 1)
                        finish(c)
                    turn(NC_ - 1)
                    output(NC_ - 1)

        @block.scalar
        def _(act):
            act.wait_ge(weights_in, 16 * len(loads))
            act.activation(neg_a[:, :], a_log[:, :], ACT.Exp).then_inc(consts, 1)
            act.wait_ge(consts, 7)
            credit(act, "act")
            with act.Fori(0, B) as i:
                g0, s0 = act.snap(i * NG), act.snap(i * NSUP)
                for s in range(NSUP):
                    s1 = act.snap(s0 + (s + 1))
                    need(act, "sq1_in", s1)
                    act.activation(rstd[:, :], ve[:, :], ACT.Sqrt).then_inc(S["sq1"], 1)
                    need(act, "sq2_in", s1)
                    act.activation(r2[:, :], ve2[:, :], ACT.Sqrt).then_inc(S["sq2"], 1)
                    for q in range(2):
                        need(act, "xn_turned", i * 2 * NSUP + (s * 2 + q + 1))
                        for k in range(CH):
                            ins = act.activation(xnF[:, k, 2 * q * P:2 * (q + 1) * P].rearrange("p (c t) -> p c t", c=2),
                                                 k_turn[q][:, :].rearrange("p (c k t) -> p c k t", c=2, k=CH)[:, :, k, :], ACT.Copy)
                        ins.then_inc(S["xnF_in"], 1)
                    for m in range(NX + 2):
                        rows = P if m < NX else DS
                        need(act, "xc_done", s0 * (NX + 2) + (s * (NX + 2) + m + 1))
                        act.activation(XC[s][0:rows, m, KC - 1:], kp[m % 2][0:rows, :], ACT.Copy).then_inc(S["xc_in"], 1)
                        if m == 1:
                            need(act, "dabs_in", s1)
                            act.activation(de[:, :, :], de[:, :, :], ACT.Exp, scale=-1.0).then_inc(S["dexp_in"], 1)
                        if m == 3:
                            need(act, "du_in", s1)
                            act.activation(dt4[:, :, :], du[:, :, :], ACT.Ln).then_inc(S["dln_in"], 1)
                    for c in range(NC_):
                        need(act, "z_done", g0 + (s * NC_ + c + 1))
                        act.activation(zs[:, c, :], kp[c % 2][:, :], ACT.Silu).then_inc(S["z_in"], 1)
                    for m in range(NX + 2):
                        rows = P if m < NX else DS
                        need(act, "cv_in", s0 * (NX + 2) + (s * (NX + 2) + m + 1))
                        act.activation(XS[0:rows, m, :], CV[0:rows, m, :], ACT.Silu, bias=conv_b[0:rows, m:m + 1]).then_inc(S["silu_in"], 1)

                    def prepare(c):
                        g, j = s * NC_ + c, c % 2
                        g1 = act.snap(g0 + (g + 1))
                        need(act, "sm_in", g1)
                        act.activation(se[j][:, :, :], sm[j][:, :, :], ACT.Exp).then_inc(S["se_in"], 1)
                        need(act, "dec_in", g1)
                        act.activation(dec[j][:, :, :], dec[j][:, :, :], ACT.Exp).then_inc(S["exp_in"], 1)

                    def finish(c):
                        j, g1 = c % 2, act.snap(g0 + (s * NC_ + c + 1))
                        need(act, "g_in", g1)
                        act.activation(squares[:, :], ya[j][:, :], ACT.Square, accum_out=ss[:, c:c + 1]).then_inc(S["ss_in"], 1)
                        need(act, "g_turned", g1)
                        act.activation(gF[:, :, :], k_off[:, :].rearrange("p (m t) -> p m t", m=NX), ACT.Copy).then_inc(S["gf_in"], 1)

                    def output(c):
                        need(act, "o_done", act.snap(g0 + (s * NC_ + c + 1)))
                        act.activation(oT[:, c, :], k_t[:, 0:C], ACT.Copy).then_inc(S["o_in"], 1)

                    prepare(0)
                    for c in range(NC_):
                        if c + 1 < NC_:
                            prepare(c + 1)
                        finish(c)
                        if c:
                            output(c - 1)
                    output(NC_ - 1)
                    need(act, "rr_in", s1)
                    act.activation(rr[:, :], vr[:, :], ACT.Sqrt).then_inc(S["rrs"], 1)
EDGES = 1048576
COLS = EDGES // P
BW, KW = 512, 64
NBLOCK, NPART = COLS // BW, BW // KW
GROUPS = NBLOCK * NPART
P_BITS = 7
NODE_BITS = M.bit_length() - 1
KEY_BASE = 0x40000000
CLASS_1, CLASS_2 = 2.0 ** 33, 2.0 ** 65
XB = 2048
TB = 4


def phase_sort(nc, D):
    with ExitStack() as ctx:
        s_ = Space(nc, ctx, "sort")
        sb, ps, sem = s_.sb, s_.ps, s_.sem
        keys = [sb("keys0", [P, COLS]), sb("keys1", [P, COLS])]
        signs = sb("signs", [P, P_BITS])
        ident, ones = sb("ident", [P, P]), sb("ones", [P, P])
        flags = sb("flags", [P, 2, XB], I32)
        lows = sb("lows", [P, NPART])
        count, sums = sb("count", [P, 2 + NPART]), sb("sums", [P, 2 + NPART])
        total = sb("total", [P, 4], I32)
        edge_of = sb("edge_of", [1, 2])
        banks = [ps(f"bank{k}", 512) for k in range(4)]
        edges_in, consts_in, stored, blocks_out = sem("edges_in"), sem("consts_in"), sem("stored"), sem("blocks_out")
        ordered, turned, read, ends_in = sem("ordered"), sem("turned"), sem("read"), sem("ends_in")
        counted, summed, known = sem("counted"), sem("summed"), sem("known")
        block = ctx.enter_context(nc.Block())
        whole, first = {}, {}
        ways = ((whole, 2), (first, 1))
        blocks_at = []

        @block.vector
        def _(v):
            n = 0

            def did(ins):
                nonlocal n
                ins.then_inc(ordered, 1)
                n += 1

            class Rows:

                def __init__(self, buf, cur, width):
                    self.buf, self.cur, self.width = buf, cur, width

                def merge(self, size, mirrored):
                    a = self.buf[self.cur].rearrange("p (n b) -> p n b", b=size)
                    o = self.buf[1 - self.cur].rearrange("p (n b) -> p n b", b=size)
                    h = size // 2
                    lo, hi = a[:, :, 0:h], a[:, :, h:size]
                    v.wait_ge(ordered, n)
                    v.tensor_tensor(o[:, :, 0:h], lo, hi[:, :, ::-1] if mirrored else hi, ALU.min)
                    did(v.tensor_tensor(o[:, :, h:size], hi, lo[:, :, ::-1] if mirrored else lo, ALU.max))
                    self.cur = 1 - self.cur

                def sort(self, k0, k1):
                    for k in range(k0, k1 + 1):
                        self.merge(1 << k, True)
                        for j in range(k - 1, 0, -1):
                            self.merge(1 << j, False)

                def flip(self, r):
                    x = self.buf[self.cur]
                    v.wait_ge(ordered, n)
                    did(v.tensor_scalar(x, x, signs[:, r:r + 1], None, ALU.mult))

                def take_turned(self, t, scale):
                    nb = self.width // (TB * P)
                    for b in range(nb):
                        v.wait_ge(turned, t * nb + b + 1)
                        o = self.buf[1 - self.cur][:, b * TB * P:(b + 1) * TB * P]
                        if scale is None:
                            ins = v.tensor_copy(o, banks[b % 4][:, :])
                        else:
                            ins = v.tensor_scalar(o, banks[b % 4][:, :], signs[:, scale:scale + 1], None, ALU.mult)
                        ins.then_inc(read, 1)
                    v.wait_ge(read, (t + 1) * nb)
                    self.cur = 1 - self.cur

                def merge_rows(self, r):
                    for q in range(r, -1, -1):
                        dirs = 2 if r < P_BITS - 1 else 1
                        shape = dict(d=dirs, s=1 << (r - q), e=2, w=1 << q)
                        a = self.buf[self.cur].rearrange("p (n d s e w) -> p n d s e w", **shape)
                        o = self.buf[1 - self.cur].rearrange("p (n d s e w) -> p n d s e w", **shape)
                        v.wait_ge(ordered, n)
                        for d in range(dirs):
                            lo, hi = a[:, :, d, :, 0, :], a[:, :, d, :, 1, :]
                            v.tensor_tensor(o[:, :, d, :, 0, :], lo, hi, ALU.max if d else ALU.min)
                            ins = v.tensor_tensor(o[:, :, d, :, 1, :], lo, hi, ALU.min if d else ALU.max)
                        did(ins)
                        self.cur = 1 - self.cur

            v.memset(edge_of[:, :], 1.0).then_inc(ends_in, 1)
            v.memset(ones[:, :], 1.0)
            v.wait_ge(edges_in, 32)
            v.wait_ge(consts_in, 32)
            dst, src = keys[0][:, :].bitcast(I32), keys[1][:, :].bitcast(I32)
            did(v.tensor_scalar(dst, dst, float(M), None, ALU.min))
            did(v.tensor_scalar(src, src, float(M - 1), None, ALU.min))
            for b in range(COLS // XB):
                cols = slice(b * XB, (b + 1) * XB)
                v.wait_ge(ordered, n)
                v.tensor_scalar(flags[:, 0, :], dst[:, cols], float(M), float(M), ALU.is_ge, ALU.mult)
                did(v.tensor_scalar(flags[:, 1, :], src[:, cols], float(M - 1), float(M), ALU.is_ge, ALU.mult))
                for f in range(2):
                    v.wait_ge(ordered, n)
                    did(v.tensor_tensor(dst[:, cols], dst[:, cols], flags[:, f, :], ALU.add))
            v.wait_ge(ordered, n)
            did(v.tensor_scalar(dst, dst, NODE_BITS, KEY_BASE, ALU.logical_shift_left, ALU.bitwise_or))
            v.wait_ge(ordered, n)
            did(v.tensor_tensor(dst, dst, src, ALU.bitwise_or))
            rows = Rows([keys[0][:, :], keys[1][:, :]], 0, COLS)
            rows.sort(1, BW.bit_length() - 1)
            at = rows.cur
            blocks_at.extend((at, n))
            v.wait_ge(ordered, n)
            v.tensor_scalar(keys[1 - at][:, :], keys[at][:, :], CLASS_1, None, ALU.is_lt, ALU.add, accum_out=count[:, 0:1])
            did(v.tensor_reduce(lows[:, :], keys[at][:, :].rearrange("p (b q w) -> p q b w", q=NPART, w=KW)[:, :, :, 0], AXX, ALU.min))
            v.wait_ge(ordered, n)
            v.tensor_scalar(count[:, 1:2], lows[:, 1:2], CLASS_1, None, ALU.is_lt)
            v.tensor_scalar(count[:, 2:], lows[:, :], CLASS_2, None, ALU.is_lt).then_inc(counted, 1)
            v.wait_ge(summed, 1)
            did(v.tensor_copy(sums[:, :], banks[0][:, 0:2 + NPART]))
            v.wait_ge(ordered, n)
            did(v.tensor_scalar(sums[:, 1:], sums[:, 1:], 1.0, None, ALU.min))
            v.wait_ge(ordered, n)
            v.tensor_scalar(total[:, 0:1], sums[:, 0:1], 1.0, None, ALU.max)
            v.tensor_copy(total[:, 1:2], sums[:, 1:2])
            v.tensor_scalar(total[:, 2:3], sums[:, 1:2], -1.0, 1.0, ALU.mult, ALU.add)
            did(v.tensor_reduce(count[:, 0:1], sums[:, 2:], AXX, ALU.add))
            v.wait_ge(ordered, n)
            v.tensor_scalar(total[:, 3:4], count[:, 0:1], float(NBLOCK), None, ALU.mult).then_inc(known, 1)
            v.wait_ge(known, 1)

            n_known = n
            flag = [v.value_load(total[0:1, w:w + 1], min_val=0, max_val=1) for _, w in ways]
            for k, (way, _) in enumerate(ways):
                with v.If(flag[k] < 1):
                    n = n_known
                    if way is first:
                        width = NBLOCK * KW
                        free = keys[1 - at]
                        rows = Rows([free[:, 0:width], free[:, width:2 * width]], 0, width)
                        did(v.tensor_copy(rows.buf[0].rearrange("p (b w) -> p b w", w=KW), keys[at][:, :].rearrange("p (b w) -> p b w", w=BW)[:, :, 0:KW]))
                        k0 = KW.bit_length()
                    else:
                        rows, k0 = Rows([keys[0][:, :], keys[1][:, :]], at, COLS), BW.bit_length()
                        v.wait_ge(blocks_out, 16 * NPART)
                    bits = rows.width.bit_length() - 1
                    rows.flip(0)
                    rows.sort(k0, bits)
                    rows.flip(0)
                    way["turns"] = []
                    for r in range(P_BITS):
                        way["turns"].append((n, rows.buf[rows.cur]))
                        rows.take_turned(2 * r, None)
                        rows.merge_rows(r)
                        way["turns"].append((n, rows.buf[rows.cur]))
                        rows.take_turned(2 * r + 1, r + 1 if r < P_BITS - 1 else None)
                        for j in range(bits, 0, -1):
                            rows.merge(1 << j, False)
                        if r < P_BITS - 1:
                            rows.flip(r + 1)
                    way.update(sorted=n, at=rows.buf[rows.cur], width=rows.width)

        @block.tensor
        def _(pe):
            pe.wait_ge(consts_in, 32)
            pe.wait_ge(counted, 1)
            pe.matmul(banks[0][:, 0:2 + NPART], ones[:, :], count[:, :], start=True, stop=True).then_inc(summed, 1)
            pe.wait_ge(known, 1)
            flag = [pe.value_load(total[0:1, w:w + 1], min_val=0, max_val=1) for _, w in ways]
            for k, (way, _) in enumerate(ways):
                nb = way["width"] // (TB * P)
                with pe.If(flag[k] < 1):
                    for t, (n, buf) in enumerate(way["turns"]):
                        pe.wait_ge(ordered, n)
                        for b in range(nb):
                            m = min(4, nb)
                            if t * nb + b >= m:
                                pe.wait_ge(read, t * nb + b + 1 - m)
                            for x in range(TB):
                                at = (b * TB + x) * P
                                mm = pe.transpose(banks[b % 4][:, x * P:(x + 1) * P], buf[:, at:at + P], ident[:, :])
                            mm.then_inc(turned, 1)

        @block.sync
        def _(sync):
            sync.dma_start(signs[:, :], D["c_signs"]).then_inc(consts_in, 16)
            sync.dma_start(ident[:, :], D["c_ident"]).then_inc(consts_in, 16)
            sync.dma_start(keys[0][:, :].bitcast(I32), D["edges"][1].rearrange("(p c) -> p c", p=P)).then_inc(edges_in, 16)
            sync.dma_start(keys[1][:, :].bitcast(I32), D["edges"][0].rearrange("(p c) -> p c", p=P)).then_inc(edges_in, 16)
            at, n = blocks_at
            sync.wait_ge(ordered, n)
            for q in range(NPART):
                sync.dma_start(D["blocks"].rearrange("(q b p w) -> q p b w", q=NPART, b=NBLOCK, w=KW)[q],
                               keys[at][:, :].rearrange("p (b q w) -> p b q w", q=NPART, w=KW)[:, :, q, :]).then_inc(blocks_out, 16)
            sync.wait_ge(known, 1)
            sync.dma_start(D["n_edges"], total[0:1, :]).then_inc(stored, 16)
            sync.wait_ge(ends_in, 1)
            sync.dma_start(D["keys"][0:1].rearrange("(a n) -> a n", a=1), edge_of[:, 0:1]).then_inc(stored, 16)
            flag = [sync.value_load(total[0:1, w:w + 1], min_val=0, max_val=1) for _, w in ways]
            for k, (way, _) in enumerate(ways):
                size = P * way["width"]
                with sync.If(flag[k] < 1):
                    sync.dma_start(D["keys"][size + 1:size + 2].rearrange("(a n) -> a n", a=1), edge_of[:, 1:2]).then_inc(stored, 16)
                    sync.wait_ge(ordered, way["sorted"])
                    sync.dma_start(D["keys"][1:size + 1].rearrange("(p c) -> p c", p=P), way["at"]).then_inc(stored, 16)
            sync.wait_ge(stored, 64)
            sync.wait_ge(blocks_out, 16 * NPART)
NE, GH = 4, 4
GF = GH * NE
NJ = M // ST


def phase_nodes(nc, D):
    with ExitStack() as ctx:
        s_ = Space(nc, ctx, "nodes")
        sb, ps, sem, sems = s_.sb, s_.ps, s_.sem, s_.sems
        ident, w_gat = sb("ident", [P, P]), sb("w_gat", [P, CH, GF])
        att = sb("att", [P, 2, GF])
        T = [sb(f"T{u}", [P, NC_, C]) for u in range(2)]
        N = sb("N", [P, NC_, C])
        stats, mv = sb("stats", [P, NC_, 6]), sb("mv", [P, NC_, 2])
        fence = sb("fence", [P, 1])
        ve, rstd = sb("ve", [P, NC_]), sb("rstd", [P, NC_])
        XF = [sb(f"XF{u}", [P, CH, ST]) for u in range(2)]
        TF = [sb(f"TF{u}", [P, CH, ST]) for u in range(2)]
        TAB = [sb(f"TAB{u}", [P, NC_, GF + GH]) for u in range(2)]
        VT = [sb(f"VT{u}", [P, NC_, GH]) for u in range(2)]
        hs = sb("hs", [P, NC_, GF])
        prod = sb("prod", [P, 2, NC_, GF])
        kx, kt, kh = [ps(f"kx{k}", 512) for k in range(CH)], [ps(f"kt{k}", 512) for k in range(CH)], ps("kh", 512)
        consts_in, own_s = sem("consts_in"), sem("vec")
        t_in, stored = sems("t_in", 2), sems("stored", 2)
        S = {n: sem(n) for n in "ve_in sd_in n_in x_turned t_turned xf_in tf_in h_done v_in".split()}
        STEPS = 5
        block = ctx.enter_context(nc.Block())
        rows = D["t2"].rearrange("b n f -> (b n) f").rearrange("(j c p) f -> j p c f", p=P, c=NC_)

        @block.gpsimd
        def _(pool):
            with pool.Fori(0, NJ // 2) as i:
                for u in range(2):
                    pool.wait_ge(S["n_in"], i * 2 + (u + 1))
                    pool.wait_ge(S["t_turned"], i * 2 + (u + 1))
                    pool.dma_start(T[u][:, :, :], rows[i * 2 + u]).then_inc(t_in[u], 16)

        @block.sync
        def _(sync):
            sync.dma_start(ident[:, :], D["c_ident"]).then_inc(consts_in, 16)
            sync.dma_start(w_gat[:, :, :], D["w_gat"]).then_inc(consts_in, 16)
            sync.dma_start(att[:, :, :], D["att"]).then_inc(consts_in, 16)
            for u in range(2):
                sync.sem_inc(stored[u], 64)
            tabv = D["table"].rearrange("(j c p) f -> j p c f", p=P, c=NC_)
            vv = D["vtable"].rearrange("(j c p) f -> j p c f", p=P, c=NC_)
            with sync.Fori(0, NJ // 2) as i:
                for u in range(2):
                    sync.wait_ge(S["xf_in"], i * 2 + (u + 2))
                    sync.dma_start(D["x3F"][i * 2 + u].rearrange("(k p) n -> p k n", p=P), XF[u][:, :, :]).then_inc(stored[u], 16)
                    sync.wait_ge(S["tf_in"], i * 2 + (u + 2))
                    sync.dma_start(D["t2F"][i * 2 + u].rearrange("(k p) n -> p k n", p=P), TF[u][:, :, :]).then_inc(stored[u], 16)
                    sync.wait_ge(S["v_in"], i * 2 + (u + 2))
                    sync.dma_start(tabv[i * 2 + u], TAB[u][:, :, :]).then_inc(stored[u], 16)
                    sync.dma_start(vv[i * 2 + u], VT[u][:, :, :]).then_inc(stored[u], 16)
            for u in range(2):
                sync.wait_ge(stored[u], 64 * (NJ // 2 + 1))

        @block.vector
        def _(v):
            own = Steps(v, own_s)
            v.wait_ge(consts_in, 48)
            v.sem_inc(S["n_in"], 2)
            with v.Fori(0, NJ // 2) as i:
                for u in range(2):
                    own.turn(i * (2 * STEPS) + u * STEPS)
                    j1 = v.snap(i * 2 + (u + 1))
                    v.wait_ge(t_in[u], i * 16 + 16)
                    for c in range(NC_):
                        ins = v.bn_stats(stats[:, c, :], T[u][:, c, :])
                    own.did(ins)
                    own.wait()
                    v.memset(fence[:, :], 0.0)
                    for c in range(NC_):
                        ins = v.bn_aggr(mv[:, c, :], stats[:, c, :])
                    own.did(ins)
                    own.wait()
                    v.tensor_scalar(ve[:, :], mv[:, :, 1], LN_EPS, None, ALU.add).then_inc(S["ve_in"], 1)
                    v.wait_ge(S["sd_in"], j1)
                    own.did(v.reciprocal(rstd[:, :], rstd[:, :]))
                    own.wait()
                    for c in range(NC_):
                        ins = v.tensor_scalar(N[:, c, :], T[u][:, c, :], mv[:, c, 0:1], rstd[:, c:c + 1], ALU.subtract, ALU.mult)
                    ins.then_inc(S["n_in"], 1)
                    v.wait_ge(S["h_done"], j1)
                    v.wait_ge(stored[u], i * 64 + 64)
                    own.did(v.tensor_copy(hs[:, :, :], kh[:, 0:NC_ * GF].rearrange("p (c f) -> p c f", f=GF)))
                    own.wait()
                    v.tensor_copy(TAB[u][:, :, 0:GF], hs[:, :, :])
                    for a in range(2):
                        ins = v.tensor_tensor(prod[:, a, :, :], hs[:, :, :], att[:, a, :].unsqueeze(1).to_broadcast([P, NC_, GF]), ALU.mult)
                    own.did(ins)
                    own.wait()
                    v.tensor_reduce(TAB[u][:, :, GF:GF + GH], prod[:, 0, :, :].rearrange("p c (h e) -> p c h e", e=NE), AXX, ALU.add)
                    v.tensor_reduce(VT[u][:, :, :], prod[:, 1, :, :].rearrange("p c (h e) -> p c h e", e=NE), AXX, ALU.add).then_inc(S["v_in"], 1)
            assert own.k == STEPS, own.k

        @block.tensor
        def _(pe):
            pe.wait_ge(consts_in, 48)
            pe.sem_inc(S["x_turned"], 1)
            pe.sem_inc(S["t_turned"], 2)
            with pe.Fori(0, NJ // 2) as i:
                for u in range(2):
                    j0 = pe.snap(i * 2 + u + 1)
                    pe.wait_ge(t_in[u], i * 16 + 16)
                    pe.wait_ge(S["tf_in"], j0)
                    for k in range(CH):
                        for c in range(NC_):
                            mm = pe.transpose(kt[k][:, c * P:(c + 1) * P], T[u][:, c, k * P:(k + 1) * P], ident[:, :])
                    mm.then_inc(S["t_turned"], 1)
                    pe.wait_ge(S["n_in"], j0 + 2)
                    pe.wait_ge(S["xf_in"], j0)
                    for k in range(CH):
                        for c in range(NC_):
                            mm = pe.transpose(kx[k][:, c * P:(c + 1) * P], N[:, c, k * P:(k + 1) * P], ident[:, :])
                    mm.then_inc(S["x_turned"], 1)
                    pe.wait_ge(S["xf_in"], j0 + 1)
                    pe.wait_ge(S["v_in"], j0)
                    for c in range(NC_):
                        for k in range(CH):
                            mm = pe.matmul(kh[:, c * GF:(c + 1) * GF], XF[u][:, k, c * P:(c + 1) * P], w_gat[:, k, :], start=(k == 0), stop=(k == CH - 1))
                    mm.then_inc(S["h_done"], 1)

        @block.scalar
        def _(act):
            act.wait_ge(consts_in, 48)
            for n in ("xf_in", "tf_in", "v_in"):
                act.sem_inc(S[n], 1)
            with act.Fori(0, NJ // 2) as i:
                for u in range(2):
                    j1 = act.snap(i * 2 + (u + 1))
                    act.wait_ge(S["ve_in"], j1)
                    act.activation(rstd[:, :], ve[:, :], ACT.Sqrt).then_inc(S["sd_in"], 1)
                    act.wait_ge(stored[u], i * 64 + 64)
                    act.wait_ge(S["t_turned"], j1 + 2)
                    for k in range(CH):
                        ins = act.activation(TF[u][:, k, :], kt[k][:, :], ACT.Copy)
                    ins.then_inc(S["tf_in"], 1)
                    act.wait_ge(S["x_turned"], j1 + 1)
                    for k in range(CH):
                        ins = act.activation(XF[u][:, k, :], kx[k][:, :], ACT.Copy)
                    ins.then_inc(S["xf_in"], 1)
CW = 64
CS = P * CW
NCHUNK = EDGES // CS
HE = NE + 1
SUMS = GH * HE
RES = GH + SUMS
FAR = 1.0e30
DECODE_STEPS, EDGE_STEPS = 3, 21
GS = 6
GROUP_CHUNKS = -(-GROUPS // GS) + (-(-GROUPS // GS)) % 2


def phase_edges(nc, D):
    with ExitStack() as ctx:
        s_ = Space(nc, ctx, "edges")
        sb, ps, sem, sems = s_.sb, s_.ps, s_.sem, s_.sems
        ident = sb("ident", [P, P])
        n_edges = sb("n_edges", [1, 4], I32)
        K = [[sb(f"K{u}_{w}", [P, CW], U32) for w in range(3)] for u in range(2)]
        dst = [sb(f"dst{w}", [P, CW], U32) for w in range(3)]
        src_i = [sb(f"src_i{u}", [P, CW], U32) for u in range(2)]
        dst_i = [sb(f"dst_i{u}", [P, CW], U32) for u in range(2)]
        end_i = [sb(f"end_i{u}", [P, CW], U32) for u in range(2)]
        cont, pen, whole = ([sb(f"{n}{u}", [P, w]) for u in range(2)] for n, w in (("cont", CW), ("pen", CW), ("whole", 1)))
        more = sb("more", [P, CW])
        G = [sb(f"G{u}", [P, CW, GF + GH]) for u in range(2)]
        V = [sb(f"V{u}", [P, CW, GH]) for u in range(2)]
        R = [sb(f"R{u}", [P, CW + 1, RES]) for u in range(2)]
        z, e = sb("z", [P, GH, CW]), sb("e", [P, GH, CW])
        ab = sb("ab", [P, 2, GH, CW])
        W = sb("W", [P, GH, HE, CW])
        rows = sb("rows", [P, 4, SUMS])
        RT = sb("RT", [SUMS, 4, P])
        cpen = sb("cpen", [SUMS, 2, P])
        EM, ES = sb("EM", [SUMS, P + 1]), sb("ES", [SUMS, P + 1])
        cab, cW = sb("cab", [SUMS, 2, P]), sb("cW", [SUMS, P])
        start = sb("start", [SUMS, 2, P])
        empty = sb("empty", [P, P, RES])
        lanes, zeros = sb("lanes", [P, P]), sb("zeros", [P, P], BF16)
        CK = [sb(f"CK{u}", [P, CW], U32) for u in range(2)]
        bits = [sb(f"bits{u}", [P, 2, CW], U32) for u in range(2)]
        digits = [sb(f"digits{u}", [P, 2, CW]) for u in range(2)]
        hot = [sb(f"hot{u}", [P, 2, CW, P], BF16) for u in range(2)]
        counts = sb("counts", [P, P])
        k_counts = ps("k_counts", 512)
        ck_in, bits_in, digits_in, hot_in = sems("ck_in", 2), sem("bits_in"), sem("digits_in"), sem("hot_in")
        hot_read, all_counted, counts_in, counts_out = sem("hot_read"), sem("all_counted"), sem("counts_in"), sem("counts_out")
        k_rows, k_start = ps("k_rows", 512), ps("k_start", 512)
        consts, own_s, decode_s = sem("consts"), sem("vec"), sem("decode")
        k_in, gathered, scattered = sems("k_in", 2), sems("gathered", 2), sems("scattered", 2)
        S = {n: sem(n) for n in "idx_in g_read ab1 ab1e rows_in rows_turned cab_in cabe start_in start_turned ab2 ab2e r_in landed went".split()}
        block = ctx.enter_context(nc.Block())
        keys = D["keys"].bitcast(U32)

        def run(eng, begin, this, ahead, group):
            eng.wait_ge(consts, 48)
            n = eng.value_load(n_edges[0:1, 0:1], min_val=1, max_val=EDGES)
            groups = eng.value_load(n_edges[0:1, 3:4], min_val=0, max_val=GROUPS) if group else None
            begin()

            def chunk(i, u, with_groups):
                with eng.If(i * (2 * CS) + u * CS < n):
                    if ahead:
                        with eng.If(i * (2 * CS) + (u + 1) * CS < n):
                            ahead(i + u, 1 - u)
                    if this:
                        this(i, u)
                if with_groups:
                    for x in range(GS):
                        g = u * GS + x
                        with eng.If(i * (2 * GS) + g < groups):
                            group(i * GS + g // 2, g % 2)

            with eng.Fori(0, GROUP_CHUNKS // 2) as i:
                for u in range(2):
                    chunk(i, u, group is not None)
            with eng.Fori(GROUP_CHUNKS // 2, NCHUNK // 2) as i:
                for u in range(2):
                    chunk(i, u, False)

        @block.sync
        def _(sync):
            sync.dma_start(ident[:, :], D["c_ident"]).then_inc(consts, 16)
            sync.dma_start(n_edges[:, :], D["n_edges"]).then_inc(consts, 16)
            sync.dma_start(lanes[:, :], D["c_lanes"]).then_inc(consts, 16)

            def load(i, u):
                at = [sync.snap(i * (2 * CS) + (u * CS + w)) if type(i) is not int else i * (2 * CS) + u * CS + w for w in range(3)]
                sync.wait_ge(S["idx_in"], i * 2 + (u + 1))
                sync.sem_inc(S["went"], 1)
                for w in range(3):
                    sync.dma_start(K[u][w][:, :], keys[bass.ds(at[w], CS)].rearrange("(p c) -> p c", p=P)).then_inc(k_in[u], 16)

            def load_group(j, u):
                sync.wait_ge(bits_in, j * 2 + (u + 1))
                at = nc.s_assert_within(sync.snap(j * 2 + u), 0, GROUPS - 1, skip_runtime_bounds_check_because="the groups that are live are below GROUPS")
                sync.sem_inc(S["went"], 1)
                sync.dma_start(CK[u][:, :], D["blocks"].bitcast(U32).rearrange("(g p w) -> g p w", p=P, w=KW)[at]).then_inc(ck_in[u], 16)

            def ahead(i, u):
                load(nc.s_assert_within(sync.snap(i), 0, NCHUNK // 2 - 1, skip_runtime_bounds_check_because="the chunk holds an edge"), u)
            run(sync, lambda: load(0, 0), None, ahead, load_group)
            sync.wait_ge(counts_in, 1)
            sync.dma_start(D["counts"].rearrange("(p q) -> p q", p=P), counts[:, :]).then_inc(counts_out, 16)
            sync.wait_ge(counts_out, 16)

        @block.gpsimd
        def _(pool):
            def begin():
                pool.sem_inc(S["landed"], 2)
                pool.memset(empty[:, :, :], 0.0).then_inc(S["r_in"], 1)
                pool.wait_ge(S["r_in"], 1)
                pool.memset(empty[:, :, 0:GH], -FAR).then_inc(S["r_in"], 1)
                pool.wait_ge(S["r_in"], 2)
                pool.dma_start(D["result"].rearrange("(p q) f -> p q f", p=P), empty[:, :, :]).then_inc(scattered[0], 16)
                gather(0, 0)
                pool.wait_ge(scattered[0], 16)

            def gather(i, u):
                pool.wait_ge(S["idx_in"], i * 2 + (u + 3))
                pool.wait_ge(S["g_read"], i * 2 + (u + 1))
                pool.sem_inc(S["went"], 1)
                for c in range(CW):
                    pool.indirect_dma_start(G[u][:, c, :], None, D["table"], bass.IndirectOffsetOnAxis(ap=src_i[u][:, c:c + 1], axis=0),
                                            bounds_check=M - 1, oob_is_err=False).then_inc(gathered[u], 16)
                    pool.indirect_dma_start(V[u][:, c, :], None, D["vtable"], bass.IndirectOffsetOnAxis(ap=dst_i[u][:, c:c + 1], axis=0),
                                            bounds_check=M - 1, oob_is_err=False).then_inc(gathered[u], 16)

            def scatter(i, u):
                pool.wait_ge(S["r_in"], i * 2 + (u + 3))
                pool.sem_inc(S["went"], 1)
                for c in range(CW):
                    pool.indirect_dma_start(D["result"], bass.IndirectOffsetOnAxis(ap=end_i[u][:, c:c + 1], axis=0), R[u][:, c + 1, :], None,
                                            bounds_check=M - 1, oob_is_err=False).then_inc(scattered[u], 16)
                pool.wait_ge(scattered[u], i * (16 * CW) + (16 * CW + (16 if u == 0 else 0)))
                pool.sem_inc(S["landed"], 1)
            run(pool, begin, scatter, gather, None)

        @block.vector
        def _(v):
            own, decoded = Steps(v, own_s), Steps(v, decode_s)

            def begin():
                v.memset(zeros[:, :], 0.0).then_inc(consts, 1)
                v.sem_inc(S["idx_in"], 2)
                v.sem_inc(S["g_read"], 2)
                v.sem_inc(bits_in, 2)
                v.memset(EM[:, P:P + 1], -FAR)
                own.did(v.memset(ES[:, P:P + 1], 0.0))
                own.wait()
                decode(0, 0)

            def decode(i, u):
                decoded.turn(i * (2 * DECODE_STEPS) + u * DECODE_STEPS)
                v.wait_ge(k_in[u], i * 48 + 48)
                v.wait_ge(S["landed"], i * 2 + (u + 1))
                v.wait_ge(S["idx_in"], i * 2 + (u + 2))
                for w in range(3):
                    v.tensor_scalar(dst[w][:, :], K[u][w][:, :], NODE_BITS, 4 * M - 1, ALU.logical_shift_right, ALU.bitwise_and)
                decoded.did(v.tensor_scalar(src_i[u][:, :], K[u][1][:, :], M - 1, None, ALU.bitwise_and))
                decoded.wait()
                v.tensor_scalar(dst_i[u][:, :], dst[1][:, :], float(M - 1), None, ALU.min)
                v.tensor_tensor(cont[u][:, :], dst[0][:, :], dst[1][:, :], ALU.is_equal)
                v.tensor_tensor(whole[u][:, :], dst[1][:, 0:1], dst[1][:, CW - 1:CW], ALU.is_equal)
                decoded.did(v.tensor_tensor(more[:, :], dst[2][:, :], dst[1][:, :], ALU.is_equal))
                decoded.wait()
                decoded.did(v.tensor_scalar(pen[u][:, :], cont[u][:, :], 1.0, FAR, ALU.subtract, ALU.mult))
                v.scalar_tensor_tensor(end_i[u][:, :], more[:, :], float(4 * M), dst[1][:, :], ALU.mult, ALU.add).then_inc(S["idx_in"], 1)

            def count_group(j, u):
                n1 = v.snap(j * 2 + (u + 1))
                v.wait_ge(ck_in[u], j * 16 + 16)
                v.tensor_scalar(bits[u][:, 0, :], CK[u][:, :], NODE_BITS + P_BITS, 4 * P - 1, ALU.logical_shift_right, ALU.bitwise_and)
                v.tensor_scalar(bits[u][:, 1, :], CK[u][:, :], NODE_BITS, P - 1, ALU.logical_shift_right, ALU.bitwise_and).then_inc(bits_in, 1)
                v.wait_ge(bits_in, n1 + 2)
                v.tensor_scalar(digits[u][:, 0, :], bits[u][:, 0, :], float(P), None, ALU.subtract)
                v.tensor_scalar(digits[u][:, 1, :], bits[u][:, 1, :], 0.0, None, ALU.add).then_inc(digits_in, 1)
                v.wait_ge(digits_in, n1)
                v.wait_ge(hot_read, n1)
                v.tensor_tensor(hot[u][:, :, :, :].rearrange("p a c n -> p (a c) n"), lanes[:, :].unsqueeze(1).to_broadcast([P, 2 * CW, P]),
                                digits[u][:, :, :].rearrange("p a c -> p (a c)").unsqueeze(2).to_broadcast([P, 2 * CW, P]), ALU.is_equal).then_inc(hot_in, 1)

            def body(i, u):
                own.turn(i * (2 * EDGE_STEPS) + (u * EDGE_STEPS + 1))
                n1 = v.snap(i * 2 + (u + 1))
                decoded.turn(i * (2 * DECODE_STEPS) + u * DECODE_STEPS)
                decoded.k = DECODE_STEPS
                decoded.wait()
                v.wait_ge(gathered[u], i * (32 * CW) + 32 * CW)
                own.did(v.tensor_tensor(z[:, :, :], G[u][:, :, GF:GF + GH].rearrange("p c h -> p h c"), V[u][:, :, :].rearrange("p c h -> p h c"), ALU.add))
                own.wait()
                own.did(v.scalar_tensor_tensor(e[:, :, :], z[:, :, :], 0.2, z[:, :, :], ALU.mult, ALU.max))
                r = R[u]
                maxima = r[:, :, 0:GH].rearrange("p c h -> p h c")

                def scans(first, name):
                    own.wait()
                    for h in range(GH):
                        ins = v.tensor_tensor_scan(r[:, 1:, h], pen[u][:, :], e[:, h, :], r[:, 0, h:h + 1], ALU.add, ALU.max)
                    own.did(ins)
                    own.wait()
                    own.did(v.tensor_tensor(z[:, :, :], maxima[:, :, 0:CW], pen[u][:, :].unsqueeze(1).to_broadcast([P, GH, CW]), ALU.add))
                    own.wait()
                    v.tensor_tensor(ab[:, 0, :, :], z[:, :, :], maxima[:, :, 1:], ALU.subtract)
                    v.tensor_tensor(ab[:, 1, :, :], e[:, :, :], maxima[:, :, 1:], ALU.subtract).then_inc(S[name], 1)
                    v.wait_ge(S[name + "e"], n1)
                    for h in range(GH):
                        v.tensor_copy(W[:, h, 0, :], ab[:, 1, h, :])
                        ins = v.tensor_tensor(W[:, h, 1:, :], G[u][:, :, h * NE:(h + 1) * NE].rearrange("p c k -> p k c"),
                                              ab[:, 1, h, :].unsqueeze(1).to_broadcast([P, NE, CW]), ALU.mult)
                    own.did(ins)
                    own.wait()
                    for h in range(GH):
                        for k in range(HE):
                            f = GH + h * HE + k
                            ins = v.tensor_tensor_scan(r[:, 1:, f], ab[:, 0, h, :], W[:, h, k, :], r[:, 0, f:f + 1], ALU.mult, ALU.add)
                    return ins

                v.memset(r[:, 0, 0:GH], -FAR)
                own.did(v.memset(r[:, 0, GH:], 0.0))
                own.did(scans(True, "ab1"))
                own.wait()
                v.tensor_copy(rows[:, 0, :].rearrange("p (h k) -> p h k", k=HE), r[:, CW, 0:GH].unsqueeze(2).to_broadcast([P, GH, HE]))
                v.tensor_copy(rows[:, 1, :], r[:, CW, GH:])
                own.did(v.tensor_copy(rows[:, 3, :], cont[u][:, 0:1].to_broadcast([P, SUMS])))
                own.wait()
                v.tensor_tensor(rows[:, 2, :], rows[:, 3, :], whole[u][:, :].to_broadcast([P, SUMS]), ALU.mult).then_inc(S["rows_in"], 1)
                v.tensor_copy(EM[:, 0:1], EM[:, P:P + 1])
                own.did(v.tensor_copy(ES[:, 0:1], ES[:, P:P + 1]))
                v.wait_ge(S["rows_turned"], n1)
                own.did(v.tensor_copy(RT[:, :, :], k_rows[0:SUMS, :].rearrange("p (a b) -> p a b", a=4)))
                own.wait()
                own.did(v.tensor_scalar(cpen[:, :, :], RT[:, 2:4, :], 1.0, FAR, ALU.subtract, ALU.mult))
                own.wait()
                own.did(v.tensor_tensor_scan(EM[:, 1:], cpen[:, 0, :], RT[:, 0, :], EM[:, 0:1], ALU.add, ALU.max))
                own.wait()
                own.did(v.tensor_tensor(cab[:, 0, :], EM[:, 0:P], cpen[:, 0, :], ALU.add))
                own.wait()
                own.did(v.tensor_tensor(cab[:, 0, :], cab[:, 0, :], EM[:, 1:], ALU.subtract))
                v.tensor_tensor(cab[:, 1, :], RT[:, 0, :], EM[:, 1:], ALU.subtract).then_inc(S["cab_in"], 1)
                own.did(v.tensor_tensor(start[:, 0, :], EM[:, 0:P], cpen[:, 1, :], ALU.add))
                v.wait_ge(S["cabe"], n1)
                own.did(v.tensor_tensor(cW[:, :], RT[:, 1, :], cab[:, 1, :], ALU.mult))
                own.wait()
                own.did(v.tensor_tensor_scan(ES[:, 1:], cab[:, 0, :], cW[:, :], ES[:, 0:1], ALU.mult, ALU.add))
                own.wait()
                v.tensor_tensor(start[:, 1, :], ES[:, 0:P], RT[:, 3, :], ALU.mult).then_inc(S["start_in"], 1)
                v.wait_ge(S["start_turned"], n1)
                v.tensor_copy(r[:, 0, 0:GH], k_start[:, 0:SUMS].rearrange("p (h k) -> p h k", k=HE)[:, :, 0])
                own.did(v.tensor_copy(r[:, 0, GH:], k_start[:, 32:32 + SUMS]))
                scans(False, "ab2").then_inc(S["r_in"], 1)
                v.wait_ge(S["r_in"], n1 + 2)
                v.memset(z[:, 0, 0:1], 0.0).then_inc(S["g_read"], 1)
            run(v, begin, body, decode, count_group)
            assert own.k == EDGE_STEPS and decoded.k == DECODE_STEPS
            v.wait_ge(all_counted, 1)
            v.tensor_copy(counts[:, :], k_counts[:, 0:P]).then_inc(counts_in, 1)

        @block.tensor
        def _(pe):
            def body(i, u):
                n1 = pe.snap(i * 2 + (u + 1))
                pe.wait_ge(S["rows_in"], n1)
                for a in range(4):
                    mm = pe.transpose(k_rows[0:SUMS, a * P:(a + 1) * P], rows[:, a, :], ident[:, :])
                mm.then_inc(S["rows_turned"], 1)
                pe.wait_ge(S["start_in"], n1)
                pe.matmul(k_start[:, 511:512], ident[:, :], ident[:, 0:1], start=True, stop=True)
                for a in range(2):
                    mm = pe.transpose(k_start[:, a * 32:a * 32 + SUMS], start[:, a, :], ident[0:SUMS, 0:SUMS])
                mm.then_inc(S["start_turned"], 1)

            def begin():
                pe.wait_ge(consts, 49)
                pe.sem_inc(hot_read, 2)
                pe.matmul(k_counts[:, 0:P], zeros[:, :], zeros[:, :], start=True, stop=False)

            def count_group(j, u):
                pe.wait_ge(hot_in, j * 2 + (u + 1))
                for c in range(CW):
                    mm = pe.matmul(k_counts[:, 0:P], hot[u][:, 0, c, :], hot[u][:, 1, c, :], start=False, stop=False)
                mm.then_inc(hot_read, 1)
            run(pe, begin, body, None, count_group)
            pe.matmul(k_counts[:, 0:P], zeros[:, :], zeros[:, :], start=False, stop=True).then_inc(all_counted, 1)

        @block.scalar
        def _(act):
            def body(i, u):
                n1 = act.snap(i * 2 + (u + 1))
                act.wait_ge(S["ab1"], n1)
                act.activation(ab[:, :, :, :], ab[:, :, :, :], ACT.Exp).then_inc(S["ab1e"], 1)
                act.wait_ge(S["cab_in"], n1)
                act.activation(cab[:, :, :], cab[:, :, :], ACT.Exp).then_inc(S["cabe"], 1)
                act.wait_ge(S["ab2"], n1)
                act.activation(ab[:, :, :, :], ab[:, :, :, :], ACT.Exp).then_inc(S["ab2e"], 1)
            run(act, lambda: None, body, None, None)
NQ = M // P


def phase_gates(nc, D):
    with ExitStack() as ctx:
        s_ = Space(nc, ctx, "gates")
        sb, sem = s_.sb, s_.sem
        R, T, V = sb("R", [P, NQ, RES]), sb("T", [P, NQ, GF + GH]), sb("V", [P, NQ, GH])
        b_gat, ln_g, ln_b = sb("b_gat", [P, GF]), sb("ln_g", [P, GF]), sb("ln_b", [P, GF])
        z, es, ec = sb("z", [P, NQ, GH]), sb("es", [P, NQ, GH]), sb("ec", [P, NQ, GH])
        N, none = sb("N", [P, NQ]), sb("none", [P, NQ])
        last = sb("last", [P, GF + GH])
        w3 = sb("w3", [P, 3, NQ, GH])
        den, num, tmp = sb("den", [P, NQ, GH]), sb("num", [P, NQ, GF]), sb("tmp", [P, NQ, GF])
        mean, var = sb("mean", [P, NQ]), sb("var", [P, NQ])
        score, rank, cmp = sb("score", [P, NE, NQ]), sb("rank", [P, NE, NQ]), sb("cmp", [P, NQ])
        top, gate, total = sb("top", [P, NQ]), sb("gate", [P, NE, NQ]), sb("total", [P, NQ])
        ins_in, out_in = sem("ins_in"), sem("out_in")
        step, exp1_in, exp1, var_in, sd_in, exp2_in, exp2, gates_in = (sem(n) for n in "step exp1_in exp1 var_in sd_in exp2_in exp2 gates_in".split())
        block = ctx.enter_context(nc.Block())

        @block.sync
        def _(sync):
            sync.dma_start(R[:, :, :], D["result"].rearrange("(p q) f -> p q f", p=P)).then_inc(ins_in, 16)
            sync.dma_start(T[:, :, :], D["table"].rearrange("(p q) f -> p q f", p=P)).then_inc(ins_in, 16)
            sync.dma_start(V[:, :, :], D["vtable"].rearrange("(p q) f -> p q f", p=P)).then_inc(ins_in, 16)
            sync.dma_start(N[:, :], D["counts"].rearrange("(p q) -> p q", p=P)).then_inc(ins_in, 16)
            sync.dma_start(last[:, :], D["table"][M - 1:M, :].to_broadcast([P, GF + GH])).then_inc(ins_in, 16)
            for dst, name in ((b_gat, "b_gat"), (ln_g, "ln_g"), (ln_b, "ln_b")):
                sync.dma_start(dst[:, :], D[name]).then_inc(ins_in, 16)
            sync.wait_ge(gates_in, 1)
            sync.dma_start(D["gates"].rearrange("e (p q) -> p e q", p=P), gate[:, :, :]).then_inc(out_in, 16)
            sync.wait_ge(out_in, 16)

        @block.vector
        def _(v):
            own = Steps(v, step)

            def do(ins):
                own.did(ins)
                own.wait()

            def wide(x, k=GF):
                return x.unsqueeze(2).to_broadcast([P, NQ, k])

            def per_feature(x):
                return x.unsqueeze(1).to_broadcast([P, NQ, GF])

            v.wait_ge(ins_in, 128)
            do(v.tensor_tensor(z[:, :, :], T[:, :, GF:], V[:, :, :], ALU.add))
            do(v.scalar_tensor_tensor(es[:, :, :], z[:, :, :], 0.2, z[:, :, :], ALU.mult, ALU.max))
            do(v.tensor_tensor(z[:, :, :], V[:, :, :], last[:, GF:].unsqueeze(1).to_broadcast([P, NQ, GH]), ALU.add))
            do(v.scalar_tensor_tensor(ec[:, :, :], z[:, :, :], 0.2, z[:, :, :], ALU.mult, ALU.max))
            do(v.tensor_scalar(none[:, :], N[:, :], 0.0, -FAR, ALU.is_equal, ALU.mult))
            do(v.tensor_tensor(ec[:, :, :], ec[:, :, :], wide(none[:, :], GH), ALU.add))
            do(v.tensor_tensor(z[:, :, :], es[:, :, :], R[:, :, 0:GH], ALU.max))
            do(v.tensor_tensor(z[:, :, :], z[:, :, :], ec[:, :, :], ALU.max))
            v.tensor_tensor(w3[:, 0, :, :], R[:, :, 0:GH], z[:, :, :], ALU.subtract)
            v.tensor_tensor(w3[:, 2, :, :], ec[:, :, :], z[:, :, :], ALU.subtract)
            v.tensor_tensor(w3[:, 1, :, :], es[:, :, :], z[:, :, :], ALU.subtract).then_inc(exp1_in, 1)
            v.wait_ge(exp1, 1)
            do(v.tensor_tensor(w3[:, 2, :, :], w3[:, 2, :, :], wide(N[:, :], GH), ALU.mult))
            sums = R[:, :, GH:].rearrange("p q (h k) -> p q h k", k=HE)
            do(v.tensor_tensor(den[:, :, :], sums[:, :, :, 0], w3[:, 0, :, :], ALU.mult))
            do(v.tensor_tensor(den[:, :, :], den[:, :, :], w3[:, 1, :, :], ALU.add))
            do(v.tensor_tensor(den[:, :, :], den[:, :, :], w3[:, 2, :, :], ALU.add))
            do(v.tensor_scalar(den[:, :, :], den[:, :, :], 1e-16, None, ALU.add))
            do(v.reciprocal(den[:, :, :], den[:, :, :]))
            for h in range(GH):
                f = slice(h * NE, (h + 1) * NE)
                v.tensor_tensor(num[:, :, f], sums[:, :, h, 1:], wide(w3[:, 0, :, h], NE), ALU.mult)
                ins = v.tensor_tensor(tmp[:, :, f], T[:, :, f], wide(w3[:, 1, :, h], NE), ALU.mult)
            do(ins)
            do(v.tensor_tensor(num[:, :, :], num[:, :, :], tmp[:, :, :], ALU.add))
            for h in range(GH):
                f = slice(h * NE, (h + 1) * NE)
                ins = v.tensor_tensor(tmp[:, :, f], last[:, f].unsqueeze(1).to_broadcast([P, NQ, NE]), wide(w3[:, 2, :, h], NE), ALU.mult)
            do(ins)
            do(v.tensor_tensor(num[:, :, :], num[:, :, :], tmp[:, :, :], ALU.add))
            for h in range(GH):
                f = slice(h * NE, (h + 1) * NE)
                ins = v.tensor_tensor(num[:, :, f], num[:, :, f], wide(den[:, :, h], NE), ALU.mult)
            do(ins)
            do(v.tensor_tensor(num[:, :, :], num[:, :, :], per_feature(b_gat[:, :]), ALU.add))
            do(v.tensor_reduce(mean[:, :], num[:, :, :], AXX, ALU.add))
            do(v.tensor_scalar(mean[:, :], mean[:, :], 1.0 / GF, None, ALU.mult))
            do(v.tensor_tensor(num[:, :, :], num[:, :, :], wide(mean[:, :]), ALU.subtract))
            do(v.tensor_tensor(tmp[:, :, :], num[:, :, :], num[:, :, :], ALU.mult))
            do(v.tensor_reduce(var[:, :], tmp[:, :, :], AXX, ALU.add))
            v.tensor_scalar(var[:, :], var[:, :], 1.0 / GF, LN_EPS, ALU.mult, ALU.add).then_inc(var_in, 1)
            v.wait_ge(sd_in, 1)
            do(v.reciprocal(var[:, :], var[:, :]))
            do(v.tensor_tensor(num[:, :, :], num[:, :, :], wide(var[:, :]), ALU.mult))
            do(v.tensor_tensor(num[:, :, :], num[:, :, :], per_feature(ln_g[:, :]), ALU.mult))
            do(v.tensor_tensor(num[:, :, :], num[:, :, :], per_feature(ln_b[:, :]), ALU.add))
            for k in range(NE):
                ins = v.tensor_reduce(score[:, k, :], num[:, :, k::NE], AXX, ALU.add)
            do(ins)
            do(v.tensor_scalar(score[:, :, :], score[:, :, :], 1.0 / GH, None, ALU.mult))
            v.memset(rank[:, :, :], 0.0)
            do(v.tensor_tensor(top[:, :], score[:, 0, :], score[:, 1, :], ALU.max))
            for k in range(2, NE):
                do(v.tensor_tensor(top[:, :], top[:, :], score[:, k, :], ALU.max))
            for k in range(NE):
                for j in range(NE):
                    if j != k:
                        do(v.tensor_tensor(cmp[:, :], score[:, j, :], score[:, k, :], ALU.is_ge if j < k else ALU.is_gt))
                        do(v.tensor_tensor(rank[:, k, :], rank[:, k, :], cmp[:, :], ALU.add))
            do(v.tensor_scalar(rank[:, :, :], rank[:, :, :], 2.0, None, ALU.is_lt))
            v.tensor_tensor(gate[:, :, :], score[:, :, :], top[:, :].unsqueeze(1).to_broadcast([P, NE, NQ]), ALU.subtract).then_inc(exp2_in, 1)
            v.wait_ge(exp2, 1)
            do(v.tensor_tensor(gate[:, :, :], gate[:, :, :], rank[:, :, :], ALU.mult))
            do(v.tensor_reduce(total[:, :], gate[:, :, :].rearrange("p e q -> p q e"), AXX, ALU.add))
            do(v.reciprocal(total[:, :], total[:, :]))
            v.tensor_tensor(gate[:, :, :], gate[:, :, :], total[:, :].unsqueeze(1).to_broadcast([P, NE, NQ]), ALU.mult).then_inc(gates_in, 1)

        @block.scalar
        def _(act):
            act.wait_ge(exp1_in, 1)
            act.activation(w3[:, :, :, :], w3[:, :, :, :], ACT.Exp).then_inc(exp1, 1)
            act.wait_ge(var_in, 1)
            act.activation(var[:, :], var[:, :], ACT.Sqrt).then_inc(sd_in, 1)
            act.wait_ge(exp2_in, 1)
            act.activation(gate[:, :, :], gate[:, :, :], ACT.Exp).then_inc(exp2, 1)


HF = 2 * C
FT = HF // P


def phase_experts(nc, D):
    with ExitStack() as ctx:
        s_ = Space(nc, ctx, "moe")
        sb, ps, sem, sems = s_.sb, s_.ps, s_.sem, s_.sems
        w1, b1 = sb("w1", [P, NE, CH, HF]), sb("b1", [P, NE, FT])
        w2, b2 = sb("w2", [P, NE, FT, C]), sb("b2", [NE, C])
        pick = sb("pick", [NE, NE, P])
        loads = [(w1, "moe1"), (b1, "moe1_b"), (w2, "moe2"), (b2, "moe2_b"), (pick, "c_pick")]
        X = [sb(f"X{u}", [P, CH, ST]) for u in range(2)]
        T = [sb(f"T{u}", [P, CH, ST]) for u in range(2)]
        g = [sb(f"g{u}", [NE, ST]) for u in range(2)]
        gb = [sb(f"gb{u}", [P, ST]) for u in range(2)]
        H = [sb(f"H{u}", [P, FT, ST]) for u in range(2)]
        O = [sb(f"O{u}", [P, CH, ST]) for u in range(2)]
        k_h = [ps(f"k_h{k}", 512) for k in range(4)]
        k_g = [ps(f"k_g{k}", 512) for k in range(2)]
        k_o = [ps(f"k_o{k}", 512) for k in range(CH)]
        weights_in = sem("weights_in")
        x_in, stored = sems("x_in", 2), sems("stored", 2)
        S = {n: sem(n) for n in "gb_done gb_in h_done gelu_in hg_in o_done o_in".split()}
        per = dict(gb_done=NE, gb_in=NE, h_done=NE * FT, gelu_in=NE * FT, hg_in=NE * FT, o_done=CH, o_in=CH)
        block = ctx.enter_context(nc.Block())

        def start(eng, names):
            for n in names.split():
                eng.sem_inc(S[n], 2 * per[n])

        @block.gpsimd
        def _(pool):
            with pool.Fori(0, NJ // 2) as i:
                for u in range(2):
                    pool.wait_ge(S["o_in"], (i * 2 + (u + 1)) * CH)
                    pool.dma_start(X[u][:, :, :], D["x3F"][i * 2 + u].rearrange("(k p) n -> p k n", p=P)).then_inc(x_in[u], 16)
                    pool.dma_start(T[u][:, :, :], D["t2F"][i * 2 + u].rearrange("(k p) n -> p k n", p=P)).then_inc(x_in[u], 16)
                    pool.dma_start(g[u][:, :], D["gates"].rearrange("e (j n) -> j e n", n=ST)[i * 2 + u]).then_inc(x_in[u], 16)

        @block.sync
        def _(sync):
            for dst, name in loads:
                sync.dma_start(dst[tuple(slice(None) for _ in dst.shape)], D[name]).then_inc(weights_in, 16)
            for u in range(2):
                sync.sem_inc(stored[u], 16)
            with sync.Fori(0, NJ // 2) as i:
                for u in range(2):
                    sync.wait_ge(S["o_in"], (i * 2 + (u + 3)) * CH)
                    sync.dma_start(D["out"][i].rearrange("(k p) n -> p k n", p=P)[:, :, u * ST:(u + 1) * ST], O[u][:, :, :]).then_inc(stored[u], 16)
            for u in range(2):
                sync.wait_ge(stored[u], 16 * (NJ // 2 + 1))

        @block.tensor
        def _(pe):
            pe.wait_ge(weights_in, 16 * len(loads))
            start(pe, "gb_done h_done o_done")
            with pe.Fori(0, NJ // 2) as i:
                for u in range(2):
                    j = pe.snap(i * 2 + (u + 2))
                    jg, jh, jo = pe.snap(j * NE), pe.snap(j * NE * FT), pe.snap(j * CH)
                    pe.wait_ge(x_in[u], i * 48 + 48)

                    def second(e):
                        for f in range(FT):
                            pe.wait_ge(S["hg_in"], jh + (e * FT + f + 1))
                            if e == 0 and f == 0:
                                pe.wait_ge(S["o_in"], jo)
                            for o in range(CH):
                                mm = pe.matmul(k_o[o][:, :], w2[:, e, f, o * P:(o + 1) * P], H[e % 2][:, f, :], start=(e == 0 and f == 0), stop=False)
                        return mm

                    for e in range(NE):
                        pe.wait_ge(S["gb_in"], jg + (e - 1))
                        pe.matmul(k_g[e % 2][:, :], pick[:, e, :], g[u][:, :], start=True, stop=True).then_inc(S["gb_done"], 1)
                        for f in range(FT):
                            n = e * FT + f
                            pe.wait_ge(S["gelu_in"], jh + (n - 3))
                            for k in range(CH):
                                mm = pe.matmul(k_h[n % 4][:, :], w1[:, e, k, f * P:(f + 1) * P], X[u][:, k, :], start=(k == 0), stop=(k == CH - 1))
                            mm.then_inc(S["h_done"], 1)
                        if e:
                            second(e - 1)
                    second(NE - 1)
                    for o in range(CH):
                        pe.matmul(k_o[o][:, :], b2[:, o * P:(o + 1) * P], g[u][:, :], start=False, stop=True).then_inc(S["o_done"], 1)

        @block.scalar
        def _(act):
            act.wait_ge(weights_in, 16 * len(loads))
            start(act, "gelu_in")
            with act.Fori(0, NJ // 2) as i:
                for u in range(2):
                    j = act.snap(i * 2 + (u + 2))
                    jh, jo = act.snap(j * NE * FT), act.snap(j * CH)
                    for e in range(NE):
                        for f in range(FT):
                            n = e * FT + f
                            act.wait_ge(S["h_done"], jh + (n + 1))
                            act.activation(H[e % 2][:, f, :], k_h[n % 4][:, :], ACT.Gelu, bias=b1[:, e, f:f + 1]).then_inc(S["gelu_in"], 1)

        @block.vector
        def _(v):
            v.wait_ge(weights_in, 16 * len(loads))
            start(v, "gb_in hg_in o_in")
            with v.Fori(0, NJ // 2) as i:
                for u in range(2):
                    j = v.snap(i * 2 + (u + 2))
                    jg, jh, jo = v.snap(j * NE), v.snap(j * NE * FT), v.snap(j * CH)
                    for e in range(NE):
                        v.wait_ge(S["gb_done"], jg + (e + 1))
                        v.tensor_copy(gb[e % 2][:, :], k_g[e % 2][:, :]).then_inc(S["gb_in"], 1)
                        for f in range(FT):
                            n = e * FT + f
                            v.wait_ge(S["gelu_in"], jh + (n + 1))
                            if f == 0:
                                v.wait_ge(S["gb_in"], jg + (e + 1))
                            v.tensor_tensor(H[e % 2][:, f, :], H[e % 2][:, f, :], gb[e % 2][:, :], ALU.mult).then_inc(S["hg_in"], 1)
                    v.wait_ge(stored[u], i * 16 + 16)
                    for o in range(CH):
                        v.wait_ge(S["o_done"], jo + (o + 1))
                        v.tensor_tensor(O[u][:, o, :], k_o[o][:, :], T[u][:, o, :], ALU.add).then_inc(S["o_in"], 1)


def build_program(nc, D):
    for name, shape, dt in (("t1", (B, C, HW), F32), ("t2", (B, HW, C), F32),
                            ("keys", (EDGES + 2,), F32), ("n_edges", (1, 4), I32), ("blocks", (EDGES,), F32),
                            ("x3F", (NJ, C, ST), F32), ("t2F", (NJ, C, ST), F32),
                            ("table", (M, GF + GH), F32), ("vtable", (M, GH), F32),
                            ("counts", (M,), F32), ("result", (M, RES), F32), ("gates", (NE, M), F32)):
        D[name] = nc.dram_tensor(name, shape, dt, kind="Internal").ap()
    phase_conv(nc, D)
    phase_ssm(nc, D)
    phase_sort(nc, D)
    phase_nodes(nc, D)
    phase_edges(nc, D)
    phase_gates(nc, D)
    phase_experts(nc, D)


def kernel(x, L0_conv_fc1_w, L0_conv_fc1_b, L0_conv_fc2_w, L0_conv_fc2_b, L0_conv_qkv_w, L0_conv_qkv_b,
           L0_conv_proj_w, L0_conv_proj_b, L0_conv_ffn1_w, L0_conv_ffn1_b, L0_conv_ffn2_w, L0_conv_ffn2_b,
           L1_attn_W_in, L1_attn_conv_w, L1_attn_conv_b, L1_attn_dt_bias, L1_attn_A_log, L1_attn_Dp,
           L1_attn_gnorm_w, L1_attn_norm_w, L1_attn_W_out,
           L1_ffn_W_gat, L1_ffn_att_src, L1_ffn_att_dst, L1_ffn_b_gat, L1_ffn_ln_gamma, L1_ffn_ln_beta,
           L1_ffn_W1, L1_ffn_b1, L1_ffn_W2, L1_ffn_b2, L1_ffn_edge_index):
    import concourse.bacc as _bacc
    from concourse import mybir as _mybir
    from concourse.bass_utils import run_bass_kernel_spmd as _run

    def rows_in_tiles(w):
        w = np.asarray(w)
        return w.reshape(-1, P, w.shape[1]).transpose(1, 0, 2)

    def vector_tiles(v):
        return np.asarray(v).reshape(-1, P).T

    def column(v):
        return np.asarray(v)[:, None]

    def on_all(v):
        v = np.asarray(v)
        return np.broadcast_to(v.reshape(1, -1), (P, v.size))

    def xbc_tiles(w):
        w = np.asarray(w)
        t = np.zeros((NX + 2, P, w.shape[1]), w.dtype)
        t[:NX] = w[:DI].reshape(NX, P, -1)
        t[NX, :DS], t[NX + 1, :DS] = w[DI:DI + DS], w[DI + DS:]
        return t.transpose(1, 0, 2)

    qkv, qkv_b = np.asarray(L0_conv_qkv_w), np.asarray(L0_conv_qkv_b)
    w_in = np.asarray(L1_attn_W_in).T
    att = np.stack([np.asarray(L1_ffn_att_src).reshape(-1), np.asarray(L1_ffn_att_dst).reshape(-1)])
    w1, w2 = np.asarray(L1_ffn_W1), np.asarray(L1_ffn_W2)
    lanes = np.arange(P)
    arrays = dict(
        x=np.asarray(x).reshape(B, C, HW),
        fc1=rows_in_tiles(np.asarray(L0_conv_fc1_w).T), fc1_b=column(L0_conv_fc1_b),
        fc2=np.asarray(L0_conv_fc2_w).T, fc2_b=vector_tiles(L0_conv_fc2_b),
        wq=np.tile(qkv[:AD].T, (1, 4)), wk=np.tile(qkv[AD:2 * AD].T, (1, 4)), wv=qkv[2 * AD:].T,
        bq=column(qkv_b[:AD]), bk=column(qkv_b[AD:2 * AD]), bv=column(qkv_b[2 * AD:]),
        proj=np.tile(np.asarray(L0_conv_proj_w).T, (1, 2)), proj_b=column(L0_conv_proj_b),
        ffn1=rows_in_tiles(np.asarray(L0_conv_ffn1_w).T), ffn1_b=vector_tiles(L0_conv_ffn1_b),
        ffn2=rows_in_tiles(np.asarray(L0_conv_ffn2_w).T), ffn2_b=vector_tiles(L0_conv_ffn2_b),
        w_z=rows_in_tiles(w_in[:, :DI]), w_x=rows_in_tiles(w_in[:, DI:2 * DI + 2 * DS]),
        w_dt=rows_in_tiles(w_in[:, 2 * DI + 2 * DS:]), w_out=rows_in_tiles(np.asarray(L1_attn_W_out).T),
        norm_w=vector_tiles(L1_attn_norm_w), gnorm_w=vector_tiles(L1_attn_gnorm_w),
        conv_w=xbc_tiles(L1_attn_conv_w), conv_b=xbc_tiles(column(L1_attn_conv_b))[:, :, 0],
        dt_b=on_all(L1_attn_dt_bias), a_log=on_all(L1_attn_A_log), dp=on_all(L1_attn_Dp),
        w_gat=rows_in_tiles(L1_ffn_W_gat), att=np.broadcast_to(att, (P, 2, GF)),
        edges=np.asarray(L1_ffn_edge_index),
        b_gat=on_all(L1_ffn_b_gat), ln_g=on_all(L1_ffn_ln_gamma), ln_b=on_all(L1_ffn_ln_beta),
        moe1=w1.reshape(NE, CH, P, HF).transpose(2, 0, 1, 3),
        moe1_b=np.asarray(L1_ffn_b1).reshape(NE, FT, P).transpose(2, 0, 1),
        moe2=w2.reshape(NE, FT, P, C).transpose(2, 0, 1, 3), moe2_b=np.asarray(L1_ffn_b2),
        c_ident=np.eye(P, dtype=np.float32), c_lanes=np.tile(np.arange(P, dtype=np.float32), (P, 1)),
        c_group=np.kron(np.eye(16, dtype=np.float32), np.full((8, 8), 1 / 8, np.float32)),
        c_upper=np.triu(np.ones((P, P), np.float32)),
        c_signs=np.stack([1.0 - 2.0 * ((lanes >> k) & 1) for k in range(P_BITS)], 1).astype(np.float32),
        c_pick=np.repeat(np.eye(NE, dtype=np.float32)[:, :, None], P, 2))
    arrays = {name: np.ascontiguousarray(a) for name, a in arrays.items()}

    nc = _bacc.Bacc("TRN2", target_bir_lowering=False, num_devices=1)
    D = {name: nc.dram_tensor(name, a.shape, _mybir.dt.from_np(a.dtype), kind="ExternalInput").ap()
         for name, a in arrays.items()}
    D["out"] = nc.dram_tensor("out", (B, C, HW), _mybir.dt.float32, kind="ExternalOutput").ap()
    build_program(nc, D)
    r = _run(nc, [arrays], core_ids=[0])
    return r.results[0]["out"].reshape(B, C, 32, 32)
```

```python
from contextlib import ExitStack

import numpy as np
import concourse.bass as bass
from concourse import mybir

ALU = mybir.AluOpType
ACT = mybir.ActivationFunctionType
AXX = mybir.AxisListType.X
F32 = mybir.dt.float32
I32 = mybir.dt.int32
U32 = mybir.dt.uint32
BF16 = mybir.dt.bfloat16

P = 128
B, C, HW = 16, 256, 1024
M = B * HW
CH = C // P
HALF = 512


class Steps:

    def __init__(self, eng, sem):
        self.eng, self.sem, self.base, self.k = eng, sem, 0, 0

    def turn(self, base):
        self.base, self.k = base, 0

    def did(self, instruction):
        instruction.then_inc(self.sem, 1)
        self.k += 1

    def wait(self):
        self.eng.wait_ge(self.sem, self.base + self.k)


class Space:

    def __init__(self, nc, ctx, phase):
        self.nc, self.ctx, self.phase, self.signals = nc, ctx, phase, []
        ctx.callback(self.clear_signals)

    def sb(self, name, shape, dt=F32):
        return self.ctx.enter_context(self.nc.sbuf_tensor(f"{self.phase}_{name}", shape, dt))

    def ps(self, name, cols, dt=F32):
        return self.ctx.enter_context(self.nc.psum_tensor(f"{self.phase}_{name}", [P, cols], dt))

    def sem(self, name):
        self.signals.append(self.nc.alloc_semaphore(name=f"{self.phase}_{name}"))
        return self.signals[-1]

    def clear_signals(self):
        self.nc.clear_and_free_semaphores(self.signals)
        self.nc.all_engine_barrier()

    def sems(self, name, n):
        return [self.sem(f"{name}{j}") for j in range(n)]


EDGES = 1048576
COLS = EDGES // P
BW, KW = 512, 64
NBLOCK, NPART = COLS // BW, BW // KW
GROUPS = NBLOCK * NPART
P_BITS = 7
BB = BW.bit_length() - 1
NODE_BITS = M.bit_length() - 1
KEY_BASE = 0x40000000
CLASS_1, CLASS_2 = 2.0 ** 33, 2.0 ** 65
AD, SC = 16, 32
HID = 4 * C
HID_T = HID // P
NT = HW // P
GN_EPS = 1e-5
SORT_STEPS = 6 + BB * (BB + 1) // 2 - 1
HEAD_STEPS = 13
VEC_TAIL = 2


def phase_conv(nc, D):
    with ExitStack() as ctx:
        s = Space(nc, ctx, "conv")
        sb, ps, sem, sems = s.sb, s.ps, s.sem, s.sems
        group = sb("group", [P, P])
        fc1 = sb("fc1", [P, CH, 64])
        fc2 = sb("fc2", [64, C])
        wq, wk = sb("wq", [SC, 4 * AD]), sb("wk", [SC, 4 * AD])
        wv = sb("wv", [SC, SC])
        proj = sb("proj", [SC, 2 * SC])
        ffn1 = sb("ffn1", [P, CH, HID])
        ffn2 = sb("ffn2", [P, HID_T, C])
        fc1_b, fc2_b = sb("fc1_b", [64, 1]), sb("fc2_b", [P, CH])
        bq, bk, bv = sb("bq", [AD, 1]), sb("bk", [AD, 1]), sb("bv", [SC, 1])
        proj_b = sb("proj_b", [SC, 1])
        ffn1_b, ffn2_b = sb("ffn1_b", [P, HID_T]), sb("ffn2_b", [P, CH])
        ident = sb("ident", [P, P])
        loads = [(group, "c_group"), (fc1, "fc1"), (fc2, "fc2"), (wq, "wq"), (wk, "wk"), (wv, "wv"),
                 (proj, "proj"), (ffn1, "ffn1"), (ffn2, "ffn2"), (fc1_b, "fc1_b"), (fc2_b, "fc2_b"),
                 (bq, "bq"), (bk, "bk"), (bv, "bv"), (proj_b, "proj_b"), (ffn1_b, "ffn1_b"),
                 (ffn2_b, "ffn2_b"), (ident, "c_ident")]
        nfc2_b, fence = sb("nfc2_b", [P, CH]), sb("fence", [P, 1])
        ones = sb("ones", [33, 2 * SC])
        X = [sb(f"X{u}", [P, CH, HW]) for u in range(2)]
        Y = [sb(f"Y{u}", [P, CH, HW]) for u in range(2)]
        T = [sb(f"T{u}", [P, CH, HW]) for u in range(2)]
        stats, mv = sb("stats", [P, CH, 2, 6]), sb("mv", [P, CH, 2])
        sq, st2 = sb("sq", [P, CH]), sb("st2", [P, 4])
        gs, var, sd, rs = sb("gs", [P, 4]), sb("var", [P, CH]), sb("sd", [P, CH]), sb("rs", [P, CH])
        nmr, sein = sb("nmr", [P, CH]), sb("sein", [P, CH])
        f1, ex, gate = sb("f1", [64, 1]), sb("ex", [P, CH]), sb("gate", [P, CH])
        scale, shift = sb("scale", [P, CH]), sb("shift", [P, CH])
        qq, kk = sb("qq", [AD + 1, HW]), sb("kk", [AD + 1, HW])
        vT = sb("vT", [P, NT, SC + 1])
        nmax, nmaxT = sb("nmax", [P, NT]), sb("nmaxT", [NT, P])
        PR = sb("PR", [P, NT, HW])
        rrow, osb, att = sb("rrow", [33, HW]), sb("osb", [SC, HW]), sb("att", [SC, HW])
        H = sb("H", [P, HID_T, HALF])
        E = [sb(f"E{u}", [P, 2, BW], I32) for u in range(2)]
        flags = sb("flags", [P, 2, BW], I32)
        K = [sb(f"K{k}", [P, BW]) for k in range(2)]
        KS = [sb(f"KS{u}", [P, BW]) for u in range(2)]
        pA, pB, pO = ps("pA", HW), ps("pB", HW), ps("pO", HW)
        pM, pF = ps("pM", HALF), ps("pF", HALF)
        pAB = [pA, pB]
        banks = [pA[:, 0:HALF], pA[:, HALF:HW], pB[:, 0:HALF], pB[:, HALF:HW]]

        weights_in, consts = sem("weights_in"), sem("consts")
        x_in, x_free = sems("x_in", 2), sems("x_free", 2)
        vec, gs_done, var_done, sd_done = sem("vec"), sem("gs_done"), sem("var_done"), sem("sd_done")
        st2_done, sein_done = sem("st2_done"), sem("sein_done")
        fc1_done, f1_done, fc2_done, ex_done = sem("fc1_done"), sem("f1_done"), sem("fc2_done"), sem("ex_done")
        y_done, qk_done, q_in, v_done, vT_in = sem("y_done"), sem("qk_done"), sem("q_in"), sem("v_done"), sem("vT_in")
        s_done, max_done = sem("s_done"), sem("max_done")
        maxT_done, maxT_in, nmax_in = sem("maxT_done"), sem("maxT_in"), sem("nmax_in")
        st_done, exp_done, pv_done = sem("st_done"), sem("exp_done"), sem("pv_done")
        rrow_done, bc_done, att_done, proj_done, y0_done = sem("rrow_done"), sem("bc_done"), sem("att_done"), sem("proj_done"), sem("y0_done")
        h_done, relu_done, o_done, t_done = sem("h_done"), sem("relu_done"), sem("o_done"), sem("t_done")
        t_out = sems("t_out", 2)
        e_in, blocks_out, sorting, sorted_, heading = sems("e_in", 2), sems("blocks_out", 2), sem("sorting"), sem("sorted"), sem("heading")
        block = ctx.enter_context(nc.Block())
        tv = D["t1"]

        @block.gpsimd
        def _(pool):
            pool.memset(ones[:, :], 1.0).then_inc(consts, 1)
            pool.memset(vT[:, :, SC:SC + 1], 1.0).then_inc(consts, 1)
            pool.memset(kk[:, :], 1.0).then_inc(consts, 1)
            with pool.Fori(0, B // 2) as i:
                n16 = pool.snap(i * 16 + 16)
                for u in range(2):
                    pool.wait_ge(x_free[u], n16)
                    pool.dma_start(X[u][:, :, :], D["x"][i * 2 + u].rearrange("(h p) n -> p h n", p=P)).then_inc(x_in[u], 16)
                    for a in range(2):
                        pool.dma_start(E[u][:, a, :], D["edges"][a].rearrange("(p b w) -> b p w", p=P, w=BW)[i * 2 + u]).then_inc(e_in[u], 16)
            pool.wait_ge(x_free[0], 16 * (B // 2) + 16)
            pool.dma_start(X[0][:, :, :], D["x"][0].rearrange("(h p) n -> p h n", p=P)).then_inc(x_in[0], 16)

        @block.sync
        def _(sync):
            for dst, name in loads:
                sync.dma_start(dst[tuple(slice(None) for _ in dst.shape)], D[name]).then_inc(weights_in, 16)
            with sync.Fori(0, B // 2) as i:
                b0 = sync.snap(i * 2)
                for u in range(2):
                    sync.wait_ge(maxT_in, b0 + (u + 1))
                    sync.dma_start(qq[AD:AD + 1, :].rearrange("a (t p) -> a t p", p=P), nmaxT[:, :]).then_inc(nmax_in, 16)
                    sync.wait_ge(sorted_, b0 + (u + 2))
                    sync.dma_start(D["blocks"].rearrange("(q b p w) -> b p q w", b=NBLOCK, p=P, w=KW)[i * 2 + u],
                                   KS[u][:, :].rearrange("p (q w) -> p q w", w=KW)).then_inc(blocks_out[u], 16)
                    sync.wait_ge(t_done, b0 * 4 + 4 * (u + 1))
                    sync.dma_start(tv[i * 2 + u].rearrange("(h p) n -> p h n", p=P), T[u][:, :, :]).then_inc(t_out[u], 16)
            for u in range(2):
                sync.wait_ge(t_out[u], 16 * (B // 2 + 1))
                sync.wait_ge(blocks_out[u], 16 * (B // 2 + 1))

        @block.vector
        def _(v):
            own, hd, srt = Steps(v, vec), Steps(v, heading), Steps(v, sorting)
            v.sem_inc(sorted_, 1)
            v.wait_ge(weights_in, 16 * len(loads))
            v.tensor_scalar(nfc2_b[:, :], fc2_b[:, :], -1.0, None, ALU.mult).then_inc(consts, 1)
            for u in range(2):
                v.sem_inc(x_free[u], 16)
                v.sem_inc(t_out[u], 16)
                v.sem_inc(blocks_out[u], 16)
            assert NBLOCK == B

            def make_keys(i, u):
                v.wait_ge(e_in[u], i * 32 + 32)
                srt.turn(i * (2 * SORT_STEPS) + u * SORT_STEPS)
                v.wait_ge(sorted_, i * 2 + (u + 1))
                src, dst = E[u][:, 0, :], E[u][:, 1, :]
                v.tensor_scalar(dst, dst, float(M), None, ALU.min)
                srt.did(v.tensor_scalar(src, src, float(M - 1), None, ALU.min))
                srt.wait()
                v.tensor_scalar(flags[:, 0, :], dst, float(M), float(M), ALU.is_ge, ALU.mult)
                srt.did(v.tensor_scalar(flags[:, 1, :], src, float(M - 1), float(M), ALU.is_ge, ALU.mult))
                for f in range(2):
                    srt.wait()
                    v.memset(fence[:, :], 0.0)
                    srt.did(v.tensor_tensor(dst, dst, flags[:, f, :], ALU.add))
                srt.wait()
                srt.did(v.tensor_scalar(dst, dst, NODE_BITS, KEY_BASE, ALU.logical_shift_left, ALU.bitwise_or))
                srt.wait()
                srt.did(v.tensor_tensor(K[0][:, :].bitcast(I32), dst, src, ALU.bitwise_or))

            def sort_keys(i, u, k0, k1):
                for k in range(k0, k1 + 1):
                    for j in range(k, 0, -1):
                        done = k * (k - 1) // 2 + k - j
                        last = k == BB and j == 1
                        n, h = 1 << j, 1 << (j - 1)
                        x = K[done % 2][:, :].rearrange("p (n b) -> p n b", b=n)
                        o = (KS[u] if last else K[1 - done % 2])[:, :].rearrange("p (n b) -> p n b", b=n)
                        lo, hi = x[:, :, 0:h], x[:, :, h:n]
                        srt.wait()
                        if last:
                            v.wait_ge(blocks_out[u], i * 16 + 16)
                        v.tensor_tensor(o[:, :, 0:h], lo, hi[:, :, ::-1] if j == k else hi, ALU.min)
                        ins = v.tensor_tensor(o[:, :, h:n], hi, lo[:, :, ::-1] if j == k else lo, ALU.max)
                        if last:
                            ins.then_inc(sorted_, 1)
                        else:
                            srt.did(ins)

            def head(i, u, part):
                b1 = i * 2 + (u + 1)
                hd.turn(i * (2 * HEAD_STEPS) + u * HEAD_STEPS)
                hd.k = (0, 3, 9)[part]
                if part == 0:
                    v.wait_ge(x_in[u], i * 16 + 16)
                    for h in range(CH):
                        for c in range(2):
                            ins = v.bn_stats(stats[:, h, c, :], X[u][:, h, c * HALF:(c + 1) * HALF])
                    hd.did(ins)
                    hd.wait()
                    v.memset(fence[:, :], 0.0)
                    for h in range(CH):
                        ins = v.bn_aggr(mv[:, h, :], stats[:, h, :, :])
                    hd.did(ins)
                    hd.wait()
                    v.tensor_copy(st2[:, 0:2], mv[:, :, 0])
                    hd.did(v.tensor_tensor(sq[:, :], mv[:, :, 0], mv[:, :, 0], ALU.mult))
                    hd.wait()
                    v.tensor_tensor(st2[:, 2:4], sq[:, :], mv[:, :, 1], ALU.add).then_inc(st2_done, 1)
                if part == 1:
                    v.wait_ge(gs_done, b1)
                    hd.did(v.tensor_copy(gs[:, :], pM[:, 0:4]))
                    hd.wait()
                    hd.did(v.tensor_tensor(sq[:, :], gs[:, 0:2], gs[:, 0:2], ALU.mult))
                    hd.wait()
                    hd.did(v.tensor_tensor(var[:, :], gs[:, 2:4], sq[:, :], ALU.subtract))
                    hd.wait()
                    v.tensor_scalar(var[:, :], var[:, :], 0.0, GN_EPS, ALU.max, ALU.add).then_inc(var_done, 1)
                    v.wait_ge(sd_done, b1)
                    hd.did(v.reciprocal(rs[:, :], sd[:, :]))
                    hd.wait()
                    hd.did(v.scalar_tensor_tensor(nmr[:, :], gs[:, 0:2], -1.0, rs[:, :], ALU.mult, ALU.mult))
                    hd.did(v.tensor_tensor(sein[:, :], st2[:, 0:2], rs[:, :], ALU.mult))
                    hd.wait()
                    v.tensor_tensor(sein[:, :], sein[:, :], nmr[:, :], ALU.add).then_inc(sein_done, 1)
                if part == 2:
                    v.wait_ge(ex_done, b1)
                    hd.did(v.tensor_scalar(gate[:, :], ex[:, :], 1.0, None, ALU.add))
                    hd.wait()
                    hd.did(v.reciprocal(gate[:, :], gate[:, :]))
                    hd.wait()
                    hd.did(v.tensor_tensor(scale[:, :], rs[:, :], gate[:, :], ALU.mult))
                    hd.did(v.tensor_tensor(shift[:, :], nmr[:, :], gate[:, :], ALU.mult))
                    hd.wait()
                    for h in range(CH):
                        ins = v.tensor_scalar(Y[u][:, h, :], X[u][:, h, :], scale[:, h:h + 1], shift[:, h:h + 1], ALU.mult, ALU.add)
                    ins.then_inc(y_done, 1)
                    assert hd.k == HEAD_STEPS

            for part in range(3):
                head(0, 0, part)
            with v.Fori(0, B // 2) as i:
                b0 = v.snap(i * 2)
                for u in range(2):
                    own.turn(i * (2 * VEC_TAIL) + u * VEC_TAIL)
                    b1 = v.snap(b0 + (u + 1))
                    v.wait_ge(v_done, b1)
                    v.tensor_copy(vT[:, :, 0:SC], pF[:, 0:NT * SC].rearrange("p (t c) -> p t c", c=SC)).then_inc(vT_in, 1)
                    for t in range(NT):
                        v.wait_ge(s_done, b0 * NT + (u * NT + t + 1))
                        v.tensor_reduce(nmax[:, t:t + 1], pAB[t % 2][:, :], AXX, ALU.max, negate=True).then_inc(max_done, 1)
                    v.wait_ge(maxT_done, b1)
                    v.tensor_copy(nmaxT[:, :], pM[0:NT, 0:P]).then_inc(maxT_in, 1)
                    v.wait_ge(pv_done, b1)
                    v.reciprocal(rrow[SC:SC + 1, :], pO[SC:SC + 1, :]).then_inc(rrow_done, 1)
                    own.did(v.tensor_copy(osb[:, :], pO[0:SC, :]))
                    v.wait_ge(bc_done, b1)
                    own.wait()
                    own.did(v.tensor_tensor(att[:, :], osb[:, :], pA[0:SC, :], ALU.mult))
                    own.wait()
                    v.tensor_scalar(att[:, :], att[:, :], bv[:, 0:1], None, ALU.add).then_inc(att_done, 1)
                    v.wait_ge(proj_done, b1)
                    v.tensor_scalar(Y[u][0:SC, 0, :], pB[0:SC, :], proj_b[:, 0:1], None, ALU.add).then_inc(y0_done, 1)
                    v.wait_ge(t_out[u], i * 16 + 16)
                    head(i + u, 1 - u, 0)
                    make_keys(i, u)
                    for th in range(2):
                        if th:
                            sort_keys(i, u, 7, BB)
                            head(i + u, 1 - u, 2)
                        else:
                            sort_keys(i, u, 1, 6)
                            head(i + u, 1 - u, 1)
                        for o in range(CH):
                            k = th * CH + o
                            v.wait_ge(o_done, b0 * 4 + (u * 4 + k + 1))
                            cols = slice(th * HALF, (th + 1) * HALF)
                            ins = v.scalar_tensor_tensor(T[u][:, o, cols], pO[:, o * HALF:(o + 1) * HALF], ffn2_b[:, o:o + 1],
                                                         X[u][:, o, cols], ALU.add, ALU.add)
                            ins.then_inc(t_done, 1)
                    v.wait_ge(t_done, b0 * 4 + 4 * (u + 1))
                    v.sem_inc(x_free[u], 16)
            assert own.k == VEC_TAIL and srt.k == SORT_STEPS

        @block.tensor
        def _(pe):
            pe.wait_ge(weights_in, 16 * len(loads))
            pe.wait_ge(consts, 4)

            def head(i, u, part):
                b1 = i * 2 + (u + 1)
                if part == 0:
                    pe.wait_ge(st2_done, b1)
                    pe.matmul(pM[:, 0:4], group[:, :], st2[:, :], start=True, stop=True).then_inc(gs_done, 1)
                if part == 1:
                    pe.wait_ge(sein_done, b1)
                    for h in range(CH):
                        mm = pe.matmul(pM[0:64, 4:5], fc1[:, h, :], sein[:, h:h + 1], start=(h == 0), stop=(h == CH - 1))
                    mm.then_inc(fc1_done, 1)
                if part == 2:
                    pe.wait_ge(f1_done, b1)
                    for h in range(CH):
                        mm = pe.matmul(pM[:, 5 + h:6 + h], fc2[:, h * P:(h + 1) * P], f1[:, :], start=True, stop=True)
                    mm.then_inc(fc2_done, 1)

            for part in range(3):
                head(0, 0, part)
            with pe.Fori(0, B // 2) as i:
                b0 = pe.snap(i * 2)
                for u in range(2):
                    b1 = pe.snap(b0 + (u + 1))
                    pe.wait_ge(y_done, b1)
                    for j in range(2):
                        cols = slice(j * HALF, (j + 1) * HALF)
                        pe.matmul(pA[0:4 * AD, cols], wq[:, :], Y[u][0:SC, 0, cols], start=True, stop=True)
                        mm = pe.matmul(pB[0:4 * AD, cols], wk[:, :], Y[u][0:SC, 0, cols], start=True, stop=True)
                    mm.then_inc(qk_done, 1)
                    for t in range(NT):
                        mm = pe.matmul(pF[:, t * SC:(t + 1) * SC], Y[u][0:SC, 0, t * P:(t + 1) * P], wv[:, :], start=True, stop=True)
                    mm.then_inc(v_done, 1)
                    pe.wait_ge(q_in, b1)
                    for t in range(NT):
                        if t >= 2:
                            pe.wait_ge(max_done, b0 * NT + (u * NT + t - 1))
                        for j in range(2):
                            mm = pe.matmul(pAB[t % 2][:, j * HALF:(j + 1) * HALF], qq[0:AD, t * P:(t + 1) * P],
                                           kk[0:AD, j * HALF:(j + 1) * HALF], start=True, stop=True)
                        mm.then_inc(s_done, 1)
                    pe.wait_ge(max_done, b0 * NT + (u + 1) * NT)
                    pe.transpose(pM[0:NT, 0:P], nmax[:, :], ident[:, :]).then_inc(maxT_done, 1)
                    pe.wait_ge(nmax_in, b1 * 16)
                    pe.wait_ge(vT_in, b1)

                    def weighted(t):
                        pe.wait_ge(exp_done, b0 * NT + (u * NT + t + 1))
                        for j in range(2):
                            mm = pe.matmul(pO[0:SC + 1, j * HALF:(j + 1) * HALF], vT[:, t, :], PR[:, t, j * HALF:(j + 1) * HALF],
                                           start=(t == 0), stop=(t == NT - 1))
                        return mm

                    for t in range(NT):
                        if t >= 2:
                            pe.wait_ge(exp_done, b0 * NT + (u * NT + t - 1))
                        for j in range(2):
                            mm = pe.matmul(pAB[t % 2][:, j * HALF:(j + 1) * HALF], kk[0:AD + 1, t * P:(t + 1) * P],
                                           qq[0:AD + 1, j * HALF:(j + 1) * HALF], start=True, stop=True)
                        mm.then_inc(st_done, 1)
                        if t >= 1:
                            weighted(t - 1)
                    weighted(NT - 1).then_inc(pv_done, 1)
                    pe.wait_ge(rrow_done, b1)
                    for j in range(2):
                        mm = pe.matmul(pA[0:2 * SC, j * HALF:(j + 1) * HALF], ones[SC:SC + 1, :], rrow[SC:SC + 1, j * HALF:(j + 1) * HALF],
                                       start=True, stop=True)
                    mm.then_inc(bc_done, 1)
                    pe.wait_ge(att_done, b1)
                    for j in range(2):
                        mm = pe.matmul(pB[0:2 * SC, j * HALF:(j + 1) * HALF], proj[:, :], att[:, j * HALF:(j + 1) * HALF], start=True, stop=True)
                    mm.then_inc(proj_done, 1)
                    pe.wait_ge(y0_done, b1)
                    for th in range(2):
                        cols = slice(th * HALF, (th + 1) * HALF)
                        for f in range(HID_T):
                            g = th * HID_T + f
                            if g >= 4:
                                pe.wait_ge(relu_done, b0 * 2 * HID_T + (u * 2 * HID_T + g - 3))
                            for h in range(CH):
                                mm = pe.matmul(banks[g % 4], ffn1[:, h, f * P:(f + 1) * P], Y[u][:, h, cols], start=(h == 0), stop=(h == CH - 1))
                            mm.then_inc(h_done, 1)
                        head(i + u, 1 - u, 2 * th)
                        pe.wait_ge(relu_done, b0 * 2 * HID_T + (u * 2 + th + 1) * HID_T)
                        for o in range(CH):
                            if th:
                                pe.wait_ge(t_done, b0 * 4 + (u * 4 + o + 1))
                            for f in range(HID_T):
                                mm = pe.matmul(pO[:, o * HALF:(o + 1) * HALF], ffn2[:, f, o * P:(o + 1) * P], H[:, f, :],
                                               start=(f == 0), stop=(f == HID_T - 1))
                            mm.then_inc(o_done, 1)
                        if th == 0:
                            head(i + u, 1 - u, 1)

        @block.scalar
        def _(act):
            act.wait_ge(weights_in, 16 * len(loads))
            act.wait_ge(consts, 4)

            def head(i, u, part):
                b1 = i * 2 + (u + 1)
                if part == 0:
                    act.wait_ge(var_done, b1)
                    act.activation(sd[:, :], var[:, :], ACT.Sqrt).then_inc(sd_done, 1)
                if part == 1:
                    act.wait_ge(fc1_done, b1)
                    act.activation(f1[:, :], pM[0:64, 4:5], ACT.Relu, bias=fc1_b[:, 0:1]).then_inc(f1_done, 1)
                if part == 2:
                    act.wait_ge(fc2_done, b1)
                    for h in range(CH):
                        ins = act.activation(ex[:, h:h + 1], pM[:, 5 + h:6 + h], ACT.Exp, bias=nfc2_b[:, h:h + 1], scale=-1.0)
                    ins.then_inc(ex_done, 1)

            for part in range(3):
                head(0, 0, part)
            with act.Fori(0, B // 2) as i:
                b0 = act.snap(i * 2)
                for u in range(2):
                    b1 = act.snap(b0 + (u + 1))
                    act.wait_ge(qk_done, b1)
                    act.activation(qq[0:AD, :], pA[0:AD, :], ACT.Identity, bias=bq[:, 0:1])
                    act.activation(kk[0:AD, :], pB[0:AD, :], ACT.Identity, bias=bk[:, 0:1]).then_inc(q_in, 1)
                    for t in range(NT):
                        act.wait_ge(st_done, b0 * NT + (u * NT + t + 1))
                        act.activation(PR[:, t, :], pAB[t % 2][:, :], ACT.Exp, scale=float(AD) ** -0.5).then_inc(exp_done, 1)
                    for th in range(2):
                        if th:
                            act.wait_ge(o_done, b0 * 4 + (u * 4 + CH))
                            head(i + u, 1 - u, 1)
                        for f in range(HID_T):
                            g = th * HID_T + f
                            act.wait_ge(h_done, b0 * 2 * HID_T + (u * 2 * HID_T + g + 1))
                            act.activation(H[:, f, :], banks[g % 4], ACT.Relu, bias=ffn1_b[:, f:f + 1]).then_inc(relu_done, 1)
                        head(i + u, 1 - u, 2 * th)


DI = 512
NH, HD, DS = 8, 64, 64
KC = 4
NX = DI // P
ST = 512
NSUP = HW // ST
NC_ = ST // P
NG = NSUP * NC_
LN_EPS = 1e-5
RMS_EPS = float(np.finfo(np.float32).eps)
CREDIT = 2
SSM_STEPS = 95
ORDER = (NX, *range(NX))
NORM_STEPS = 7
PIECES = 8


def phase_ssm(nc, D):
    with ExitStack() as ctx:
        s_ = Space(nc, ctx, "ssm")
        sb, ps, sem, sems = s_.sb, s_.ps, s_.sem, s_.sems
        w_x = sb("w_x", [P, CH, DI + 2 * DS])
        w_z = sb("w_z", [P, CH, DI])
        w_dt = sb("w_dt", [P, CH, NH])
        w_out = sb("w_out", [P, NX, C])
        norm_w, gnorm_w = sb("norm_w", [P, CH]), sb("gnorm_w", [P, NX])
        conv_w, conv_b = sb("conv_w", [P, NX + 1, KC]), sb("conv_b", [P, NX + 1])
        dt_b, a_log, dp = sb("dt_b", [P, NH]), sb("a_log", [P, NH]), sb("dp", [P, NH])
        ident, upper, ones = sb("ident", [P, P]), sb("upper", [P, P]), sb("ones", [P, P])
        loads = [(w_x, "w_x"), (w_z, "w_z"), (w_dt, "w_dt"), (w_out, "w_out"), (norm_w, "norm_w"), (gnorm_w, "gnorm_w"),
                 (conv_w, "conv_w"), (conv_b, "conv_b"), (dt_b, "dt_b"), (a_log, "a_log"), (dp, "dp"),
                 (ident, "c_ident"), (upper, "c_upper")]
        neg_a, fence = sb("neg_a", [P, NH]), sb("fence", [P, 1])
        X = [sb(f"X{s}", [P, CH, ST]) for s in range(NSUP)]
        tTs = [sb(f"tT{s}", [P, NC_, C]) for s in range(NSUP)]
        stats, mvs = sb("stats", [P, NC_, 6]), [sb(f"mv{s}", [P, NC_, 2]) for s in range(NSUP)]
        rstds = [sb(f"rstd{s}", [P, NC_]) for s in range(NSUP)]
        ve, ve2, r2, xr = (sb(n, [P, NC_]) for n in ("ve", "ve2", "r2", "xr"))
        xnT = [sb(f"xnT{j}", [P, C]) for j in range(NC_)]
        xnF = sb("xnF", [P, CH, ST])
        XC = [sb(f"XC{s}", [P, NX + 1, KC - 1 + ST]) for s in range(NSUP)]
        CV = sb("CV", [P, NX + 1, ST])
        XS = sb("XS", [P, NX + 2, ST])
        zs = sb("zs", [P, NC_, DI])
        dv, de, du, dd, dt4, dtA = (sb(n, [P, NC_, NH]) for n in ("dv", "de", "du", "dd", "dt4", "dtA"))
        cumS = [sb(f"cumS{j}", [P, 2 * NH]) for j in range(2)]
        sm = [sb(f"sm{j}", [P, 3, NH]) for j in range(2)]
        se = [sb(f"se{j}", [P, 3, NH]) for j in range(2)]
        dec = [sb(f"dec{j}", [P, NH, P]) for j in range(2)]
        Mm = [sb(f"Mm{j}", [P, P]) for j in range(2)]
        BT = [sb(f"BT{j}", [P, DS]) for j in range(2)]
        xdt = [sb(f"xdt{j}", [P, DI]) for j in range(2)]
        xw = [sb(f"xw{j}", [P, DI]) for j in range(2)]
        xd = [sb(f"xd{j}", [P, DI]) for j in range(2)]
        ya = [sb(f"ya{j}", [P, DI]) for j in range(2)]
        state, state_dec = sb("state", [DS, DI]), sb("state_dec", [DS, DI])
        yo = sb("yo", [P, DI])
        squares = sb("squares", [P, DI])
        ss = sb("ss", [P, NC_])
        vr, rr = sb("vr", [P, NC_]), sb("rr", [P, NC_])
        gF = sb("gF", [P, NX, P])
        oT = sb("oT", [P, NC_, C])
        OUT = [sb(f"OUT{s}", [P, NC_, C]) for s in range(NSUP)]
        k_turn, k_p0, k_p1, k_s = ps("k_turn", 512), ps("k_p0", 512), ps("k_p1", 512), ps("k_s", 512)
        k_decay, k_y, k_off = ps("k_decay", 1024), ps("k_y", 512), ps("k_off", 512)
        kp = [k_p0, k_p1]
        DTP, CUM, TOT, MT, BTP = (k_s[:, a:a + n] for a, n in ((0, 32), (32, NH), (32 + NH, NH), (128, P), (256, DS)))

        weights_in, consts, own_s, norm_s = sem("weights_in"), sem("consts"), sem("vec"), sem("norm")
        names = ("t_turned sq1_in sq1 sq2_in sq2 xn_in xn_turned xnF_in xc_done xc_in cv_in silu_in z_done z_in dt_done "
                 "dabs_in dexp_in du_in dln_in dt_in cum_done xs_turned t_in dec_in exp_in sm_in se_in bt_in xdt_in xw_in w_in sdec_in px_read "
                 "y_done off_done snew_done h_in g_in g_turned gf_in o_done o_in ss_in rr_in rrs t2_in").split()
        S = {n: sem(n) for n in names}
        x_in, out_out = sems("x_in", NSUP), sems("out_out", NSUP)
        block = ctx.enter_context(nc.Block())

        def need(eng, name, value):
            eng.wait_ge(S[name], value + CREDIT)

        by_engine = {"pool": "xw_in w_in sdec_in",
                     "act": "sq1 sq2 xnF_in xc_in silu_in z_in dexp_in dln_in exp_in se_in gf_in o_in ss_in rrs",
                     "pe": "t_turned xn_turned xc_done z_done dt_done cum_done xs_turned y_done off_done snew_done g_turned o_done"}

        def reg(eng, value):
            return value if type(value) is int else eng.snap(value)

        def credit(eng, which):
            mine = by_engine[which].split() if which in by_engine else [n for n in names if n not in " ".join(by_engine.values()).split()]
            for n in mine:
                eng.sem_inc(S[n], CREDIT)

        @block.gpsimd
        def _(pool):
            pool.memset(ones[:, :], 1.0).then_inc(consts, 1)
            pool.memset(XC[0][:, :, 0:KC - 1], 0.0).then_inc(consts, 1)
            pool.wait_ge(consts, 5)
            credit(pool, "pool")
            with pool.Fori(0, B) as i:
                g0 = pool.snap(i * NG)
                for s in range(NSUP):
                    def decay_state(c):
                        j, g1 = c % 2, g0 + (s * NC_ + c + 1)
                        need(pool, "se_in", g1)
                        need(pool, "h_in", g1)
                        pool.tensor_tensor(state_dec[:, :].rearrange("p (h d) -> p h d", h=NH), state[:, :].rearrange("p (h d) -> p h d", h=NH),
                                           se[j][0:DS, 2, :].unsqueeze(2).to_broadcast([DS, NH, HD]), ALU.mult).then_inc(S["sdec_in"], 1)

                    for c in range(NC_):
                        if c:
                            decay_state(c - 1)
                        j, g1 = c % 2, pool.snap(g0 + (s * NC_ + c + 1))
                        need(pool, "off_done", g1 - 2)
                        need(pool, "se_in", g1)
                        need(pool, "xdt_in", g1)
                        pool.tensor_tensor(xw[j][:, :].rearrange("p (h d) -> p h d", h=NH), xdt[j][:, :].rearrange("p (h d) -> p h d", h=NH),
                                           se[j][:, 0, :].unsqueeze(2).to_broadcast([P, NH, HD]), ALU.mult).then_inc(S["xw_in"], 1)
                        need(pool, "exp_in", g1)
                        need(pool, "bt_in", g1)
                        pool.tensor_tensor(dec[j][:, :, :], dec[j][:, :, :], Mm[j][:, :].unsqueeze(1).to_broadcast([P, NH, P]), ALU.mult).then_inc(S["w_in"], 1)
                    if s < NSUP - 1:
                        decay_state(NC_ - 1)

        @block.sync
        def _(sync):
            for dst, name in loads:
                sync.dma_start(dst[tuple(slice(None) for _ in dst.shape)], D[name]).then_inc(weights_in, 16)

            def load(i, s):
                sync.dma_start(X[s][:, :, :], D["t1"][i].rearrange("(h p) n -> p h n", p=P)[:, :, s * ST:(s + 1) * ST]).then_inc(x_in[s], 16)

            def store(i, s):
                need(sync, "t2_in", i * NG + (s + 1) * NC_)
                sync.dma_start(D["t2"][i].rearrange("(s c p) f -> s p c f", p=P, c=NC_)[s], OUT[s][:, :, :]).then_inc(out_out[s], 16)

            load(0, 0)
            load(0, 1)
            with sync.Fori(0, B - 1) as i:
                for s in range(NSUP):
                    store(i, s)
                    load(i + 1, s)
            store(B - 1, 0)
            load(0, 0)
            store(B - 1, 1)
            for s in range(NSUP):
                sync.wait_ge(out_out[s], 16 * (B + 1))

        @block.vector
        def _(v):
            own, norm = Steps(v, own_s), Steps(v, norm_s)
            v.wait_ge(weights_in, 16 * len(loads))
            for s in range(NSUP):
                v.sem_inc(out_out[s], 16)
            for k in range(CH):
                for w in (w_x, w_z, w_dt):
                    v.tensor_scalar(w[:, k, :], w[:, k, :], norm_w[:, k:k + 1], None, ALU.mult)
            for k in range(NX):
                ins = v.tensor_scalar(w_out[:, k, :], w_out[:, k, :], gnorm_w[:, k:k + 1], None, ALU.mult)
            ins.then_inc(consts, 1)
            v.wait_ge(consts, 4)
            v.tensor_scalar(neg_a[:, :], neg_a[:, :], -1.0, None, ALU.mult).then_inc(consts, 1)
            v.wait_ge(consts, 5)
            credit(v, "v")

            def normalize(i, s, piece):
                tT, mv, rstd = tTs[s], mvs[s], rstds[s]
                s1 = reg(v, i * NSUP + (s + 1))
                norm.turn(i * (NSUP * NORM_STEPS) + s * NORM_STEPS)
                norm.k = {4: 2, 5: 5}.get(piece, 0)
                if piece in (1, 3):
                    q = piece // 2
                    need(v, "t_turned", i * (2 * NSUP) + (s * 2 + q + 1))
                    v.tensor_copy(tT[:, 2 * q:2 * q + 2, :], k_turn[:, :].rearrange("p (c f) -> p c f", c=2)).then_inc(S["t_in"], 1)
                if piece == 3:
                    need(v, "t_in", i * (2 * NSUP) + (s + 1) * 2)
                    for c in range(NC_):
                        ins = v.bn_stats(stats[:, c, :], tT[:, c, :])
                    norm.did(ins)
                    norm.wait()
                    v.memset(fence[:, :], 0.0)
                    for c in range(NC_):
                        ins = v.bn_aggr(mv[:, c, :], stats[:, c, :])
                    norm.did(ins)
                    norm.wait()
                    v.tensor_scalar(ve[:, :], mv[:, :, 1], LN_EPS, None, ALU.add).then_inc(S["sq1_in"], 1)
                if piece == 4:
                    need(v, "sq1", s1)
                    norm.did(v.reciprocal(rstd[:, :], rstd[:, :]))
                    norm.wait()
                    norm.did(v.tensor_tensor(ve2[:, :], mv[:, :, 1], rstd[:, :], ALU.mult))
                    norm.wait()
                    norm.did(v.tensor_tensor(ve2[:, :], ve2[:, :], rstd[:, :], ALU.mult))
                    norm.wait()
                    v.tensor_scalar(ve2[:, :], ve2[:, :], RMS_EPS, None, ALU.add).then_inc(S["sq2_in"], 1)
                if piece == 5:
                    need(v, "sq2", s1)
                    norm.did(v.reciprocal(r2[:, :], r2[:, :]))
                    norm.wait()
                    norm.did(v.tensor_tensor(xr[:, :], r2[:, :], rstd[:, :], ALU.mult))
                    norm.wait()
                    for c in range(NC_):
                        v.tensor_scalar(xnT[c][:, :], tT[:, c, :], mv[:, c, 0:1], xr[:, c:c + 1], ALU.subtract, ALU.mult).then_inc(S["xn_in"], 1)
                    assert norm.k == NORM_STEPS

            for piece in range(PIECES):
                normalize(0, 0, piece)
            with v.Fori(0, B) as i:
                own.turn(i * SSM_STEPS)
                g0, s0 = v.snap(i * NG), v.snap(i * NSUP)
                for s in range(NSUP):
                    s1 = v.snap(s0 + (s + 1))
                    tT, mv, rstd = tTs[s], mvs[s], rstds[s]
                    if s:
                        own.did(v.tensor_copy(XC[s][:, :, 0:KC - 1], XC[0][:, :, ST:ST + KC - 1]))
                    def conv(m):
                        need(v, "xc_in", s0 * (NX + 1) + (s * (NX + 1) + ORDER.index(m) + 1))
                        own.wait()
                        own.did(v.tensor_scalar(CV[:, m, :], XC[s][:, m, 0:ST], conv_w[:, m, 0:1], None, ALU.mult))
                        for k in range(1, KC):
                            own.wait()
                            ins = v.scalar_tensor_tensor(CV[:, m, :], XC[s][:, m, k:k + ST], conv_w[:, m, k:k + 1], CV[:, m, :], ALU.mult, ALU.add)
                            if k < KC - 1:
                                own.did(ins)
                        ins.then_inc(S["cv_in"], 1)
                    need(v, "dt_done", s1)
                    own.did(v.tensor_tensor(dv[:, :, :], DTP.rearrange("p (c h) -> p c h", h=NH), dt_b[:, :].unsqueeze(1).to_broadcast([P, NC_, NH]), ALU.add))
                    own.wait()
                    v.scalar_tensor_tensor(de[:, :, :], dv[:, :, :], -1.0, dv[:, :, :], ALU.mult, ALU.max).then_inc(S["dabs_in"], 1)
                    conv(NX)
                    need(v, "dexp_in", s1)
                    v.tensor_scalar(du[:, :, :], de[:, :, :], 1.0, None, ALU.add).then_inc(S["du_in"], 1)
                    need(v, "du_in", s1)
                    own.did(v.tensor_scalar(dd[:, :, :], du[:, :, :], 1.0, None, ALU.subtract))
                    own.wait()
                    own.did(v.tensor_scalar(dtA[:, :, :], dd[:, :, :], 0.0, None, ALU.is_equal))
                    own.did(v.tensor_scalar(dd[:, :, :], dd[:, :, :], 1e-30, None, ALU.max))
                    own.wait()
                    own.did(v.reciprocal(dd[:, :, :], dd[:, :, :]))
                    conv(0)
                    need(v, "dln_in", s1)
                    own.wait()
                    own.did(v.tensor_tensor(dd[:, :, :], dt4[:, :, :], dd[:, :, :], ALU.mult))
                    own.wait()
                    own.did(v.tensor_tensor(dd[:, :, :], dtA[:, :, :], dd[:, :, :], ALU.add))
                    own.wait()
                    own.did(v.tensor_tensor(dd[:, :, :], de[:, :, :], dd[:, :, :], ALU.mult))
                    own.wait()
                    own.did(v.scalar_tensor_tensor(dt4[:, :, :], dv[:, :, :], 0.0, dd[:, :, :], ALU.max, ALU.add))
                    own.wait()
                    v.tensor_tensor(dtA[:, :, :], dt4[:, :, :], neg_a[:, :].unsqueeze(1).to_broadcast([P, NC_, NH]), ALU.mult).then_inc(S["dt_in"], 1)
                    for m in range(1, NX):
                        conv(m)
                    def prepare(c):
                        g, j = s * NC_ + c, c % 2
                        g1 = v.snap(g0 + (g + 1))
                        if g == 0:
                            v.memset(state[:, :], 0.0).then_inc(S["h_in"], 1)
                        need(v, "cum_done", g1)
                        own.did(v.tensor_copy(cumS[j][:, :], k_s[:, 32:32 + 2 * NH]))
                        own.wait()
                        v.tensor_tensor(sm[j][:, 0, :], cumS[j][:, NH:2 * NH], cumS[j][:, 0:NH], ALU.subtract)
                        v.tensor_copy(sm[j][:, 1:3, :], cumS[j][:, :].rearrange("p (a h) -> p a h", h=NH)).then_inc(S["sm_in"], 1)
                        for h in range(NH):
                            ins = v.tensor_scalar(dec[j][:, h, :], k_decay[:, h * P:(h + 1) * P], cumS[j][:, h:h + 1], 0.0, ALU.subtract, ALU.min)
                        ins.then_inc(S["dec_in"], 1)
                        own.did(v.tensor_tensor(Mm[j][:, :], MT, upper[:, :], ALU.mult))
                        v.tensor_copy(BT[j][:, :], BTP).then_inc(S["bt_in"], 1)
                        need(v, "xs_turned", g1)
                        heads = k_p0[:, :].rearrange("p (h d) -> p h d", h=NH)
                        v.tensor_tensor(xdt[j][:, :].rearrange("p (h d) -> p h d", h=NH), heads, dt4[:, c, :].unsqueeze(2).to_broadcast([P, NH, HD]), ALU.mult).then_inc(S["xdt_in"], 1)
                        v.tensor_tensor(xd[j][:, :].rearrange("p (h d) -> p h d", h=NH), heads, dp[:, :].unsqueeze(2).to_broadcast([P, NH, HD]), ALU.mult).then_inc(S["px_read"], 1)

                    def finish(c):
                        g, j = s * NC_ + c, c % 2
                        g1 = v.snap(g0 + (g + 1))
                        need(v, "se_in", g1)
                        if g < NG - 1:
                            need(v, "sdec_in", i * (NG - 1) + (g + 1))
                            need(v, "snew_done", i * (NG - 1) + (g + 1))
                            need(v, "off_done", g1)
                            own.wait()
                            v.tensor_tensor(state[:, :], state_dec[:, :], k_p1[0:DS, :], ALU.add).then_inc(S["h_in"], 1)
                        need(v, "y_done", g1)
                        need(v, "px_read", g1)
                        own.wait()
                        own.did(v.tensor_tensor(ya[j][:, :], xd[j][:, :], k_y[:, :], ALU.add))
                        need(v, "off_done", g1)
                        own.did(v.tensor_tensor(yo[:, :].rearrange("p (h d) -> p h d", h=NH), k_off[:, :].rearrange("p (h d) -> p h d", h=NH),
                                                se[j][:, 1, :].unsqueeze(2).to_broadcast([P, NH, HD]), ALU.mult))
                        own.wait()
                        own.did(v.tensor_tensor(ya[j][:, :], ya[j][:, :], yo[:, :], ALU.add))
                        need(v, "z_in", g1)
                        own.wait()
                        v.tensor_tensor(ya[j][:, :], ya[j][:, :], zs[:, c, :], ALU.mult).then_inc(S["g_in"], 1)

                    prepare(0)
                    for c in range(NC_):
                        if c + 1 < NC_:
                            prepare(c + 1)
                        if c == 2:
                            normalize(i + s, 1 - s, 4)
                            normalize(i + s, 1 - s, 5)
                        finish(c)
                        if c < 2:
                            normalize(i + s, 1 - s, 2 * c + 1)
                    v.wait_ge(out_out[s], i * 16 + 16)
                    for c in range(NC_):
                        ins = v.tensor_scalar(OUT[s][:, c, :], tT[:, c, :], mv[:, c, 0:1], rstd[:, c:c + 1], ALU.subtract, ALU.mult)
                    own.did(ins)
                    need(v, "ss_in", g0 + (s + 1) * NC_)
                    v.tensor_scalar(vr[:, :], ss[:, :], 1.0 / DI, LN_EPS, ALU.mult, ALU.add).then_inc(S["rr_in"], 1)
                    need(v, "rrs", s1)
                    own.did(v.reciprocal(rr[:, :], rr[:, :]))
                    own.wait()
                    for c in range(NC_):
                        need(v, "o_in", g0 + (s * NC_ + c + 1))
                        ins = v.scalar_tensor_tensor(oT[:, c, :], oT[:, c, :], rr[:, c:c + 1], tT[:, c, :], ALU.mult, ALU.add)
                    own.did(ins)
                    own.wait()
                    for c in range(NC_):
                        v.tensor_tensor(OUT[s][:, c, :], OUT[s][:, c, :], oT[:, c, :], ALU.add).then_inc(S["t2_in"], 1)
            assert own.k == SSM_STEPS

        @block.tensor
        def _(pe):
            pe.wait_ge(weights_in, 16 * len(loads))
            pe.wait_ge(consts, 5)
            credit(pe, "pe")

            def normalize(i, s, piece):
                n2 = i * (2 * NSUP) + s * 2
                if piece in (0, 2):
                    q = piece // 2
                    if q == 0:
                        pe.wait_ge(x_in[s], i * 16 + 16)
                        need(pe, "xnF_in", n2)
                    else:
                        need(pe, "t_in", n2 + 1)
                    for c in (2 * q, 2 * q + 1):
                        for k in range(CH):
                            mm = pe.transpose(k_turn[:, (c % 2) * C + k * P:(c % 2) * C + (k + 1) * P], X[s][:, k, c * P:(c + 1) * P], ident[:, :])
                    mm.then_inc(S["t_turned"], 1)
                if piece in (6, 7):
                    q = piece - 6
                    need(pe, "xn_in", i * NG + (s * NC_ + 2 * q + 2))
                    need(pe, "xnF_in" if q else "t_in", n2 + (1 if q else 2))
                    for c in (2 * q, 2 * q + 1):
                        for k in range(CH):
                            mm = pe.transpose(k_turn[:, (c % 2) * C + k * P:(c % 2) * C + (k + 1) * P], xnT[c][:, k * P:(k + 1) * P], ident[:, :])
                    mm.then_inc(S["xn_turned"], 1)

            for piece in range(PIECES):
                normalize(0, 0, piece)
            with pe.Fori(0, B) as i:
                g0, s0 = pe.snap(i * NG), pe.snap(i * NSUP)
                for s in range(NSUP):
                    s1 = pe.snap(s0 + (s + 1))
                    need(pe, "xnF_in", i * 2 * NSUP + (s + 1) * 2)
                    for c in range(NC_):
                        for k in range(CH):
                            mm = pe.matmul(DTP[:, c * NH:(c + 1) * NH], xnF[:, k, c * P:(c + 1) * P], w_dt[:, k, :], start=(k == 0), stop=(k == CH - 1))
                    mm.then_inc(S["dt_done"], 1)
                    need(pe, "o_in", g0 + s * NC_)
                    if s:
                        need(pe, "h_in", g0 + s * NC_)
                    for n, m in enumerate(ORDER):
                        if n >= 2:
                            need(pe, "xc_in", s0 * (NX + 1) + (s * (NX + 1) + n - 1))
                        for k in range(CH):
                            mm = pe.matmul(kp[n % 2][:, :], w_x[:, k, m * P:(m + 1) * P], xnF[:, k, :], start=(k == 0), stop=(k == CH - 1))
                        mm.then_inc(S["xc_done"], 1)
                    for c in range(NC_):
                        if c < 2:
                            need(pe, "xc_in", s0 * (NX + 1) + (s * (NX + 1) + NX + c))
                        else:
                            need(pe, "z_in", g0 + (s * NC_ + c - 1))
                        for k in range(CH):
                            mm = pe.matmul(kp[(NX + 1 + c) % 2][:, :], xnF[:, k, c * P:(c + 1) * P], w_z[:, k, :], start=(k == 0), stop=(k == CH - 1))
                        mm.then_inc(S["z_done"], 1)
                    need(pe, "z_in", g0 + (s + 1) * NC_)
                    need(pe, "dt_in", s1)

                    def prepare(c):
                        g, j = s * NC_ + c, c % 2
                        g1 = pe.snap(g0 + (g + 1))
                        cols = slice(c * P, (c + 1) * P)
                        need(pe, "bt_in", g0 + g)
                        pe.matmul(CUM, upper[:, :], dtA[:, c, :], start=True, stop=True)
                        pe.matmul(TOT, ones[:, :], dtA[:, c, :], start=True, stop=True)
                        for h in range(NH):
                            pe.matmul(k_decay[:, h * P:(h + 1) * P], dtA[:, c, h:h + 1].to_broadcast([P, P]), upper[:, :], start=True, stop=True)
                        if c == 0:
                            need(pe, "silu_in", s0 * (NX + 1) + (s + 1) * (NX + 1))
                            pe.matmul(k_s[:, 511:512], ident[:, :], ident[:, 0:1], start=True, stop=True)
                        pe.transpose(BTP, XS[0:DS, NX, cols], ident[0:DS, 0:DS])
                        pe.matmul(MT, XS[0:DS, NX, cols], XS[0:DS, NX + 1, cols], start=True, stop=True).then_inc(S["cum_done"], 1)
                        need(pe, "px_read", g0 + g)
                        need(pe, "o_in", g0 + (s * NC_ + max(c - 2, 0)))
                        for m in range(NX):
                            mm = pe.transpose(k_p0[:, m * P:(m + 1) * P], XS[:, m, cols], ident[:, :])
                        mm.then_inc(S["xs_turned"], 1)

                    def finish(c):
                        g, j = s * NC_ + c, c % 2
                        g1 = pe.snap(g0 + (g + 1))
                        cols = slice(c * P, (c + 1) * P)
                        need(pe, "w_in", g1)
                        need(pe, "g_in", g0 + g)
                        for h in range(NH):
                            mm = pe.matmul(k_y[:, h * HD:(h + 1) * HD], dec[j][:, h, :], xdt[j][:, h * HD:(h + 1) * HD], start=True, stop=True)
                        mm.then_inc(S["y_done"], 1)
                        need(pe, "h_in", g1)
                        if g < NG - 1:
                            need(pe, "xw_in", g1)
                            need(pe, "bt_in", g1)
                            pe.matmul(k_p1[0:DS, :], BT[j][:, :], xw[j][:, :], start=True, stop=True).then_inc(S["snew_done"], 1)
                        if c:
                            output(c - 1)
                        need(pe, "gf_in", g0 + g)
                        pe.matmul(k_off[:, :], XS[0:DS, NX + 1, cols], state[:, :], start=True, stop=True).then_inc(S["off_done"], 1)

                    def turn(c):
                        g, j = s * NC_ + c, c % 2
                        need(pe, "g_in", g0 + (g + 1))
                        for m in range(NX):
                            mm = pe.transpose(k_off[:, m * P:(m + 1) * P], ya[j][:, m * P:(m + 1) * P], ident[:, :])
                        mm.then_inc(S["g_turned"], 1)

                    def output(c):
                        g1 = pe.snap(g0 + (s * NC_ + c + 1))
                        need(pe, "gf_in", g1)
                        need(pe, "px_read", g0 + (s * NC_ + min(c + 3, NC_)))
                        for m in range(NX):
                            mm = pe.matmul(k_p0[:, 0:C], gF[:, m, :], w_out[:, m, :], start=(m == 0), stop=(m == NX - 1))
                        mm.then_inc(S["o_done"], 1)

                    prepare(0)
                    for c in range(NC_):
                        if c + 1 < NC_:
                            prepare(c + 1)
                        if c < 2:
                            normalize(i + s, 1 - s, 2 * c)
                        if c:
                            turn(c - 1)
                        finish(c)
                        if c >= 2:
                            normalize(i + s, 1 - s, c + 4)
                    turn(NC_ - 1)
                    output(NC_ - 1)

        @block.scalar
        def _(act):
            act.wait_ge(weights_in, 16 * len(loads))
            act.activation(neg_a[:, :], a_log[:, :], ACT.Exp).then_inc(consts, 1)
            act.wait_ge(consts, 5)
            credit(act, "act")

            def normalize(i, s, piece):
                s1 = reg(act, i * NSUP + (s + 1))
                if piece == 3:
                    need(act, "sq1_in", s1)
                    act.activation(rstds[s][:, :], ve[:, :], ACT.Sqrt).then_inc(S["sq1"], 1)
                if piece == 4:
                    need(act, "sq2_in", s1)
                    act.activation(r2[:, :], ve2[:, :], ACT.Sqrt).then_inc(S["sq2"], 1)
                if piece in (6, 7):
                    q = piece - 6
                    need(act, "xn_turned", i * (2 * NSUP) + (s * 2 + q + 1))
                    for k in range(CH):
                        ins = act.activation(xnF[:, k, 2 * q * P:2 * (q + 1) * P].rearrange("p (c t) -> p c t", c=2),
                                             k_turn[:, :].rearrange("p (c k t) -> p c k t", c=2, k=CH)[:, :, k, :], ACT.Copy)
                    ins.then_inc(S["xnF_in"], 1)

            for piece in range(PIECES):
                normalize(0, 0, piece)
            with act.Fori(0, B) as i:
                g0, s0 = act.snap(i * NG), act.snap(i * NSUP)
                for s in range(NSUP):
                    s1 = act.snap(s0 + (s + 1))
                    for n, m in enumerate(ORDER):
                        need(act, "xc_done", s0 * (NX + 1) + (s * (NX + 1) + n + 1))
                        act.activation(XC[s][:, m, KC - 1:], kp[n % 2][:, :], ACT.Copy).then_inc(S["xc_in"], 1)
                        if n == 2:
                            need(act, "dabs_in", s1)
                            act.activation(de[:, :, :], de[:, :, :], ACT.Exp, scale=-1.0).then_inc(S["dexp_in"], 1)
                        if n == 4:
                            need(act, "du_in", s1)
                            act.activation(dt4[:, :, :], du[:, :, :], ACT.Ln).then_inc(S["dln_in"], 1)
                    def xs(m):
                        need(act, "cv_in", s0 * (NX + 1) + (s * (NX + 1) + ORDER.index(m) + 1))
                        if m < NX:
                            ins = act.activation(XS[:, m, :], CV[:, m, :], ACT.Silu, bias=conv_b[:, m:m + 1])
                        else:
                            for x in range(2):
                                part = slice(x * DS, (x + 1) * DS)
                                ins = act.activation(XS[0:DS, NX + x, :], CV[part, NX, :], ACT.Silu, bias=conv_b[part, NX:NX + 1])
                        ins.then_inc(S["silu_in"], 1)

                    for c in range(NC_):
                        need(act, "z_done", g0 + (s * NC_ + c + 1))
                        act.activation(zs[:, c, :], kp[(NX + 1 + c) % 2][:, :], ACT.Silu).then_inc(S["z_in"], 1)
                        xs(ORDER[c])
                    xs(ORDER[NX])

                    def prepare(c):
                        g, j = s * NC_ + c, c % 2
                        g1 = act.snap(g0 + (g + 1))
                        need(act, "sm_in", g1)
                        act.activation(se[j][:, :, :], sm[j][:, :, :], ACT.Exp).then_inc(S["se_in"], 1)
                        need(act, "dec_in", g1)
                        act.activation(dec[j][:, :, :], dec[j][:, :, :], ACT.Exp).then_inc(S["exp_in"], 1)

                    def turned(c):
                        need(act, "g_turned", act.snap(g0 + (s * NC_ + c + 1)))
                        act.activation(gF[:, :, :], k_off[:, :].rearrange("p (m t) -> p m t", m=NX), ACT.Copy).then_inc(S["gf_in"], 1)

                    def output(c):
                        need(act, "o_done", act.snap(g0 + (s * NC_ + c + 1)))
                        act.activation(oT[:, c, :], k_p0[:, 0:C], ACT.Copy).then_inc(S["o_in"], 1)

                    prepare(0)
                    for c in range(NC_):
                        if c + 1 < NC_:
                            prepare(c + 1)
                        if c:
                            turned(c - 1)
                            if c == 2:
                                normalize(i + s, 1 - s, 4)
                            output(c - 1)
                        need(act, "g_in", act.snap(g0 + (s * NC_ + c + 1)))
                        act.activation(squares[:, :], ya[c % 2][:, :], ACT.Square, accum_out=ss[:, c:c + 1]).then_inc(S["ss_in"], 1)
                        if c:
                            normalize(i + s, 1 - s, (3, 6, 7)[c - 1])
                    turned(NC_ - 1)
                    output(NC_ - 1)
                    need(act, "rr_in", s1)
                    act.activation(rr[:, :], vr[:, :], ACT.Sqrt).then_inc(S["rrs"], 1)
TB = 4


def phase_sort(nc, D):
    with ExitStack() as ctx:
        s_ = Space(nc, ctx, "sort")
        sb, ps, sem = s_.sb, s_.ps, s_.sem
        keys = [sb("keys0", [P, COLS]), sb("keys1", [P, COLS])]
        signs = sb("signs", [P, P_BITS])
        ident, ones = sb("ident", [P, P]), sb("ones", [P, P])
        lows = sb("lows", [P, NPART])
        count, sums = sb("count", [P, 2 + NPART]), sb("sums", [P, 2 + NPART])
        total = sb("total", [P, 4], I32)
        edge_of = sb("edge_of", [1, 2])
        banks = [ps(f"bank{k}", 512) for k in range(4)]
        blocks_in, consts_in, stored = sem("blocks_in"), sem("consts_in"), sem("stored")
        ordered, turned, read, ends_in = sem("ordered"), sem("turned"), sem("read"), sem("ends_in")
        counted, summed, known = sem("counted"), sem("summed"), sem("known")
        block = ctx.enter_context(nc.Block())
        whole, first = {}, {}
        ways = ((whole, 2), (first, 1))

        @block.vector
        def _(v):
            n = 0

            def did(ins):
                nonlocal n
                ins.then_inc(ordered, 1)
                n += 1

            class Rows:

                def __init__(self, buf, cur, width):
                    self.buf, self.cur, self.width = buf, cur, width

                def merge(self, size, mirrored):
                    a = self.buf[self.cur].rearrange("p (n b) -> p n b", b=size)
                    o = self.buf[1 - self.cur].rearrange("p (n b) -> p n b", b=size)
                    h = size // 2
                    lo, hi = a[:, :, 0:h], a[:, :, h:size]
                    v.wait_ge(ordered, n)
                    v.tensor_tensor(o[:, :, 0:h], lo, hi[:, :, ::-1] if mirrored else hi, ALU.min)
                    did(v.tensor_tensor(o[:, :, h:size], hi, lo[:, :, ::-1] if mirrored else lo, ALU.max))
                    self.cur = 1 - self.cur

                def sort(self, k0, k1):
                    for k in range(k0, k1 + 1):
                        self.merge(1 << k, True)
                        for j in range(k - 1, 0, -1):
                            self.merge(1 << j, False)

                def flip(self, r):
                    x = self.buf[self.cur]
                    v.wait_ge(ordered, n)
                    did(v.tensor_scalar(x, x, signs[:, r:r + 1], None, ALU.mult))

                def take_turned(self, t, scale):
                    nb = self.width // (TB * P)
                    for b in range(nb):
                        v.wait_ge(turned, t * nb + b + 1)
                        o = self.buf[1 - self.cur][:, b * TB * P:(b + 1) * TB * P]
                        if scale is None:
                            ins = v.tensor_copy(o, banks[b % 4][:, :])
                        else:
                            ins = v.tensor_scalar(o, banks[b % 4][:, :], signs[:, scale:scale + 1], None, ALU.mult)
                        ins.then_inc(read, 1)
                    v.wait_ge(read, (t + 1) * nb)
                    self.cur = 1 - self.cur

                def merge_rows(self, r):
                    for q in range(r, -1, -1):
                        dirs = 2 if r < P_BITS - 1 else 1
                        shape = dict(d=dirs, s=1 << (r - q), e=2, w=1 << q)
                        a = self.buf[self.cur].rearrange("p (n d s e w) -> p n d s e w", **shape)
                        o = self.buf[1 - self.cur].rearrange("p (n d s e w) -> p n d s e w", **shape)
                        v.wait_ge(ordered, n)
                        for d in range(dirs):
                            lo, hi = a[:, :, d, :, 0, :], a[:, :, d, :, 1, :]
                            v.tensor_tensor(o[:, :, d, :, 0, :], lo, hi, ALU.max if d else ALU.min)
                            ins = v.tensor_tensor(o[:, :, d, :, 1, :], lo, hi, ALU.min if d else ALU.max)
                        did(ins)
                        self.cur = 1 - self.cur

            v.memset(edge_of[:, :], 1.0).then_inc(ends_in, 1)
            v.memset(ones[:, :], 1.0)
            v.wait_ge(blocks_in, 16 * NPART)
            v.wait_ge(consts_in, 32)
            at = 0
            v.tensor_scalar(keys[1 - at][:, :], keys[at][:, :], CLASS_1, None, ALU.is_lt, ALU.add, accum_out=count[:, 0:1])
            did(v.tensor_reduce(lows[:, :], keys[at][:, :].rearrange("p (b q w) -> p q b w", q=NPART, w=KW)[:, :, :, 0], AXX, ALU.min))
            v.wait_ge(ordered, n)
            v.tensor_scalar(count[:, 1:2], lows[:, 1:2], CLASS_1, None, ALU.is_lt)
            v.tensor_scalar(count[:, 2:], lows[:, :], CLASS_2, None, ALU.is_lt).then_inc(counted, 1)
            v.wait_ge(summed, 1)
            did(v.tensor_copy(sums[:, :], banks[0][:, 0:2 + NPART]))
            v.wait_ge(ordered, n)
            did(v.tensor_scalar(sums[:, 1:], sums[:, 1:], 1.0, None, ALU.min))
            v.wait_ge(ordered, n)
            v.tensor_scalar(total[:, 0:1], sums[:, 0:1], 1.0, None, ALU.max)
            v.tensor_copy(total[:, 1:2], sums[:, 1:2])
            v.tensor_scalar(total[:, 2:3], sums[:, 1:2], -1.0, 1.0, ALU.mult, ALU.add)
            did(v.tensor_reduce(count[:, 0:1], sums[:, 2:], AXX, ALU.add))
            v.wait_ge(ordered, n)
            v.tensor_scalar(total[:, 3:4], count[:, 0:1], float(NBLOCK), None, ALU.mult).then_inc(known, 1)
            v.wait_ge(known, 1)

            n_known = n
            flag = [v.value_load(total[0:1, w:w + 1], min_val=0, max_val=1) for _, w in ways]
            for k, (way, _) in enumerate(ways):
                with v.If(flag[k] < 1):
                    n = n_known
                    if way is first:
                        width = NBLOCK * KW
                        free = keys[1 - at]
                        rows = Rows([free[:, 0:width], free[:, width:2 * width]], 0, width)
                        did(v.tensor_copy(rows.buf[0].rearrange("p (b w) -> p b w", w=KW), keys[at][:, :].rearrange("p (b w) -> p b w", w=BW)[:, :, 0:KW]))
                        k0 = KW.bit_length()
                    else:
                        rows, k0 = Rows([keys[0][:, :], keys[1][:, :]], at, COLS), BW.bit_length()
                    bits = rows.width.bit_length() - 1
                    rows.flip(0)
                    rows.sort(k0, bits)
                    rows.flip(0)
                    way["turns"] = []
                    for r in range(P_BITS):
                        way["turns"].append((n, rows.buf[rows.cur]))
                        rows.take_turned(2 * r, None)
                        rows.merge_rows(r)
                        way["turns"].append((n, rows.buf[rows.cur]))
                        rows.take_turned(2 * r + 1, r + 1 if r < P_BITS - 1 else None)
                        for j in range(bits, 0, -1):
                            rows.merge(1 << j, False)
                        if r < P_BITS - 1:
                            rows.flip(r + 1)
                    way.update(sorted=n, at=rows.buf[rows.cur], width=rows.width)

        @block.tensor
        def _(pe):
            pe.wait_ge(consts_in, 32)
            pe.wait_ge(counted, 1)
            pe.matmul(banks[0][:, 0:2 + NPART], ones[:, :], count[:, :], start=True, stop=True).then_inc(summed, 1)
            pe.wait_ge(known, 1)
            flag = [pe.value_load(total[0:1, w:w + 1], min_val=0, max_val=1) for _, w in ways]
            for k, (way, _) in enumerate(ways):
                nb = way["width"] // (TB * P)
                with pe.If(flag[k] < 1):
                    for t, (n, buf) in enumerate(way["turns"]):
                        pe.wait_ge(ordered, n)
                        for b in range(nb):
                            m = min(4, nb)
                            if t * nb + b >= m:
                                pe.wait_ge(read, t * nb + b + 1 - m)
                            for x in range(TB):
                                at = (b * TB + x) * P
                                mm = pe.transpose(banks[b % 4][:, x * P:(x + 1) * P], buf[:, at:at + P], ident[:, :])
                            mm.then_inc(turned, 1)

        @block.sync
        def _(sync):
            sync.dma_start(signs[:, :], D["c_signs"]).then_inc(consts_in, 16)
            sync.dma_start(ident[:, :], D["c_ident"]).then_inc(consts_in, 16)
            for q in range(NPART):
                sync.dma_start(keys[0][:, :].rearrange("p (b q w) -> p b q w", q=NPART, w=KW)[:, :, q, :],
                               D["blocks"].rearrange("(q b p w) -> q p b w", q=NPART, b=NBLOCK, w=KW)[q]).then_inc(blocks_in, 16)
            sync.wait_ge(known, 1)
            sync.dma_start(D["n_edges"], total[0:1, :]).then_inc(stored, 16)
            sync.wait_ge(ends_in, 1)
            sync.dma_start(D["keys"][0:1].rearrange("(a n) -> a n", a=1), edge_of[:, 0:1]).then_inc(stored, 16)
            flag = [sync.value_load(total[0:1, w:w + 1], min_val=0, max_val=1) for _, w in ways]
            for k, (way, _) in enumerate(ways):
                size = P * way["width"]
                with sync.If(flag[k] < 1):
                    sync.dma_start(D["keys"][size + 1:size + 2].rearrange("(a n) -> a n", a=1), edge_of[:, 1:2]).then_inc(stored, 16)
                    sync.wait_ge(ordered, way["sorted"])
                    sync.dma_start(D["keys"][1:size + 1].rearrange("(p c) -> p c", p=P), way["at"]).then_inc(stored, 16)
            sync.wait_ge(stored, 64)
NE, GH = 4, 4
GF = GH * NE
NJ = M // ST


def phase_nodes(nc, D):
    with ExitStack() as ctx:
        s_ = Space(nc, ctx, "nodes")
        sb, ps, sem, sems = s_.sb, s_.ps, s_.sem, s_.sems
        ident, w_gat = sb("ident", [P, P]), sb("w_gat", [P, CH, GF])
        att = sb("att", [P, 2, GF])
        T = [sb(f"T{u}", [P, NC_, C]) for u in range(2)]
        N = sb("N", [P, NC_, C])
        stats, mv = sb("stats", [P, NC_, 6]), sb("mv", [P, NC_, 2])
        fence = sb("fence", [P, 1])
        ve, rstd = sb("ve", [P, NC_]), sb("rstd", [P, NC_])
        XF = [sb(f"XF{u}", [P, CH, ST]) for u in range(2)]
        TF = [sb(f"TF{u}", [P, CH, ST]) for u in range(2)]
        TAB = [sb(f"TAB{u}", [P, NC_, GF + GH]) for u in range(2)]
        VT = [sb(f"VT{u}", [P, NC_, GH]) for u in range(2)]
        hs = sb("hs", [P, NC_, GF])
        prod = sb("prod", [P, 2, NC_, GF])
        kx, kt, kh = [ps(f"kx{k}", 512) for k in range(CH)], [ps(f"kt{k}", 512) for k in range(CH)], ps("kh", 512)
        consts_in, own_s = sem("consts_in"), sem("vec")
        t_in, stored = sems("t_in", 2), sems("stored", 2)
        S = {n: sem(n) for n in "ve_in sd_in n_in x_turned t_turned xf_in tf_in h_done v_in".split()}
        STEPS = 5
        block = ctx.enter_context(nc.Block())
        rows = D["t2"].rearrange("b n f -> (b n) f").rearrange("(j c p) f -> j p c f", p=P, c=NC_)

        @block.gpsimd
        def _(pool):
            with pool.Fori(0, NJ // 2) as i:
                for u in range(2):
                    pool.wait_ge(S["n_in"], i * 2 + (u + 1))
                    pool.wait_ge(S["t_turned"], i * 2 + (u + 1))
                    pool.dma_start(T[u][:, :, :], rows[i * 2 + u]).then_inc(t_in[u], 16)

        @block.sync
        def _(sync):
            sync.dma_start(ident[:, :], D["c_ident"]).then_inc(consts_in, 16)
            sync.dma_start(w_gat[:, :, :], D["w_gat"]).then_inc(consts_in, 16)
            sync.dma_start(att[:, :, :], D["att"]).then_inc(consts_in, 16)
            for u in range(2):
                sync.sem_inc(stored[u], 64)
            tabv = D["table"].rearrange("(j c p) f -> j p c f", p=P, c=NC_)
            vv = D["vtable"].rearrange("(j c p) f -> j p c f", p=P, c=NC_)
            with sync.Fori(0, NJ // 2) as i:
                for u in range(2):
                    sync.wait_ge(S["xf_in"], i * 2 + (u + 2))
                    sync.dma_start(D["x3F"][i * 2 + u].rearrange("(k p) n -> p k n", p=P), XF[u][:, :, :]).then_inc(stored[u], 16)
                    sync.wait_ge(S["tf_in"], i * 2 + (u + 2))
                    sync.dma_start(D["t2F"][i * 2 + u].rearrange("(k p) n -> p k n", p=P), TF[u][:, :, :]).then_inc(stored[u], 16)
                    sync.wait_ge(S["v_in"], i * 2 + (u + 2))
                    sync.dma_start(tabv[i * 2 + u], TAB[u][:, :, :]).then_inc(stored[u], 16)
                    sync.dma_start(vv[i * 2 + u], VT[u][:, :, :]).then_inc(stored[u], 16)
            for u in range(2):
                sync.wait_ge(stored[u], 64 * (NJ // 2 + 1))

        @block.vector
        def _(v):
            own = Steps(v, own_s)
            v.wait_ge(consts_in, 48)
            v.sem_inc(S["n_in"], 2)
            with v.Fori(0, NJ // 2) as i:
                for u in range(2):
                    own.turn(i * (2 * STEPS) + u * STEPS)
                    j1 = v.snap(i * 2 + (u + 1))
                    v.wait_ge(t_in[u], i * 16 + 16)
                    for c in range(NC_):
                        ins = v.bn_stats(stats[:, c, :], T[u][:, c, :])
                    own.did(ins)
                    own.wait()
                    v.memset(fence[:, :], 0.0)
                    for c in range(NC_):
                        ins = v.bn_aggr(mv[:, c, :], stats[:, c, :])
                    own.did(ins)
                    own.wait()
                    v.tensor_scalar(ve[:, :], mv[:, :, 1], LN_EPS, None, ALU.add).then_inc(S["ve_in"], 1)
                    v.wait_ge(S["sd_in"], j1)
                    own.did(v.reciprocal(rstd[:, :], rstd[:, :]))
                    own.wait()
                    for c in range(NC_):
                        ins = v.tensor_scalar(N[:, c, :], T[u][:, c, :], mv[:, c, 0:1], rstd[:, c:c + 1], ALU.subtract, ALU.mult)
                    ins.then_inc(S["n_in"], 1)
                    v.wait_ge(S["h_done"], j1)
                    v.wait_ge(stored[u], i * 64 + 64)
                    own.did(v.tensor_copy(hs[:, :, :], kh[:, 0:NC_ * GF].rearrange("p (c f) -> p c f", f=GF)))
                    own.wait()
                    v.tensor_copy(TAB[u][:, :, 0:GF], hs[:, :, :])
                    for a in range(2):
                        ins = v.tensor_tensor(prod[:, a, :, :], hs[:, :, :], att[:, a, :].unsqueeze(1).to_broadcast([P, NC_, GF]), ALU.mult)
                    own.did(ins)
                    own.wait()
                    v.tensor_reduce(TAB[u][:, :, GF:GF + GH], prod[:, 0, :, :].rearrange("p c (h e) -> p c h e", e=NE), AXX, ALU.add)
                    v.tensor_reduce(VT[u][:, :, :], prod[:, 1, :, :].rearrange("p c (h e) -> p c h e", e=NE), AXX, ALU.add).then_inc(S["v_in"], 1)
            assert own.k == STEPS, own.k

        @block.tensor
        def _(pe):
            pe.wait_ge(consts_in, 48)
            pe.sem_inc(S["x_turned"], 1)
            pe.sem_inc(S["t_turned"], 2)
            with pe.Fori(0, NJ // 2) as i:
                for u in range(2):
                    j0 = pe.snap(i * 2 + u + 1)
                    pe.wait_ge(t_in[u], i * 16 + 16)
                    pe.wait_ge(S["tf_in"], j0)
                    for k in range(CH):
                        for c in range(NC_):
                            mm = pe.transpose(kt[k][:, c * P:(c + 1) * P], T[u][:, c, k * P:(k + 1) * P], ident[:, :])
                    mm.then_inc(S["t_turned"], 1)
                    pe.wait_ge(S["n_in"], j0 + 2)
                    pe.wait_ge(S["xf_in"], j0)
                    for k in range(CH):
                        for c in range(NC_):
                            mm = pe.transpose(kx[k][:, c * P:(c + 1) * P], N[:, c, k * P:(k + 1) * P], ident[:, :])
                    mm.then_inc(S["x_turned"], 1)
                    pe.wait_ge(S["xf_in"], j0 + 1)
                    pe.wait_ge(S["v_in"], j0)
                    for c in range(NC_):
                        for k in range(CH):
                            mm = pe.matmul(kh[:, c * GF:(c + 1) * GF], XF[u][:, k, c * P:(c + 1) * P], w_gat[:, k, :], start=(k == 0), stop=(k == CH - 1))
                    mm.then_inc(S["h_done"], 1)

        @block.scalar
        def _(act):
            act.wait_ge(consts_in, 48)
            for n in ("xf_in", "tf_in", "v_in"):
                act.sem_inc(S[n], 1)
            with act.Fori(0, NJ // 2) as i:
                for u in range(2):
                    j1 = act.snap(i * 2 + (u + 1))
                    act.wait_ge(S["ve_in"], j1)
                    act.activation(rstd[:, :], ve[:, :], ACT.Sqrt).then_inc(S["sd_in"], 1)
                    act.wait_ge(stored[u], i * 64 + 64)
                    act.wait_ge(S["t_turned"], j1 + 2)
                    for k in range(CH):
                        ins = act.activation(TF[u][:, k, :], kt[k][:, :], ACT.Copy)
                    ins.then_inc(S["tf_in"], 1)
                    act.wait_ge(S["x_turned"], j1 + 1)
                    for k in range(CH):
                        ins = act.activation(XF[u][:, k, :], kx[k][:, :], ACT.Copy)
                    ins.then_inc(S["xf_in"], 1)
CW = 64
CS = P * CW
NCHUNK = EDGES // CS
HE = NE + 1
SUMS = GH * HE
RES = GH + SUMS
FAR = 1.0e30
DECODE_STEPS, EDGE_STEPS = 3, 21
GS = 6
GROUP_CHUNKS = -(-GROUPS // GS) + (-(-GROUPS // GS)) % 2


def phase_edges(nc, D):
    with ExitStack() as ctx:
        s_ = Space(nc, ctx, "edges")
        sb, ps, sem, sems = s_.sb, s_.ps, s_.sem, s_.sems
        ident = sb("ident", [P, P])
        n_edges = sb("n_edges", [1, 4], I32)
        K = [[sb(f"K{u}_{w}", [P, CW], U32) for w in range(3)] for u in range(2)]
        dst = [sb(f"dst{w}", [P, CW], U32) for w in range(3)]
        src_i = [sb(f"src_i{u}", [P, CW], U32) for u in range(2)]
        dst_i = [sb(f"dst_i{u}", [P, CW], U32) for u in range(2)]
        end_i = [sb(f"end_i{u}", [P, CW], U32) for u in range(2)]
        cont, pen, whole = ([sb(f"{n}{u}", [P, w]) for u in range(2)] for n, w in (("cont", CW), ("pen", CW), ("whole", 1)))
        more = sb("more", [P, CW])
        G = [sb(f"G{u}", [P, CW, GF + GH]) for u in range(2)]
        V = [sb(f"V{u}", [P, CW, GH]) for u in range(2)]
        R = [sb(f"R{u}", [P, CW + 1, RES]) for u in range(2)]
        z, e = sb("z", [P, GH, CW]), sb("e", [P, GH, CW])
        ab = sb("ab", [P, 2, GH, CW])
        W = sb("W", [P, GH, HE, CW])
        rows = sb("rows", [P, 4, SUMS])
        RT = sb("RT", [SUMS, 4, P])
        cpen = sb("cpen", [SUMS, 2, P])
        EM, ES = sb("EM", [SUMS, P + 1]), sb("ES", [SUMS, P + 1])
        cab, cW = sb("cab", [SUMS, 2, P]), sb("cW", [SUMS, P])
        start = sb("start", [SUMS, 2, P])
        empty = sb("empty", [P, P, RES])
        lanes, zeros = sb("lanes", [P, P]), sb("zeros", [P, P], BF16)
        CK = [sb(f"CK{u}", [P, CW], U32) for u in range(2)]
        bits = [sb(f"bits{u}", [P, 2, CW], U32) for u in range(2)]
        digits = [sb(f"digits{u}", [P, 2, CW]) for u in range(2)]
        hot = [sb(f"hot{u}", [P, 2, CW, P], BF16) for u in range(2)]
        counts = sb("counts", [P, P])
        k_counts = ps("k_counts", 512)
        ck_in, bits_in, digits_in, hot_in = sems("ck_in", 2), sem("bits_in"), sem("digits_in"), sem("hot_in")
        hot_read, all_counted, counts_in, counts_out = sem("hot_read"), sem("all_counted"), sem("counts_in"), sem("counts_out")
        k_rows, k_start = ps("k_rows", 512), ps("k_start", 512)
        consts, own_s, decode_s = sem("consts"), sem("vec"), sem("decode")
        k_in, gathered, scattered = sems("k_in", 2), sems("gathered", 2), sems("scattered", 2)
        S = {n: sem(n) for n in "idx_in g_read ab1 ab1e rows_in rows_turned cab_in cabe start_in start_turned ab2 ab2e r_in landed went".split()}
        block = ctx.enter_context(nc.Block())
        keys = D["keys"].bitcast(U32)

        def run(eng, begin, this, ahead, group):
            eng.wait_ge(consts, 48)
            n = eng.value_load(n_edges[0:1, 0:1], min_val=1, max_val=EDGES)
            groups = eng.value_load(n_edges[0:1, 3:4], min_val=0, max_val=GROUPS) if group else None
            begin()

            def chunk(i, u, with_groups):
                with eng.If(i * (2 * CS) + u * CS < n):
                    if ahead:
                        with eng.If(i * (2 * CS) + (u + 1) * CS < n):
                            ahead(i + u, 1 - u)
                    if this:
                        this(i, u)
                if with_groups:
                    with eng.If(i * (2 * GS) + u * GS < groups):
                        for x in range(GS):
                            g = u * GS + x
                            with eng.If(i * (2 * GS) + g < groups):
                                group(i * GS + g // 2, g % 2)

            with eng.Fori(0, GROUP_CHUNKS // 2) as i:
                for u in range(2):
                    chunk(i, u, group is not None)
            with eng.If(GROUP_CHUNKS * CS - n < 0):
                with eng.Fori(GROUP_CHUNKS // 2, NCHUNK // 2) as i:
                    for u in range(2):
                        chunk(i, u, False)

        @block.sync
        def _(sync):
            sync.dma_start(ident[:, :], D["c_ident"]).then_inc(consts, 16)
            sync.dma_start(n_edges[:, :], D["n_edges"]).then_inc(consts, 16)
            sync.dma_start(lanes[:, :], D["c_lanes"]).then_inc(consts, 16)

            def load(i, u):
                at = [sync.snap(i * (2 * CS) + (u * CS + w)) if type(i) is not int else i * (2 * CS) + u * CS + w for w in range(3)]
                sync.wait_ge(S["idx_in"], i * 2 + (u + 1))
                sync.sem_inc(S["went"], 1)
                for w in range(3):
                    sync.dma_start(K[u][w][:, :], keys[bass.ds(at[w], CS)].rearrange("(p c) -> p c", p=P)).then_inc(k_in[u], 16)

            def load_group(j, u):
                sync.wait_ge(bits_in, j * 2 + (u + 1))
                at = nc.s_assert_within(sync.snap(j * 2 + u), 0, GROUPS - 1, skip_runtime_bounds_check_because="the groups that are live are below GROUPS")
                sync.sem_inc(S["went"], 1)
                sync.dma_start(CK[u][:, :], D["blocks"].bitcast(U32).rearrange("(g p w) -> g p w", p=P, w=KW)[at]).then_inc(ck_in[u], 16)

            def ahead(i, u):
                load(nc.s_assert_within(sync.snap(i), 0, NCHUNK // 2 - 1, skip_runtime_bounds_check_because="the chunk holds an edge"), u)
            run(sync, lambda: load(0, 0), None, ahead, load_group)
            sync.wait_ge(counts_in, 1)
            sync.dma_start(D["counts"].rearrange("(p q) -> p q", p=P), counts[:, :]).then_inc(counts_out, 16)
            sync.wait_ge(counts_out, 16)

        @block.gpsimd
        def _(pool):
            def begin():
                pool.sem_inc(S["landed"], 2)
                pool.memset(empty[:, :, :], 0.0).then_inc(S["r_in"], 1)
                pool.wait_ge(S["r_in"], 1)
                pool.memset(empty[:, :, 0:GH], -FAR).then_inc(S["r_in"], 1)
                pool.wait_ge(S["r_in"], 2)
                pool.dma_start(D["result"].rearrange("(p q) f -> p q f", p=P), empty[:, :, :]).then_inc(scattered[0], 16)
                gather(0, 0)
                pool.wait_ge(scattered[0], 16)

            def gather(i, u):
                pool.wait_ge(S["idx_in"], i * 2 + (u + 3))
                pool.wait_ge(S["g_read"], i * 2 + (u + 1))
                pool.sem_inc(S["went"], 1)
                for c in range(CW):
                    pool.indirect_dma_start(G[u][:, c, :], None, D["table"], bass.IndirectOffsetOnAxis(ap=src_i[u][:, c:c + 1], axis=0),
                                            bounds_check=M - 1, oob_is_err=False).then_inc(gathered[u], 16)
                    pool.indirect_dma_start(V[u][:, c, :], None, D["vtable"], bass.IndirectOffsetOnAxis(ap=dst_i[u][:, c:c + 1], axis=0),
                                            bounds_check=M - 1, oob_is_err=False).then_inc(gathered[u], 16)

            def scatter(i, u):
                pool.wait_ge(S["r_in"], i * 2 + (u + 3))
                pool.sem_inc(S["went"], 1)
                for c in range(CW):
                    pool.indirect_dma_start(D["result"], bass.IndirectOffsetOnAxis(ap=end_i[u][:, c:c + 1], axis=0), R[u][:, c + 1, :], None,
                                            bounds_check=M - 1, oob_is_err=False).then_inc(scattered[u], 16)
                pool.wait_ge(scattered[u], i * (16 * CW) + (16 * CW + (16 if u == 0 else 0)))
                pool.sem_inc(S["landed"], 1)
            run(pool, begin, scatter, gather, None)

        @block.vector
        def _(v):
            own, decoded = Steps(v, own_s), Steps(v, decode_s)

            def begin():
                v.memset(zeros[:, :], 0.0).then_inc(consts, 1)
                v.sem_inc(S["idx_in"], 2)
                v.sem_inc(S["g_read"], 2)
                v.sem_inc(bits_in, 2)
                v.memset(EM[:, P:P + 1], -FAR)
                own.did(v.memset(ES[:, P:P + 1], 0.0))
                own.wait()
                decode(0, 0)

            def decode(i, u):
                decoded.turn(i * (2 * DECODE_STEPS) + u * DECODE_STEPS)
                v.wait_ge(k_in[u], i * 48 + 48)
                v.wait_ge(S["landed"], i * 2 + (u + 1))
                v.wait_ge(S["idx_in"], i * 2 + (u + 2))
                for w in range(3):
                    v.tensor_scalar(dst[w][:, :], K[u][w][:, :], NODE_BITS, 4 * M - 1, ALU.logical_shift_right, ALU.bitwise_and)
                decoded.did(v.tensor_scalar(src_i[u][:, :], K[u][1][:, :], M - 1, None, ALU.bitwise_and))
                decoded.wait()
                v.tensor_scalar(dst_i[u][:, :], dst[1][:, :], float(M - 1), None, ALU.min)
                v.tensor_tensor(cont[u][:, :], dst[0][:, :], dst[1][:, :], ALU.is_equal)
                v.tensor_tensor(whole[u][:, :], dst[1][:, 0:1], dst[1][:, CW - 1:CW], ALU.is_equal)
                decoded.did(v.tensor_tensor(more[:, :], dst[2][:, :], dst[1][:, :], ALU.is_equal))
                decoded.wait()
                decoded.did(v.tensor_scalar(pen[u][:, :], cont[u][:, :], 1.0, FAR, ALU.subtract, ALU.mult))
                v.scalar_tensor_tensor(end_i[u][:, :], more[:, :], float(4 * M), dst[1][:, :], ALU.mult, ALU.add).then_inc(S["idx_in"], 1)

            def count_group(j, u):
                n1 = v.snap(j * 2 + (u + 1))
                v.wait_ge(ck_in[u], j * 16 + 16)
                v.tensor_scalar(bits[u][:, 0, :], CK[u][:, :], NODE_BITS + P_BITS, 4 * P - 1, ALU.logical_shift_right, ALU.bitwise_and)
                v.tensor_scalar(bits[u][:, 1, :], CK[u][:, :], NODE_BITS, P - 1, ALU.logical_shift_right, ALU.bitwise_and).then_inc(bits_in, 1)
                v.wait_ge(bits_in, n1 + 2)
                v.tensor_scalar(digits[u][:, 0, :], bits[u][:, 0, :], float(P), None, ALU.subtract)
                v.tensor_scalar(digits[u][:, 1, :], bits[u][:, 1, :], 0.0, None, ALU.add).then_inc(digits_in, 1)
                v.wait_ge(digits_in, n1)
                v.wait_ge(hot_read, n1)
                v.tensor_tensor(hot[u][:, :, :, :].rearrange("p a c n -> p (a c) n"), lanes[:, :].unsqueeze(1).to_broadcast([P, 2 * CW, P]),
                                digits[u][:, :, :].rearrange("p a c -> p (a c)").unsqueeze(2).to_broadcast([P, 2 * CW, P]), ALU.is_equal).then_inc(hot_in, 1)

            def body(i, u):
                own.turn(i * (2 * EDGE_STEPS) + (u * EDGE_STEPS + 1))
                n1 = v.snap(i * 2 + (u + 1))
                decoded.turn(i * (2 * DECODE_STEPS) + u * DECODE_STEPS)
                decoded.k = DECODE_STEPS
                decoded.wait()
                v.wait_ge(gathered[u], i * (32 * CW) + 32 * CW)
                own.did(v.tensor_tensor(z[:, :, :], G[u][:, :, GF:GF + GH].rearrange("p c h -> p h c"), V[u][:, :, :].rearrange("p c h -> p h c"), ALU.add))
                own.wait()
                own.did(v.scalar_tensor_tensor(e[:, :, :], z[:, :, :], 0.2, z[:, :, :], ALU.mult, ALU.max))
                r = R[u]
                maxima = r[:, :, 0:GH].rearrange("p c h -> p h c")

                def scans(name):
                    own.wait()
                    for h in range(GH):
                        ins = v.tensor_tensor_scan(r[:, 1:, h], pen[u][:, :], e[:, h, :], r[:, 0, h:h + 1], ALU.add, ALU.max)
                    own.did(ins)
                    own.wait()
                    own.did(v.tensor_tensor(z[:, :, :], maxima[:, :, 0:CW], pen[u][:, :].unsqueeze(1).to_broadcast([P, GH, CW]), ALU.add))
                    own.wait()
                    v.tensor_tensor(ab[:, 0, :, :], z[:, :, :], maxima[:, :, 1:], ALU.subtract)
                    v.tensor_tensor(ab[:, 1, :, :], e[:, :, :], maxima[:, :, 1:], ALU.subtract).then_inc(S[name], 1)
                    v.wait_ge(S[name + "e"], n1)
                    for h in range(GH):
                        v.tensor_copy(W[:, h, 0, :], ab[:, 1, h, :])
                        ins = v.tensor_tensor(W[:, h, 1:, :], G[u][:, :, h * NE:(h + 1) * NE].rearrange("p c k -> p k c"),
                                              ab[:, 1, h, :].unsqueeze(1).to_broadcast([P, NE, CW]), ALU.mult)
                    own.did(ins)
                    own.wait()
                    for h in range(GH):
                        for k in range(HE):
                            f = GH + h * HE + k
                            ins = v.tensor_tensor_scan(r[:, 1:, f], ab[:, 0, h, :], W[:, h, k, :], r[:, 0, f:f + 1], ALU.mult, ALU.add)
                    return ins

                v.memset(r[:, 0, 0:GH], -FAR)
                own.did(v.memset(r[:, 0, GH:], 0.0))
                own.did(scans("ab1"))
                own.wait()
                v.tensor_copy(rows[:, 0, :].rearrange("p (h k) -> p h k", k=HE), r[:, CW, 0:GH].unsqueeze(2).to_broadcast([P, GH, HE]))
                v.tensor_copy(rows[:, 1, :], r[:, CW, GH:])
                own.did(v.tensor_copy(rows[:, 3, :], cont[u][:, 0:1].to_broadcast([P, SUMS])))
                own.wait()
                v.tensor_tensor(rows[:, 2, :], rows[:, 3, :], whole[u][:, :].to_broadcast([P, SUMS]), ALU.mult).then_inc(S["rows_in"], 1)
                v.tensor_copy(EM[:, 0:1], EM[:, P:P + 1])
                own.did(v.tensor_copy(ES[:, 0:1], ES[:, P:P + 1]))
                v.wait_ge(S["rows_turned"], n1)
                own.did(v.tensor_copy(RT[:, :, :], k_rows[0:SUMS, :].rearrange("p (a b) -> p a b", a=4)))
                own.wait()
                own.did(v.tensor_scalar(cpen[:, :, :], RT[:, 2:4, :], 1.0, FAR, ALU.subtract, ALU.mult))
                own.wait()
                own.did(v.tensor_tensor_scan(EM[:, 1:], cpen[:, 0, :], RT[:, 0, :], EM[:, 0:1], ALU.add, ALU.max))
                own.wait()
                own.did(v.tensor_tensor(cab[:, 0, :], EM[:, 0:P], cpen[:, 0, :], ALU.add))
                own.wait()
                own.did(v.tensor_tensor(cab[:, 0, :], cab[:, 0, :], EM[:, 1:], ALU.subtract))
                v.tensor_tensor(cab[:, 1, :], RT[:, 0, :], EM[:, 1:], ALU.subtract).then_inc(S["cab_in"], 1)
                own.did(v.tensor_tensor(start[:, 0, :], EM[:, 0:P], cpen[:, 1, :], ALU.add))
                v.wait_ge(S["cabe"], n1)
                own.did(v.tensor_tensor(cW[:, :], RT[:, 1, :], cab[:, 1, :], ALU.mult))
                own.wait()
                own.did(v.tensor_tensor_scan(ES[:, 1:], cab[:, 0, :], cW[:, :], ES[:, 0:1], ALU.mult, ALU.add))
                own.wait()
                v.tensor_tensor(start[:, 1, :], ES[:, 0:P], RT[:, 3, :], ALU.mult).then_inc(S["start_in"], 1)
                v.wait_ge(S["start_turned"], n1)
                v.tensor_copy(r[:, 0, 0:GH], k_start[:, 0:SUMS].rearrange("p (h k) -> p h k", k=HE)[:, :, 0])
                own.did(v.tensor_copy(r[:, 0, GH:], k_start[:, 32:32 + SUMS]))
                scans("ab2").then_inc(S["r_in"], 1)
                v.wait_ge(S["r_in"], n1 + 2)
                v.memset(z[:, 0, 0:1], 0.0).then_inc(S["g_read"], 1)
            run(v, begin, body, decode, count_group)
            assert own.k == EDGE_STEPS and decoded.k == DECODE_STEPS
            v.wait_ge(all_counted, 1)
            v.tensor_copy(counts[:, :], k_counts[:, 0:P]).then_inc(counts_in, 1)

        @block.tensor
        def _(pe):
            def body(i, u):
                n1 = pe.snap(i * 2 + (u + 1))
                pe.wait_ge(S["rows_in"], n1)
                for a in range(4):
                    mm = pe.transpose(k_rows[0:SUMS, a * P:(a + 1) * P], rows[:, a, :], ident[:, :])
                mm.then_inc(S["rows_turned"], 1)
                pe.wait_ge(S["start_in"], n1)
                pe.matmul(k_start[:, 511:512], ident[:, :], ident[:, 0:1], start=True, stop=True)
                for a in range(2):
                    mm = pe.transpose(k_start[:, a * 32:a * 32 + SUMS], start[:, a, :], ident[0:SUMS, 0:SUMS])
                mm.then_inc(S["start_turned"], 1)

            def begin():
                pe.wait_ge(consts, 49)
                pe.sem_inc(hot_read, 2)
                pe.matmul(k_counts[:, 0:P], zeros[:, :], zeros[:, :], start=True, stop=False)

            def count_group(j, u):
                pe.wait_ge(hot_in, j * 2 + (u + 1))
                for c in range(CW):
                    mm = pe.matmul(k_counts[:, 0:P], hot[u][:, 0, c, :], hot[u][:, 1, c, :], start=False, stop=False)
                mm.then_inc(hot_read, 1)
            run(pe, begin, body, None, count_group)
            pe.matmul(k_counts[:, 0:P], zeros[:, :], zeros[:, :], start=False, stop=True).then_inc(all_counted, 1)

        @block.scalar
        def _(act):
            def body(i, u):
                n1 = act.snap(i * 2 + (u + 1))
                act.wait_ge(S["ab1"], n1)
                act.activation(ab[:, :, :, :], ab[:, :, :, :], ACT.Exp).then_inc(S["ab1e"], 1)
                act.wait_ge(S["cab_in"], n1)
                act.activation(cab[:, :, :], cab[:, :, :], ACT.Exp).then_inc(S["cabe"], 1)
                act.wait_ge(S["ab2"], n1)
                act.activation(ab[:, :, :, :], ab[:, :, :, :], ACT.Exp).then_inc(S["ab2e"], 1)
            run(act, lambda: None, body, None, None)
NQ = M // P


def phase_gates(nc, D):
    with ExitStack() as ctx:
        s_ = Space(nc, ctx, "gates")
        sb, sem = s_.sb, s_.sem
        R, T, V = sb("R", [P, NQ, RES]), sb("T", [P, NQ, GF + GH]), sb("V", [P, NQ, GH])
        b_gat, ln_g, ln_b = sb("b_gat", [P, GF]), sb("ln_g", [P, GF]), sb("ln_b", [P, GF])
        z, es, ec = sb("z", [P, NQ, GH]), sb("es", [P, NQ, GH]), sb("ec", [P, NQ, GH])
        N, none = sb("N", [P, NQ]), sb("none", [P, NQ])
        last = sb("last", [P, GF + GH])
        w3 = sb("w3", [P, 3, NQ, GH])
        den, num, tmp = sb("den", [P, NQ, GH]), sb("num", [P, NQ, GF]), sb("tmp", [P, NQ, GF])
        mean, var = sb("mean", [P, NQ]), sb("var", [P, NQ])
        score, rank, cmp = sb("score", [P, NE, NQ]), sb("rank", [P, NE, NQ]), sb("cmp", [P, NQ])
        top, gate, total = sb("top", [P, NQ]), sb("gate", [P, NE, NQ]), sb("total", [P, NQ])
        ins_in, out_in = sem("ins_in"), sem("out_in")
        step, exp1_in, exp1, var_in, sd_in, exp2_in, exp2, gates_in = (sem(n) for n in "step exp1_in exp1 var_in sd_in exp2_in exp2 gates_in".split())
        block = ctx.enter_context(nc.Block())

        @block.sync
        def _(sync):
            sync.dma_start(R[:, :, :], D["result"].rearrange("(p q) f -> p q f", p=P)).then_inc(ins_in, 16)
            sync.dma_start(T[:, :, :], D["table"].rearrange("(p q) f -> p q f", p=P)).then_inc(ins_in, 16)
            sync.dma_start(V[:, :, :], D["vtable"].rearrange("(p q) f -> p q f", p=P)).then_inc(ins_in, 16)
            sync.dma_start(N[:, :], D["counts"].rearrange("(p q) -> p q", p=P)).then_inc(ins_in, 16)
            sync.dma_start(last[:, :], D["table"][M - 1:M, :].to_broadcast([P, GF + GH])).then_inc(ins_in, 16)
            for dst, name in ((b_gat, "b_gat"), (ln_g, "ln_g"), (ln_b, "ln_b")):
                sync.dma_start(dst[:, :], D[name]).then_inc(ins_in, 16)
            sync.wait_ge(gates_in, 1)
            sync.dma_start(D["gates"].rearrange("e (p q) -> p e q", p=P), gate[:, :, :]).then_inc(out_in, 16)
            sync.wait_ge(out_in, 16)

        @block.vector
        def _(v):
            own = Steps(v, step)

            def do(ins):
                own.did(ins)
                own.wait()

            def wide(x, k=GF):
                return x.unsqueeze(2).to_broadcast([P, NQ, k])

            def per_feature(x):
                return x.unsqueeze(1).to_broadcast([P, NQ, GF])

            v.wait_ge(ins_in, 128)
            do(v.tensor_tensor(z[:, :, :], T[:, :, GF:], V[:, :, :], ALU.add))
            do(v.scalar_tensor_tensor(es[:, :, :], z[:, :, :], 0.2, z[:, :, :], ALU.mult, ALU.max))
            do(v.tensor_tensor(z[:, :, :], V[:, :, :], last[:, GF:].unsqueeze(1).to_broadcast([P, NQ, GH]), ALU.add))
            do(v.scalar_tensor_tensor(ec[:, :, :], z[:, :, :], 0.2, z[:, :, :], ALU.mult, ALU.max))
            do(v.tensor_scalar(none[:, :], N[:, :], 0.0, -FAR, ALU.is_equal, ALU.mult))
            do(v.tensor_tensor(ec[:, :, :], ec[:, :, :], wide(none[:, :], GH), ALU.add))
            do(v.tensor_tensor(z[:, :, :], es[:, :, :], R[:, :, 0:GH], ALU.max))
            do(v.tensor_tensor(z[:, :, :], z[:, :, :], ec[:, :, :], ALU.max))
            v.tensor_tensor(w3[:, 0, :, :], R[:, :, 0:GH], z[:, :, :], ALU.subtract)
            v.tensor_tensor(w3[:, 2, :, :], ec[:, :, :], z[:, :, :], ALU.subtract)
            v.tensor_tensor(w3[:, 1, :, :], es[:, :, :], z[:, :, :], ALU.subtract).then_inc(exp1_in, 1)
            v.wait_ge(exp1, 1)
            do(v.tensor_tensor(w3[:, 2, :, :], w3[:, 2, :, :], wide(N[:, :], GH), ALU.mult))
            sums = R[:, :, GH:].rearrange("p q (h k) -> p q h k", k=HE)
            do(v.tensor_tensor(den[:, :, :], sums[:, :, :, 0], w3[:, 0, :, :], ALU.mult))
            do(v.tensor_tensor(den[:, :, :], den[:, :, :], w3[:, 1, :, :], ALU.add))
            do(v.tensor_tensor(den[:, :, :], den[:, :, :], w3[:, 2, :, :], ALU.add))
            do(v.tensor_scalar(den[:, :, :], den[:, :, :], 1e-16, None, ALU.add))
            do(v.reciprocal(den[:, :, :], den[:, :, :]))
            for h in range(GH):
                f = slice(h * NE, (h + 1) * NE)
                v.tensor_tensor(num[:, :, f], sums[:, :, h, 1:], wide(w3[:, 0, :, h], NE), ALU.mult)
                ins = v.tensor_tensor(tmp[:, :, f], T[:, :, f], wide(w3[:, 1, :, h], NE), ALU.mult)
            do(ins)
            do(v.tensor_tensor(num[:, :, :], num[:, :, :], tmp[:, :, :], ALU.add))
            for h in range(GH):
                f = slice(h * NE, (h + 1) * NE)
                ins = v.tensor_tensor(tmp[:, :, f], last[:, f].unsqueeze(1).to_broadcast([P, NQ, NE]), wide(w3[:, 2, :, h], NE), ALU.mult)
            do(ins)
            do(v.tensor_tensor(num[:, :, :], num[:, :, :], tmp[:, :, :], ALU.add))
            for h in range(GH):
                f = slice(h * NE, (h + 1) * NE)
                ins = v.tensor_tensor(num[:, :, f], num[:, :, f], wide(den[:, :, h], NE), ALU.mult)
            do(ins)
            do(v.tensor_tensor(num[:, :, :], num[:, :, :], per_feature(b_gat[:, :]), ALU.add))
            do(v.tensor_reduce(mean[:, :], num[:, :, :], AXX, ALU.add))
            do(v.tensor_scalar(mean[:, :], mean[:, :], 1.0 / GF, None, ALU.mult))
            do(v.tensor_tensor(num[:, :, :], num[:, :, :], wide(mean[:, :]), ALU.subtract))
            do(v.tensor_tensor(tmp[:, :, :], num[:, :, :], num[:, :, :], ALU.mult))
            do(v.tensor_reduce(var[:, :], tmp[:, :, :], AXX, ALU.add))
            v.tensor_scalar(var[:, :], var[:, :], 1.0 / GF, LN_EPS, ALU.mult, ALU.add).then_inc(var_in, 1)
            v.wait_ge(sd_in, 1)
            do(v.reciprocal(var[:, :], var[:, :]))
            do(v.tensor_tensor(num[:, :, :], num[:, :, :], wide(var[:, :]), ALU.mult))
            do(v.tensor_tensor(num[:, :, :], num[:, :, :], per_feature(ln_g[:, :]), ALU.mult))
            do(v.tensor_tensor(num[:, :, :], num[:, :, :], per_feature(ln_b[:, :]), ALU.add))
            for k in range(NE):
                ins = v.tensor_reduce(score[:, k, :], num[:, :, k::NE], AXX, ALU.add)
            do(ins)
            do(v.tensor_scalar(score[:, :, :], score[:, :, :], 1.0 / GH, None, ALU.mult))
            v.memset(rank[:, :, :], 0.0)
            do(v.tensor_tensor(top[:, :], score[:, 0, :], score[:, 1, :], ALU.max))
            for k in range(2, NE):
                do(v.tensor_tensor(top[:, :], top[:, :], score[:, k, :], ALU.max))
            for k in range(NE):
                for j in range(NE):
                    if j != k:
                        do(v.tensor_tensor(cmp[:, :], score[:, j, :], score[:, k, :], ALU.is_ge if j < k else ALU.is_gt))
                        do(v.tensor_tensor(rank[:, k, :], rank[:, k, :], cmp[:, :], ALU.add))
            do(v.tensor_scalar(rank[:, :, :], rank[:, :, :], 2.0, None, ALU.is_lt))
            v.tensor_tensor(gate[:, :, :], score[:, :, :], top[:, :].unsqueeze(1).to_broadcast([P, NE, NQ]), ALU.subtract).then_inc(exp2_in, 1)
            v.wait_ge(exp2, 1)
            do(v.tensor_tensor(gate[:, :, :], gate[:, :, :], rank[:, :, :], ALU.mult))
            do(v.tensor_reduce(total[:, :], gate[:, :, :].rearrange("p e q -> p q e"), AXX, ALU.add))
            do(v.reciprocal(total[:, :], total[:, :]))
            v.tensor_tensor(gate[:, :, :], gate[:, :, :], total[:, :].unsqueeze(1).to_broadcast([P, NE, NQ]), ALU.mult).then_inc(gates_in, 1)

        @block.scalar
        def _(act):
            act.wait_ge(exp1_in, 1)
            act.activation(w3[:, :, :, :], w3[:, :, :, :], ACT.Exp).then_inc(exp1, 1)
            act.wait_ge(var_in, 1)
            act.activation(var[:, :], var[:, :], ACT.Sqrt).then_inc(sd_in, 1)
            act.wait_ge(exp2_in, 1)
            act.activation(gate[:, :, :], gate[:, :, :], ACT.Exp).then_inc(exp2, 1)


HF = 2 * C
FT = HF // P


def phase_experts(nc, D):
    with ExitStack() as ctx:
        s_ = Space(nc, ctx, "moe")
        sb, ps, sem, sems = s_.sb, s_.ps, s_.sem, s_.sems
        w1, b1 = sb("w1", [P, NE, CH, HF]), sb("b1", [P, NE, FT])
        w2, b2 = sb("w2", [P, NE, FT, C]), sb("b2", [NE, C])
        pick = sb("pick", [NE, NE, P])
        loads = [(w1, "moe1"), (b1, "moe1_b"), (w2, "moe2"), (b2, "moe2_b"), (pick, "c_pick")]
        X = [sb(f"X{u}", [P, CH, ST]) for u in range(2)]
        T = [sb(f"T{u}", [P, CH, ST]) for u in range(2)]
        g = [sb(f"g{u}", [NE, ST]) for u in range(2)]
        gb = [sb(f"gb{u}", [P, ST]) for u in range(2)]
        H = [sb(f"H{u}", [P, FT, ST]) for u in range(2)]
        O = [sb(f"O{u}", [P, CH, ST]) for u in range(2)]
        k_h = [ps(f"k_h{k}", 512) for k in range(4)]
        k_g = [ps(f"k_g{k}", 512) for k in range(2)]
        k_o = [ps(f"k_o{k}", 512) for k in range(CH)]
        weights_in = sem("weights_in")
        x_in, stored = sems("x_in", 2), sems("stored", 2)
        S = {n: sem(n) for n in "gb_done gb_in h_done gelu_in hg_in o_done o_in".split()}
        per = dict(gb_done=NE, gb_in=NE, h_done=NE * FT, gelu_in=NE * FT, hg_in=NE * FT, o_done=CH, o_in=CH)
        block = ctx.enter_context(nc.Block())

        def start(eng, names):
            for n in names.split():
                eng.sem_inc(S[n], 2 * per[n])

        @block.gpsimd
        def _(pool):
            with pool.Fori(0, NJ // 2) as i:
                for u in range(2):
                    pool.wait_ge(S["o_in"], (i * 2 + (u + 1)) * CH)
                    pool.dma_start(X[u][:, :, :], D["x3F"][i * 2 + u].rearrange("(k p) n -> p k n", p=P)).then_inc(x_in[u], 16)
                    pool.dma_start(T[u][:, :, :], D["t2F"][i * 2 + u].rearrange("(k p) n -> p k n", p=P)).then_inc(x_in[u], 16)
                    pool.dma_start(g[u][:, :], D["gates"].rearrange("e (j n) -> j e n", n=ST)[i * 2 + u]).then_inc(x_in[u], 16)

        @block.sync
        def _(sync):
            for dst, name in loads:
                sync.dma_start(dst[tuple(slice(None) for _ in dst.shape)], D[name]).then_inc(weights_in, 16)
            for u in range(2):
                sync.sem_inc(stored[u], 16)
            with sync.Fori(0, NJ // 2) as i:
                for u in range(2):
                    sync.wait_ge(S["o_in"], (i * 2 + (u + 3)) * CH)
                    sync.dma_start(D["out"][i].rearrange("(k p) n -> p k n", p=P)[:, :, u * ST:(u + 1) * ST], O[u][:, :, :]).then_inc(stored[u], 16)
            for u in range(2):
                sync.wait_ge(stored[u], 16 * (NJ // 2 + 1))

        @block.tensor
        def _(pe):
            pe.wait_ge(weights_in, 16 * len(loads))
            start(pe, "gb_done h_done o_done")
            with pe.Fori(0, NJ // 2) as i:
                for u in range(2):
                    j = pe.snap(i * 2 + (u + 2))
                    jg, jh, jo = pe.snap(j * NE), pe.snap(j * NE * FT), pe.snap(j * CH)
                    pe.wait_ge(x_in[u], i * 48 + 48)

                    def second(e):
                        for f in range(FT):
                            pe.wait_ge(S["hg_in"], jh + (e * FT + f + 1))
                            if e == 0 and f == 0:
                                pe.wait_ge(S["o_in"], jo)
                            for o in range(CH):
                                mm = pe.matmul(k_o[o][:, :], w2[:, e, f, o * P:(o + 1) * P], H[e % 2][:, f, :], start=(e == 0 and f == 0), stop=False)
                        return mm

                    for e in range(NE):
                        pe.wait_ge(S["gb_in"], jg + (e - 1))
                        pe.matmul(k_g[e % 2][:, :], pick[:, e, :], g[u][:, :], start=True, stop=True).then_inc(S["gb_done"], 1)
                        for f in range(FT):
                            n = e * FT + f
                            pe.wait_ge(S["gelu_in"], jh + (n - 3))
                            for k in range(CH):
                                mm = pe.matmul(k_h[n % 4][:, :], w1[:, e, k, f * P:(f + 1) * P], X[u][:, k, :], start=(k == 0), stop=(k == CH - 1))
                            mm.then_inc(S["h_done"], 1)
                        if e:
                            second(e - 1)
                    second(NE - 1)
                    for o in range(CH):
                        pe.matmul(k_o[o][:, :], b2[:, o * P:(o + 1) * P], g[u][:, :], start=False, stop=True).then_inc(S["o_done"], 1)

        @block.scalar
        def _(act):
            act.wait_ge(weights_in, 16 * len(loads))
            start(act, "gelu_in")
            with act.Fori(0, NJ // 2) as i:
                for u in range(2):
                    j = act.snap(i * 2 + (u + 2))
                    jh, jo = act.snap(j * NE * FT), act.snap(j * CH)
                    for e in range(NE):
                        for f in range(FT):
                            n = e * FT + f
                            act.wait_ge(S["h_done"], jh + (n + 1))
                            act.activation(H[e % 2][:, f, :], k_h[n % 4][:, :], ACT.Gelu, bias=b1[:, e, f:f + 1]).then_inc(S["gelu_in"], 1)

        @block.vector
        def _(v):
            v.wait_ge(weights_in, 16 * len(loads))
            start(v, "gb_in hg_in o_in")
            with v.Fori(0, NJ // 2) as i:
                for u in range(2):
                    j = v.snap(i * 2 + (u + 2))
                    jg, jh, jo = v.snap(j * NE), v.snap(j * NE * FT), v.snap(j * CH)
                    for e in range(NE):
                        v.wait_ge(S["gb_done"], jg + (e + 1))
                        v.tensor_copy(gb[e % 2][:, :], k_g[e % 2][:, :]).then_inc(S["gb_in"], 1)
                        for f in range(FT):
                            n = e * FT + f
                            v.wait_ge(S["gelu_in"], jh + (n + 1))
                            if f == 0:
                                v.wait_ge(S["gb_in"], jg + (e + 1))
                            v.tensor_tensor(H[e % 2][:, f, :], H[e % 2][:, f, :], gb[e % 2][:, :], ALU.mult).then_inc(S["hg_in"], 1)
                    v.wait_ge(stored[u], i * 16 + 16)
                    for o in range(CH):
                        v.wait_ge(S["o_done"], jo + (o + 1))
                        v.tensor_tensor(O[u][:, o, :], k_o[o][:, :], T[u][:, o, :], ALU.add).then_inc(S["o_in"], 1)


def build_program(nc, D):
    for name, shape, dt in (("t1", (B, C, HW), F32), ("t2", (B, HW, C), F32),
                            ("keys", (EDGES + 2,), F32), ("n_edges", (1, 4), I32), ("blocks", (EDGES,), F32),
                            ("x3F", (NJ, C, ST), F32), ("t2F", (NJ, C, ST), F32),
                            ("table", (M, GF + GH), F32), ("vtable", (M, GH), F32),
                            ("counts", (M,), F32), ("result", (M, RES), F32), ("gates", (NE, M), F32)):
        D[name] = nc.dram_tensor(name, shape, dt, kind="Internal").ap()
    phase_conv(nc, D)
    phase_ssm(nc, D)
    phase_sort(nc, D)
    phase_nodes(nc, D)
    phase_edges(nc, D)
    phase_gates(nc, D)
    phase_experts(nc, D)


def kernel(x, L0_conv_fc1_w, L0_conv_fc1_b, L0_conv_fc2_w, L0_conv_fc2_b, L0_conv_qkv_w, L0_conv_qkv_b,
           L0_conv_proj_w, L0_conv_proj_b, L0_conv_ffn1_w, L0_conv_ffn1_b, L0_conv_ffn2_w, L0_conv_ffn2_b,
           L1_attn_W_in, L1_attn_conv_w, L1_attn_conv_b, L1_attn_dt_bias, L1_attn_A_log, L1_attn_Dp,
           L1_attn_gnorm_w, L1_attn_norm_w, L1_attn_W_out,
           L1_ffn_W_gat, L1_ffn_att_src, L1_ffn_att_dst, L1_ffn_b_gat, L1_ffn_ln_gamma, L1_ffn_ln_beta,
           L1_ffn_W1, L1_ffn_b1, L1_ffn_W2, L1_ffn_b2, L1_ffn_edge_index):
    import concourse.bacc as _bacc
    from concourse import mybir as _mybir
    from concourse.bass_utils import run_bass_kernel_spmd as _run

    def rows_in_tiles(w):
        w = np.asarray(w)
        return w.reshape(-1, P, w.shape[1]).transpose(1, 0, 2)

    def vector_tiles(v):
        return np.asarray(v).reshape(-1, P).T

    def column(v):
        return np.asarray(v)[:, None]

    def on_all(v):
        v = np.asarray(v)
        return np.broadcast_to(v.reshape(1, -1), (P, v.size))

    qkv, qkv_b = np.asarray(L0_conv_qkv_w), np.asarray(L0_conv_qkv_b)
    w_in = np.asarray(L1_attn_W_in).T
    att = np.stack([np.asarray(L1_ffn_att_src).reshape(-1), np.asarray(L1_ffn_att_dst).reshape(-1)])
    w1, w2 = np.asarray(L1_ffn_W1), np.asarray(L1_ffn_W2)
    lanes = np.arange(P)
    arrays = dict(
        x=np.asarray(x).reshape(B, C, HW),
        fc1=rows_in_tiles(np.asarray(L0_conv_fc1_w).T), fc1_b=column(L0_conv_fc1_b),
        fc2=np.asarray(L0_conv_fc2_w).T, fc2_b=vector_tiles(L0_conv_fc2_b),
        wq=np.tile(qkv[:AD].T, (1, 4)), wk=np.tile(qkv[AD:2 * AD].T, (1, 4)), wv=qkv[2 * AD:].T,
        bq=column(qkv_b[:AD]), bk=column(qkv_b[AD:2 * AD]), bv=column(qkv_b[2 * AD:]),
        proj=np.tile(np.asarray(L0_conv_proj_w).T, (1, 2)), proj_b=column(L0_conv_proj_b),
        ffn1=rows_in_tiles(np.asarray(L0_conv_ffn1_w).T), ffn1_b=vector_tiles(L0_conv_ffn1_b),
        ffn2=rows_in_tiles(np.asarray(L0_conv_ffn2_w).T), ffn2_b=vector_tiles(L0_conv_ffn2_b),
        w_z=rows_in_tiles(w_in[:, :DI]), w_x=rows_in_tiles(w_in[:, DI:2 * DI + 2 * DS]),
        w_dt=rows_in_tiles(w_in[:, 2 * DI + 2 * DS:]), w_out=rows_in_tiles(np.asarray(L1_attn_W_out).T),
        norm_w=vector_tiles(L1_attn_norm_w), gnorm_w=vector_tiles(L1_attn_gnorm_w),
        conv_w=rows_in_tiles(L1_attn_conv_w), conv_b=vector_tiles(L1_attn_conv_b),
        dt_b=on_all(L1_attn_dt_bias), a_log=on_all(L1_attn_A_log), dp=on_all(L1_attn_Dp),
        w_gat=rows_in_tiles(L1_ffn_W_gat), att=np.broadcast_to(att, (P, 2, GF)),
        edges=np.asarray(L1_ffn_edge_index),
        b_gat=on_all(L1_ffn_b_gat), ln_g=on_all(L1_ffn_ln_gamma), ln_b=on_all(L1_ffn_ln_beta),
        moe1=w1.reshape(NE, CH, P, HF).transpose(2, 0, 1, 3),
        moe1_b=np.asarray(L1_ffn_b1).reshape(NE, FT, P).transpose(2, 0, 1),
        moe2=w2.reshape(NE, FT, P, C).transpose(2, 0, 1, 3), moe2_b=np.asarray(L1_ffn_b2),
        c_ident=np.eye(P, dtype=np.float32), c_lanes=np.tile(np.arange(P, dtype=np.float32), (P, 1)),
        c_group=np.kron(np.eye(16, dtype=np.float32), np.full((8, 8), 1 / 8, np.float32)),
        c_upper=np.triu(np.ones((P, P), np.float32)),
        c_signs=np.stack([1.0 - 2.0 * ((lanes >> k) & 1) for k in range(P_BITS)], 1).astype(np.float32),
        c_pick=np.repeat(np.eye(NE, dtype=np.float32)[:, :, None], P, 2))
    arrays = {name: np.ascontiguousarray(a) for name, a in arrays.items()}

    nc = _bacc.Bacc("TRN2", target_bir_lowering=False, num_devices=1)
    D = {name: nc.dram_tensor(name, a.shape, _mybir.dt.from_np(a.dtype), kind="ExternalInput").ap()
         for name, a in arrays.items()}
    D["out"] = nc.dram_tensor("out", (B, C, HW), _mybir.dt.float32, kind="ExternalOutput").ap()
    build_program(nc, D)
    r = _run(nc, [arrays], core_ids=[0])
    return r.results[0]["out"].reshape(B, C, 32, 32)
```
